# Optimizing a Trainium2 kernel written in Bass

```python
import numpy as np
import jax
import jax.numpy as jnp

def _softmax(x, axis=-1):
    return jax.nn.softmax(x, axis=axis)

def _gelu(x):
    return jax.nn.gelu(x, approximate=True)

def _silu(x):
    return jax.nn.silu(x)

def _sigmoid(x):
    return jax.nn.sigmoid(x)

def _layernorm(x, axis=-1, eps=1e-05):
    m = jnp.mean(x, axis=axis, keepdims=True)
    v = jnp.var(x, axis=axis, keepdims=True)
    return (x - m) / jnp.sqrt(v + eps)

def _scatter_add(tgt, idx, src, axis=0):
    return tgt.at[idx].add(src)

def _segment_sum(src, seg, n):
    return jax.ops.segment_sum(src, seg, n)
kernel_name = 'mk_recurrent_d2_jaxref_r8_b4a26f'

def setup_inputs(seed: int=0):
    np.random.seed(seed)
    _w = jnp.asarray

    def _L0_attn_setup():
        import jax, jax.numpy as jnp
        import numpy as np
        B, S, HID = (2, 256, 256)
        NH = 16
        Q_LORA, KV_LORA = (192, 64)
        NOPE, ROPE_D, VH = (128, 64, 128)
        Q_HEAD = NOPE + ROPE_D
        EPS = 1e-06
        THETA = 10000.0
        SCALE = Q_HEAD ** (-0.5)

        def rmsnorm(x, w):
            return x * jax.lax.rsqrt(jnp.mean(x * x, axis=-1, keepdims=True) + EPS) * w

        def rope_cos_sin(s):
            inv = 1.0 / THETA ** (jnp.arange(0, ROPE_D, 2, dtype=jnp.float32) / ROPE_D)
            f = jnp.arange(s, dtype=jnp.float32)[:, None] * inv[None, :]
            emb = jnp.concatenate([f, f], axis=-1)
            return (jnp.cos(emb), jnp.sin(emb))

        def apply_rope(x, cos, sin):
            b, h, s, d = x.shape
            xp = x.reshape(b, h, s, d // 2, 2)
            x = jnp.concatenate([xp[..., 0], xp[..., 1]], axis=-1)
            x1, x2 = jnp.split(x, 2, axis=-1)
            rot = jnp.concatenate([-x2, x1], axis=-1)
            return x * cos + rot * sin
        key = jax.random.key(seed)
        ks = jax.random.split(key, 7)
        sd = 0.02
        return {'hidden_states': jax.random.normal(ks[0], (B, S, HID), jnp.float32), 'wq_a': jax.random.normal(ks[1], (Q_LORA, HID), jnp.float32) * sd, 'q_a_ln_w': jnp.ones((Q_LORA,), jnp.float32), 'wq_b': jax.random.normal(ks[2], (NH * Q_HEAD, Q_LORA), jnp.float32) * sd, 'wkv_a': jax.random.normal(ks[3], (KV_LORA + ROPE_D, HID), jnp.float32) * sd, 'kv_a_ln_w': jnp.ones((KV_LORA,), jnp.float32), 'wkv_b': jax.random.normal(ks[4], (NH * (NOPE + VH), KV_LORA), jnp.float32) * sd, 'wo': jax.random.normal(ks[5], (HID, NH * VH), jnp.float32) * sd}
    _L0_attn_in = _L0_attn_setup()

    def _L0_ffn_setup():
        import jax, jax.numpy as jnp
        import numpy as np
        import math
        N_EMBD = 256
        N_HEAD = 16
        HEAD_DIM = N_EMBD // N_HEAD
        B, T = (2, 256)
        key = jax.random.key(seed)
        k1, k2, k3 = jax.random.split(key, 3)
        x = jax.random.normal(k1, (B, T, N_EMBD), dtype=jnp.float32)
        W_gate = jax.random.normal(k2, (N_HEAD, N_EMBD), dtype=jnp.float32) * 0.02
        W_qkv = jax.random.normal(k3, (3 * N_EMBD, N_EMBD), dtype=jnp.float32) * 0.02
        return {'x': x, 'W_gate': W_gate, 'W_qkv': W_qkv}
    _L0_ffn_in = _L0_ffn_setup()

    def _L1_attn_setup():
        import jax, jax.numpy as jnp
        import numpy as np
        B, T, H = (4, 512, 256)
        G_EPS = 0.5
        LN_EPS = 1e-05
        INIT_STD = 0.02

        def _g_log(x):
            return jnp.where(x >= 0, jnp.log(jax.nn.relu(x) + G_EPS), -jax.nn.softplus(-x))
        key = jax.random.key(seed)
        ks = jax.random.split(key, 4)
        return {'hidden_states': jax.random.normal(ks[0], (B, T, H), jnp.float32), 'W_z': jax.random.normal(ks[1], (H, H), jnp.float32) * INIT_STD, 'b_z': jnp.zeros((H,), jnp.float32), 'W_h': jax.random.normal(ks[2], (H, H), jnp.float32) * INIT_STD, 'b_h': jnp.zeros((H,), jnp.float32), 'ln_w': jnp.ones((H,), jnp.float32), 'ln_b': jnp.zeros((H,), jnp.float32), 'h0': jax.random.normal(ks[3], (H,), jnp.float32) * INIT_STD}
    _L1_attn_in = _L1_attn_setup()

    def _L1_ffn_setup():
        import jax, jax.numpy as jnp
        import numpy as np
        B, S, D, F, E, K = (2, 256, 256, 512, 8, 1)

        def _silu_mul(gu):
            g, u = jnp.split(gu, 2, axis=-1)
            return jax.nn.silu(g) * u

        def _moe_forward(hidden_states, router_w, w_gate_up, w_down, shared_gate_up, shared_down, top_k=K):
            b, s, d = hidden_states.shape
            x = hidden_states.reshape(-1, d)
            router_logits = x @ router_w.T
            topk_vals, topk_ids = jax.lax.top_k(router_logits, top_k)
            gate = jax.nn.sigmoid(topk_vals.astype(jnp.float32)).astype(x.dtype)
            xs = (x[:, None, :] * gate[:, :, None]).reshape(-1, d)
            ids_flat = topk_ids.reshape(-1)
            n_experts = w_gate_up.shape[0]

            def body(acc, inp):
                wg, wd, e = inp
                h = _silu_mul(xs @ wg)
                o = h @ wd
                mask = (ids_flat == e)[:, None]
                return (acc + jnp.where(mask, o, jnp.zeros((), o.dtype)), None)
            acc0 = jnp.zeros_like(xs)
            routed, _ = jax.lax.scan(body, acc0, (w_gate_up, w_down, jnp.arange(n_experts)))
            routed = routed.reshape(-1, top_k, d).sum(1)
            shared = _silu_mul(x @ shared_gate_up) @ shared_down
            return (routed + shared).reshape(b, s, d)
        key = jax.random.key(seed)
        ks = jax.random.split(key, 6)
        scale = 0.02
        return {'hidden_states': jax.random.normal(ks[0], (B, S, D), jnp.float32), 'router_w': jax.random.normal(ks[1], (E, D), jnp.float32) * scale, 'w_gate_up': jax.random.normal(ks[2], (E, D, 2 * F), jnp.float32) * scale, 'w_down': jax.random.normal(ks[3], (E, F, D), jnp.float32) * scale, 'shared_gate_up': jax.random.normal(ks[4], (D, 2 * F), jnp.float32) * scale, 'shared_down': jax.random.normal(ks[5], (F, D), jnp.float32) * scale}
    _L1_ffn_in = _L1_ffn_setup()
    _d = {'L0_attn_hidden_states': _L0_attn_in['hidden_states'], 'L0_attn_wq_a': _L0_attn_in['wq_a'], 'L0_attn_q_a_ln_w': _L0_attn_in['q_a_ln_w'], 'L0_attn_wq_b': _L0_attn_in['wq_b'], 'L0_attn_wkv_a': _L0_attn_in['wkv_a'], 'L0_attn_kv_a_ln_w': _L0_attn_in['kv_a_ln_w'], 'L0_attn_wkv_b': _L0_attn_in['wkv_b'], 'L0_attn_wo': _L0_attn_in['wo'], 'L0_ffn_W_gate': _L0_ffn_in['W_gate'], 'L0_ffn_W_qkv': _L0_ffn_in['W_qkv'], 'L1_attn_W_z': _L1_attn_in['W_z'], 'L1_attn_b_z': _L1_attn_in['b_z'], 'L1_attn_W_h': _L1_attn_in['W_h'], 'L1_attn_b_h': _L1_attn_in['b_h'], 'L1_attn_ln_w': _L1_attn_in['ln_w'], 'L1_attn_ln_b': _L1_attn_in['ln_b'], 'L1_attn_h0': _L1_attn_in['h0'], 'L1_ffn_router_w': _L1_ffn_in['router_w'], 'L1_ffn_w_gate_up': _L1_ffn_in['w_gate_up'], 'L1_ffn_w_down': _L1_ffn_in['w_down'], 'L1_ffn_shared_gate_up': _L1_ffn_in['shared_gate_up'], 'L1_ffn_shared_down': _L1_ffn_in['shared_down']}
    _x0 = _d['L0_attn_hidden_states']
    _d['L0_attn_hidden_states'] = jax.random.normal(jax.random.fold_in(jax.random.key(seed), 1), (4, 256, 256), dtype=_x0.dtype)
    del _x0
    return _d

def reference(L0_attn_hidden_states, L0_attn_wq_a, L0_attn_q_a_ln_w, L0_attn_wq_b, L0_attn_wkv_a, L0_attn_kv_a_ln_w, L0_attn_wkv_b, L0_attn_wo, L0_ffn_W_gate, L0_ffn_W_qkv, L1_attn_W_z, L1_attn_b_z, L1_attn_W_h, L1_attn_b_h, L1_attn_ln_w, L1_attn_ln_b, L1_attn_h0, L1_ffn_router_w, L1_ffn_w_gate_up, L1_ffn_w_down, L1_ffn_shared_gate_up, L1_ffn_shared_down):

    def _L0_attn_ref(hidden_states, wq_a, q_a_ln_w, wq_b, wkv_a, kv_a_ln_w, wkv_b, wo):
        import jax, jax.numpy as jnp
        import numpy as np
        B, S, HID = (2, 256, 256)
        NH = 16
        Q_LORA, KV_LORA = (192, 64)
        NOPE, ROPE_D, VH = (128, 64, 128)
        Q_HEAD = NOPE + ROPE_D
        EPS = 1e-06
        THETA = 10000.0
        SCALE = Q_HEAD ** (-0.5)

        def rmsnorm(x, w):
            return x * jax.lax.rsqrt(jnp.mean(x * x, axis=-1, keepdims=True) + EPS) * w

        def rope_cos_sin(s):
            inv = 1.0 / THETA ** (jnp.arange(0, ROPE_D, 2, dtype=jnp.float32) / ROPE_D)
            f = jnp.arange(s, dtype=jnp.float32)[:, None] * inv[None, :]
            emb = jnp.concatenate([f, f], axis=-1)
            return (jnp.cos(emb), jnp.sin(emb))

        def apply_rope(x, cos, sin):
            b, h, s, d = x.shape
            xp = x.reshape(b, h, s, d // 2, 2)
            x = jnp.concatenate([xp[..., 0], xp[..., 1]], axis=-1)
            x1, x2 = jnp.split(x, 2, axis=-1)
            rot = jnp.concatenate([-x2, x1], axis=-1)
            return x * cos + rot * sin
        b, s, _ = hidden_states.shape
        q = rmsnorm(hidden_states @ wq_a.T, q_a_ln_w) @ wq_b.T
        q = q.reshape(b, s, NH, Q_HEAD).transpose(0, 2, 1, 3)
        q_nope, q_pe = (q[..., :NOPE], q[..., NOPE:])
        ckv = hidden_states @ wkv_a.T
        kv = rmsnorm(ckv[..., :KV_LORA], kv_a_ln_w)
        k_pe = ckv[..., KV_LORA:][:, None, :, :]
        cos, sin = rope_cos_sin(s)
        q_pe = apply_rope(q_pe, cos, sin)
        k_pe = apply_rope(k_pe, cos, sin)
        w = wkv_b.reshape(NH, NOPE + VH, KV_LORA)
        q_absorb = w[:, :NOPE, :]
        out_absorb = w[:, VH:, :]
        q_abs = jnp.einsum('bhsd,hdc->bhsc', q_nope, q_absorb)
        scores = (jnp.einsum('bhsc,btc->bhst', q_abs, kv) + jnp.einsum('bhsd,bxtd->bhst', q_pe, k_pe)) * SCALE
        causal = jnp.tril(jnp.ones((s, s), bool))
        scores = jnp.where(causal, scores, jnp.finfo(scores.dtype).min)
        attn = jax.nn.softmax(scores, axis=-1)
        x = jnp.einsum('bhst,btc->bhsc', attn, kv)
        x = jnp.einsum('bhsc,hdc->bhsd', x, out_absorb)
        x = x.transpose(0, 2, 1, 3).reshape(b, s, NH * VH)
        return x @ wo.T

    def _L0_ffn_ref(x, W_gate, W_qkv):
        import jax, jax.numpy as jnp
        import numpy as np
        import math
        N_EMBD = 256
        N_HEAD = 16
        HEAD_DIM = N_EMBD // N_HEAD
        B, T = (2, 256)
        Bb, Tt, C = x.shape
        H, hd = (N_HEAD, HEAD_DIM)
        gating = jax.nn.softmax(x @ W_gate.T, axis=-1)
        idx = jnp.argmax(gating, axis=-1)
        indicator = jax.nn.one_hot(idx, H, dtype=gating.dtype)
        top1_val = jnp.max(gating, axis=-1, keepdims=True)
        gating_top1 = indicator * top1_val
        qkv = x @ W_qkv.T
        q, k, v = jnp.split(qkv, 3, axis=-1)
        k = k.reshape(Bb, Tt, H, hd)
        v = v.reshape(Bb, Tt, H, hd)
        k_shared = jnp.einsum('bth,bthd->btd', indicator, k)
        v_shared = jnp.einsum('bth,bthd->btd', gating_top1, v)
        q = q.reshape(Bb, Tt, H, hd).transpose(0, 2, 1, 3)
        att = jnp.einsum('bhqd,bkd->bhqk', q, k_shared) * (1.0 / math.sqrt(hd))
        causal = jnp.tril(jnp.ones((Tt, Tt), dtype=bool))
        att = jnp.where(causal[None, None, :, :], att, -jnp.inf)
        att = jax.nn.softmax(att, axis=-1)
        y = jnp.einsum('bhqk,bkd->bhqd', att, v_shared)
        y = y.transpose(0, 2, 1, 3).reshape(Bb, Tt, C)
        return y

    def _L1_attn_ref(hidden_states, W_z, b_z, W_h, b_h, ln_w, ln_b, h0):
        import jax, jax.numpy as jnp
        import numpy as np
        B, T, H = (4, 512, 256)
        G_EPS = 0.5
        LN_EPS = 1e-05
        INIT_STD = 0.02

        def _g_log(x):
            return jnp.where(x >= 0, jnp.log(jax.nn.relu(x) + G_EPS), -jax.nn.softplus(-x))
        Bc, Tc, Hc = hidden_states.shape
        k = hidden_states @ W_z.T + b_z
        log_z = -jax.nn.softplus(-k)
        log_coeffs = -jax.nn.softplus(k)
        log_tilde_h = _g_log(hidden_states @ W_h.T + b_h)
        log_h0 = jnp.broadcast_to(_g_log(h0), (Bc, 1, Hc))
        log_values = jnp.concatenate([log_h0, log_z + log_tilde_h], axis=1)
        a_star = jnp.pad(jnp.cumsum(log_coeffs, axis=-1), ((0, 0), (1, 0), (0, 0)))
        log_h = a_star + jax.lax.cumlogsumexp(log_values - a_star, axis=1)
        log_h = (log_h - log_h.mean()) / jnp.std(log_h, ddof=1)
        h = jnp.exp(log_h)[:, 1:, :]
        x = h + hidden_states
        mu = x.mean(axis=-1, keepdims=True)
        var = x.var(axis=-1, keepdims=True)
        return (x - mu) * jax.lax.rsqrt(var + LN_EPS) * ln_w + ln_b

    def _L1_ffn_ref(hidden_states, router_w, w_gate_up, w_down, shared_gate_up, shared_down):
        import jax, jax.numpy as jnp
        import numpy as np
        B, S, D, F, E, K = (2, 256, 256, 512, 8, 1)

        def _silu_mul(gu):
            g, u = jnp.split(gu, 2, axis=-1)
            return jax.nn.silu(g) * u

        def _moe_forward(hidden_states, router_w, w_gate_up, w_down, shared_gate_up, shared_down, top_k=K):
            b, s, d = hidden_states.shape
            x = hidden_states.reshape(-1, d)
            router_logits = x @ router_w.T
            topk_vals, topk_ids = jax.lax.top_k(router_logits, top_k)
            gate = jax.nn.sigmoid(topk_vals.astype(jnp.float32)).astype(x.dtype)
            xs = (x[:, None, :] * gate[:, :, None]).reshape(-1, d)
            ids_flat = topk_ids.reshape(-1)
            n_experts = w_gate_up.shape[0]

            def body(acc, inp):
                wg, wd, e = inp
                h = _silu_mul(xs @ wg)
                o = h @ wd
                mask = (ids_flat == e)[:, None]
                return (acc + jnp.where(mask, o, jnp.zeros((), o.dtype)), None)
            acc0 = jnp.zeros_like(xs)
            routed, _ = jax.lax.scan(body, acc0, (w_gate_up, w_down, jnp.arange(n_experts)))
            routed = routed.reshape(-1, top_k, d).sum(1)
            shared = _silu_mul(x @ shared_gate_up) @ shared_down
            return (routed + shared).reshape(b, s, d)
        return _moe_forward(hidden_states, router_w, w_gate_up, w_down, shared_gate_up, shared_down)
    x = L0_attn_hidden_states
    xn = _layernorm(x, axis=-1)
    s = _L0_attn_ref(xn, L0_attn_wq_a, L0_attn_q_a_ln_w, L0_attn_wq_b, L0_attn_wkv_a, L0_attn_kv_a_ln_w, L0_attn_wkv_b, L0_attn_wo)
    g = _silu(_L0_ffn_ref(xn, L0_ffn_W_gate, L0_ffn_W_qkv))
    x = x + s * g
    xn = _layernorm(x, axis=-1)
    s = _L1_attn_ref(xn, L1_attn_W_z, L1_attn_b_z, L1_attn_W_h, L1_attn_b_h, L1_attn_ln_w, L1_attn_ln_b, L1_attn_h0)
    g = _silu(_L1_ffn_ref(xn, L1_ffn_router_w, L1_ffn_w_gate_up, L1_ffn_w_down, L1_ffn_shared_gate_up, L1_ffn_shared_down))
    x = x + s * g
    return x

_drawn_inputs = setup_inputs


def setup_inputs(seed=0):
    import zlib

    import numpy as np

    out = dict(_drawn_inputs(seed))
    spreads = {'L0_attn_q_a_ln_w': (1.0, 0.6),
     'L0_attn_kv_a_ln_w': (1.0, 0.6),
     'L1_attn_b_z': (0.0, 0.8),
     'L1_attn_b_h': (0.0, 2.0),
     'L1_attn_ln_w': (1.0, 0.6),
     'L1_attn_ln_b': (0.0, 0.8)}
    factors = {'L0_attn_wq_a': 8.0,
     'L0_attn_wq_b': 8.0,
     'L0_attn_wkv_a': 8.0,
     'L0_attn_wkv_b': 8.0,
     'L0_attn_wo': 8.0,
     'L0_ffn_W_gate': 8.0,
     'L0_ffn_W_qkv': 8.0,
     'L1_attn_W_z': 7.241,
     'L1_attn_W_h': 8.0,
     'L1_attn_h0': 64.0,
     'L1_ffn_router_w': 8.0,
     'L1_ffn_w_gate_up': 8.0,
     'L1_ffn_w_down': 8.0,
     'L1_ffn_shared_gate_up': 4.473,
     'L1_ffn_shared_down': 4.464}
    for name, (base, spread) in spreads.items():
        noise = np.random.default_rng([zlib.crc32(name.encode()), seed]).standard_normal(out[name].shape)
        drawn = base * np.exp(spread * noise) if base else spread * noise
        out[name] = jnp.asarray(drawn.astype(out[name].dtype))
    for name, factor in factors.items():
        out[name] = (out[name] * factor).astype(out[name].dtype)
    return out
```

```python
import concourse.bass as bass
from concourse import mybir
from contextlib import ExitStack

P = 128
NB, S, D = 4, 256, 256
TOK = NB * S
NT = TOK // P
DK = D // P
NH = 16
QL, KVL, NOPE, ROPE, VH = 192, 64, 128, 64, 128
QL2 = QL - P
SCALE = float(NOPE + ROPE) ** -0.5
HD = D // NH
SLOT = 32
FSCALE = float(HD) ** -0.5
W_IN = QL + KVL + ROPE + NH
FF, E = 512, 8
NW = E + 1
T1 = S + 1
BIG = 3.0e38
WIDE = 3 * P


def constants():
    import numpy as np
    i = np.arange(P)
    ident = np.eye(P, dtype=np.float32)
    upper = (i[:, None] <= i[None, :]).astype(np.float32)
    diag = np.where(i[None, :] > i[:, None], np.float32(BIG), np.float32(0))
    mask = np.concatenate([diag, np.zeros((P, P), np.float32), diag], axis=1)
    inv = (np.float32(1.0) / np.float32(10000.0) ** (np.arange(0, ROPE, 2, dtype=np.float32) / np.float32(ROPE))).astype(np.float32)
    f = np.arange(S, dtype=np.float32)[:, None] * inv[None, :]
    cos, sin = np.cos(f.astype(np.float64)), np.sin(f.astype(np.float64))
    tok = np.concatenate([cos.reshape(2, P, 32), sin.reshape(2, P, 32)], axis=0).transpose(1, 0, 2)
    feat = np.zeros((P, 2, S))
    feat[64:, 0] = np.concatenate([cos.T, cos.T], axis=0) * -SCALE
    feat[64:, 1] = np.concatenate([-sin.T, sin.T], axis=0) * -SCALE
    return {
        "c_ident": ident, "c_upper": upper, "c_mask": mask,
        "c_rope_tok": np.ascontiguousarray(tok, dtype=np.float32).reshape(P, 4 * 32),
        "c_rope_feat": feat.astype(np.float32).reshape(P, 2 * S),
        "c_iota": np.broadcast_to(np.arange(NH, dtype=np.float32), (P, NH)).copy(),
    }


def recurrent_kernel(nc, a, out, debug=None):
    f32 = mybir.dt.float32
    ALU = mybir.AluOpType
    ACT = mybir.ActivationFunctionType
    X = mybir.AxisListType.X
    ds = bass.ds

    ctx = ExitStack()
    with ctx:
        def sb(name, shape):
            return ctx.enter_context(nc.sbuf_tensor(name, shape, f32))

        sems = {}

        def sem(name):
            if name not in sems:
                sems[name] = ctx.enter_context(nc.semaphore(name))
            return sems[name]

        ident = sb("ident", [P, P])
        upper = sb("upper", [P, P])
        ones = sb("ones", [P, P])
        mask = sb("mask", [P, WIDE])
        rope_tok = sb("rope_tok", [P, 4, 32])
        rope_feat = sb("rope_feat", [P, 2, S])
        iota = sb("iota", [P, NH])
        x_res = sb("x_res", [P, NT, D])
        xn = sb("xn", [P, NT, D])
        xnT = sb("xnT", [P, DK, TOK])
        y = sb("y", [P, NT, D])
        st = sb("st", [P, NT, 6])
        mv = sb("mv", [P, NT, 2])
        half_neg = sb("half_neg", [P, 2 * NT])
        ve = sb("ve", [P, NT])
        rstd = sb("rstd", [P, NT])
        scr = [sb(f"scr{k}", [P, WIDE]) for k in range(2)]
        prob = [sb(f"prob{k}", [P, WIDE]) for k in range(2)]
        probT = [sb(f"probT{k}", [P, WIDE]) for k in range(2)]
        mx = sb("mx", [P, 2, 8])
        stand = sb("stand", [P, 16])
        rs = sb("rs", [P, 2, 8])
        ri = sb("ri", [P, 2, 8])
        qaT0 = sb("qaT0", [P, TOK])
        qaT1 = sb("qaT1", [QL2, TOK])
        kT = sb("kT", [P, TOK])
        kc = sb("kc", [P, NT, P])
        kshT = sb("kshT", [P, TOK])
        vsh = sb("vsh", [P, NT, HD])
        wo_abs = sb("wo_abs", [P, NH // 2, D])
        RA = sb("RA", [P, 8192])
        RB = sb("RB", [P, 9216])
        RC = sb("RC", [P, 4096])
        RD = sb("RD", [P, 8192])

        ps = ctx.enter_context(nc.psum_tensor("ps", [P, 8, 512], f32))

        kvraw = RA[:, 0:4096].rearrange("p (t c) -> p t c", t=NT)
        gtmp = RA[:, 4096:6144].rearrange("p (t d h) -> p t d h", t=NT, d=HD)
        qs = RA[:, 6144:6144 + NT * QL].rearrange("p (t c) -> p t c", t=NT)
        xcT = RA[:, :].rearrange("p (n t) -> p n t", n=NH // 2)
        w_nope = RB[:, 0:NH * QL].rearrange("p (h c) -> p h c", h=NH)
        w_kabs = RB[:, 3072:4096].rearrange("p (h c) -> p h c", h=NH)
        w_oabs = RB[:, 4096:5120].rearrange("p (h c) -> p h c", h=NH)
        w_o = RB[:, 5120:9216].rearrange("p (h c) -> p h c", h=NH)
        QT = RC[:, :].rearrange("p (g t) -> p g t", g=4)
        w_in = sb("w_in", [P, DK, W_IN])
        w_kv = sb("w_kv", [P, DK, 2 * D])
        w_q = sb("w_q", [P, DK, 512])
        yflat = y[:, :, :].rearrange("p t c -> p (t c)")
        w_pe0 = yflat[:, 0:1024].rearrange("p (h c) -> p h c", h=NH)
        w_pe1 = yflat[0:QL2, 1024:2048].rearrange("p (h c) -> p h c", h=NH)
        w_abs0 = RB[:, 0:1024].rearrange("p (h c) -> p h c", h=NH)
        w_abs1 = RB[0:QL2, 1024:2048].rearrange("p (h c) -> p h c", h=NH)
        lnq = sb("lnq", [P, 2])
        lnkv = sb("lnkv", [P, KVL])
        praw = RD[:, 0:NT * W_IN].rearrange("p (t c) -> p t c", t=NT)
        qh = [RD[:, k * 1024:(k + 1) * 1024] for k in range(2)]
        rot = RD[:, 2048:3072]
        t1 = RD[:, 3072:4096]
        t2 = RD[:, 4096:5120]
        xcn = RD[:, 5120:6144].rearrange("p (t c) -> p t c", t=NT)
        ws0 = [RD[:, 6144 + k * P:6144 + (k + 1) * P] for k in range(2)]
        ws1 = [RD[0:QL2, 6400 + k * P:6400 + (k + 1) * P] for k in range(2)]
        QS = RD[:, 6656:7680]
        small = sb("small", [P, 32, NT])
        oneh = sb("oneh", [P, NT, NH])
        gsm = RD[:, 7936:8064].rearrange("p (t h) -> p t h", t=NT)
        kred = RD[:, 7680:7936].rearrange("p (w t d) -> p w t d", w=2, t=NT)
        krep = RD[:, 4096:5120].rearrange("p (t r s) -> p t r s", t=NT, r=4)

        bar = {}
        marks = []

        def dump(eng, name, ap):
            if debug is not None and name in debug:
                eng.dma_start(debug[name], ap).then_inc(sem("s_dbg"), 16)
                marks.append(name)
                eng.wait_ge(sem("s_dbg"), 16 * len(marks))

        def phase_end(eng, k):
            eng.drain().then_inc(sem(f"s_phase{k}"), 1)
            eng.wait_ge(sem(f"s_phase{k}"), 5)

        def chain(eng, name):
            n = [0]

            def link(ins):
                n[0] += 1
                ins.then_inc(sem(name), 1)
                eng.wait_ge(sem(name), n[0])
                return ins
            return link

        SB = [0, 1]
        TB = [2, 3]
        AB = 4

        class Core:
            def __init__(self, tag, heads, vw, q_of, k_of, v_of, contraction):
                self.tag, self.heads, self.vw = tag, heads, vw
                self.q_of, self.k_of, self.v_of = q_of, k_of, v_of
                self.U = heads * NB
                s = lambda x: sem(f"{x}_{tag}")
                self.s_S, self.s_mx, self.s_P, self.s_T = s("s_scores"), s("s_max"), s("s_probs"), s("s_turned")
                self.s_pt, self.s_av, self.s_xn, self.s_ri = s("s_turned_sb"), s("s_heads"), s("s_normed"), s("s_recip")
                self.av = ps[:, AB, 0:NT * vw].rearrange("p (t c) -> p t c", t=NT)

        def pe_scores(pe, c, i, l, first):
            j, b, u = l // NB, l % NB, i * c.U + l
            if not (first and l < 2):
                pe.wait_ge(c.s_mx, u - 1)
            bank = ps[:, SB[l % 2], :]
            nc.tensor.matmul(bank[:, 0:P], c.q_of(j, 2 * b), c.k_of(j, b, P), start=True, stop=True)
            nc.tensor.matmul(bank[:, P:WIDE], c.q_of(j, 2 * b + 1), c.k_of(j, b, S), start=True, stop=True)\
                .then_inc(c.s_S, 1)

        def pe_turn(pe, c, u, l, early):
            pe.wait_ge(c.s_P, u + 1)
            if not early:
                pe.wait_ge(c.s_pt, u - 1)
            for k in range(3):
                last = nc.tensor.transpose(ps[:, TB[l % 2], k * P:(k + 1) * P], prob[l % 2][:, k * P:(k + 1) * P],
                                           ident[:, :])
            last.then_inc(c.s_T, 1)

        def pe_heads(pe, c, u, l, n, b, early):
            pe.wait_ge(c.s_pt, u + 1)
            if b == 0 and not early:
                pe.wait_ge(c.s_xn, n)
            pt = probT[l % 2]
            nc.tensor.matmul(c.av[:, 2 * b, :], pt[:, 0:P], c.v_of(2 * b), start=True, stop=True)
            nc.tensor.matmul(c.av[:, 2 * b + 1, :], pt[:, P:2 * P], c.v_of(2 * b), start=True, stop=False)
            nc.tensor.matmul(c.av[:, 2 * b + 1, :], pt[:, 2 * P:WIDE], c.v_of(2 * b + 1), start=False, stop=True)\
                .then_inc(c.s_av, 1)

        def dve_max(dve, c, i, l, first):
            j, b, u = l // NB, l % NB, i * c.U + l
            dve.wait_ge(c.s_S, u + 1)
            if not (first and l < 2):
                dve.wait_ge(c.s_P, u - 1)
            if not isinstance(i, int):
                nc.vector.memset(stand[:, l:l + 1], 0.0)
            for q, (lo, hi) in enumerate(((0, P), (P, WIDE))):
                last = nc.vector.tensor_tensor_reduce(
                    out=scr[l % 2][:, lo:hi], in0=ps[:, SB[l % 2], lo:hi], in1=mask[:, lo:hi], scale=1.0, scalar=BIG,
                    op0=ALU.add, op1=ALU.min, accum_out=mx[:, j % 2, 2 * b + q:2 * b + q + 1])
                last.then_inc(c.s_mx, 1) if q else None

        def dve_turned(dve, c, u, l, early):
            dve.wait_ge(c.s_T, u + 1)
            if not early:
                dve.wait_ge(c.s_av, u - 1)
            nc.vector.tensor_copy(probT[l % 2][:, :], ps[:, TB[l % 2], 0:WIDE]).then_inc(c.s_pt, 1)

        def dve_norm(dve, c, n, j, dst):
            dve.wait_ge(c.s_P, 4 * n + 4)
            nc.vector.reciprocal(ri[:, j % 2, :], rs[:, j % 2, :]).then_inc(c.s_ri, 1)
            dve.wait_ge(c.s_av, 4 * n + 4)
            dve.wait_ge(c.s_ri, n + 1)
            nc.vector.tensor_tensor(dst, c.av, ri[:, j % 2, :].unsqueeze(2).broadcast_to([P, NT, c.vw]), ALU.mult)\
                .then_inc(c.s_xn, 1)

        def act_exp(act, c, i, l, first):
            j, b, u = l // NB, l % NB, i * c.U + l
            act.wait_ge(c.s_mx, u + 1)
            if not (first and l < 2):
                act.wait_ge(c.s_T, u - 1)
            if b == 0 and not (first and j < 2):
                act.wait_ge(c.s_xn, i * c.heads + j - 1)
            for q, (lo, hi) in enumerate(((0, P), (P, WIDE))):
                last = nc.scalar.activation(prob[l % 2][:, lo:hi], scr[l % 2][:, lo:hi], ACT.Exp,
                                            bias=mx[:, j % 2, 2 * b + q:2 * b + q + 1], scale=-1.0,
                                            accum_out=rs[:, j % 2, 2 * b + q:2 * b + q + 1])
            last.then_inc(c.s_P, 1)

        mla = Core("mla", 2, KVL, lambda j, t: qh[j][:, t * P:(t + 1) * P],
                   lambda j, b, w: kT[:, b * S:b * S + w], lambda t: kc[:, t, 0:KVL], P)
        gat = Core("gat", 4, HD, lambda j, t: QS[SLOT * j:SLOT * (j + 1), t * P:(t + 1) * P],
                   lambda j, b, w: kshT[SLOT * j:SLOT * (j + 1), b * S:b * S + w], lambda t: vsh[:, t, :], SLOT)

        def loop(eng, iters, body):
            body(0, True, False)
            with eng.Fori(1, iters - 1) as i:
                body(i, False, False)
            body(iters - 1, False, True)

        QB = (5, 6)
        XB = 7
        NP = NH // 2
        Qp = ps[:, 5:7, :].rearrange("p k c -> p (k c)")

        hcat = RA[:, 0:2 * NB * T1].rearrange("p (f b t) -> p f b t", f=2, b=NB)
        kk = RA[:, 2056:2056 + 2048].rearrange("p (f t) -> p f t", f=2)
        mnh = RA[:, 4104:4104 + 2056].rearrange("p (f b t) -> p f b t", f=2, b=NB)
        e1 = RB[:, 0:2048].rearrange("p (f t) -> p f t", f=2)
        e2 = RB[:, 2048:2048 + 2056].rearrange("p (f b t) -> p f b t", f=2, b=NB)
        l3 = RB[:, 4104:4104 + 2056].rearrange("p (f b t) -> p f b t", f=2, b=NB)
        dd = RB[:, 6160:6160 + 2056].rearrange("p (f b t) -> p f b t", f=2, b=NB)
        mk = RC[:, 0:2048].rearrange("p (f t) -> p f t", f=2)
        sp = RC[:, 2048:4096].rearrange("p (f t) -> p f t", f=2)
        acum = RD[:, 0:2048].rearrange("p (f t) -> p f t", f=2)
        mm = RD[:, 2048:2048 + 2056].rearrange("p (f b t) -> p f b t", f=2, b=NB)
        ss = RD[:, 4104:4104 + 2056].rearrange("p (f b t) -> p f b t", f=2, b=NB)
        hout = RA[:, 0:2048].rearrange("p (f t) -> p f t", f=2)
        s1 = RC[:, 0:2048].rearrange("p (t c) -> p t c", t=NT)
        x2 = RC[:, 2048:4096].rearrange("p (t c) -> p t c", t=NT)
        wz = w_kv[:, :, 0:D]
        wh = w_kv[:, :, D:2 * D]
        bz = sb("bz", [P, 3, 2])
        ln1 = sb("ln1", [P, 2, D])
        wr = sb("wr", [P, DK, E])
        wgu = [RD[:, k * 2048:(k + 1) * 2048].rearrange("p (k c) -> p k c", k=DK) for k in range(2)]
        wd = [RD[:, 4096 + k * 1024:4096 + (k + 1) * 1024].rearrange("p (k c) -> p k c", k=4) for k in range(2)]
        gcol = sb("gcol", [P, NT, NW])
        ccol = sb("ccol", [P, NT, NW])
        rl = sb("rl", [P, NT, E])
        roneh = sb("roneh", [P, NT, E])
        acc = RB[:, 0:2048].rearrange("p (t c) -> p t c", t=NT)
        hg = [RB[:, 2048 + k * 512:2560 + k * 512] for k in range(2)]
        hh = [RB[:, 3072 + k * 512:3584 + k * 512] for k in range(2)]
        hT = [RB[:, 4096 + k * 512:4608 + k * 512] for k in range(2)]
        EPI = 2

        block = ctx.enter_context(nc.Block())

        @block.sync
        def _(sp_):
            eng = sp_
            x_v = a["x"].rearrange("(t p) d -> p t d", p=P)
            load = lambda s, dst, src: eng.dma_start(dst, src).then_inc(sem(s), 16)
            for h in range(2):
                load(f"s_x{h}", x_res[:, 4 * h:4 * h + 4, :], x_v[:, 4 * h:4 * h + 4, :])
            load("s_ident", ident[:, :], a["c_ident"])
            kview = lambda w: w.rearrange("(k p) c -> p k c", p=P)
            load("s_win", w_in[:, :, :], kview(a["w_in"]))
            load("s_wkv", w_kv[:, :, :], kview(a["w_kv"]))
            load("s_wq", w_q[:, :, :], kview(a["w_q"]))
            load("s_wnope", w_nope, a["w_nope"].rearrange("h p c -> p h c"))
            load("s_wkabs", w_kabs, a["w_kabs"].rearrange("h p c -> p h c"))
            load("s_woabs", w_oabs, a["w_oabs"].rearrange("h p c -> p h c"))
            load("s_wo", w_o, a["w_o"].rearrange("(h p) c -> p h c", p=P))
            load("s_small", w_pe0[:, :, :], a["w_pe"][0:P].rearrange("p (h c) -> p h c", h=NH))
            load("s_small", w_pe1[:, :, :], a["w_pe"][P:QL].rearrange("p (h c) -> p h c", h=NH))
            load("s_small", lnq[:, 0:1], a["q_ln"][0:P].unsqueeze(1))
            load("s_small", lnq[0:QL2, 1:2], a["q_ln"][P:QL].unsqueeze(1))
            load("s_small", lnkv[:, :], a["kv_ln"].unsqueeze(0).broadcast_to([P, KVL]))
            load("s_small", mask[:, :], a["c_mask"])
            load("s_small", upper[:, :], a["c_upper"])
            load("s_small", rope_tok[:, :, :], a["c_rope_tok"].rearrange("p (k c) -> p k c", k=4))
            load("s_small", rope_feat[:, :, :], a["c_rope_feat"].rearrange("p (k c) -> p k c", k=2))
            load("s_small", iota[:, :], a["c_iota"])
            load("s_small", bz[:, :, :], a["rows_l1"])
            for k, name in enumerate(("ln_w", "ln_b")):
                load("s_small", ln1[:, k, :], a[name].unsqueeze(0).broadcast_to([P, D]))
            load("s_small", wr[:, :, :], kview(a["w_router"]))
            phase_end(eng, 0)
            load("s_wz", wz, kview(a["w_z"]))
            load("s_wz", wh, kview(a["w_h"]))
            for k in range(1, 5):
                phase_end(eng, k)
            def weights(n, k, wait):
                if wait is not None:
                    eng.wait_ge(sem("s_down"), wait)
                gu = a["w_gu"] if not (isinstance(n, int) and n == E) else a["w_shared_gu"]
                dn = a["w_dn"] if not (isinstance(n, int) and n == E) else a["w_shared_dn"]
                if isinstance(n, int) and n == E:
                    eng.dma_start(wgu[k], gu.rearrange("(k p) c -> p k c", p=P)).then_inc(sem(f"s_wexp{k}"), 16)
                    eng.dma_start(wd[k], dn.rearrange("(k p) c -> p k c", p=P)).then_inc(sem(f"s_wexp{k}"), 16)
                else:
                    g = gu[ds(n, 1)].rearrange("e (k p) c -> p (e k) c", p=P)
                    d = dn[ds(n, 1)].rearrange("e (k p) c -> p (e k) c", p=P)
                    eng.dma_start(wgu[k], g).then_inc(sem(f"s_wexp{k}"), 16)
                    eng.dma_start(wd[k], d).then_inc(sem(f"s_wexp{k}"), 16)
            weights(0, 0, None)
            weights(1, 1, None)
            with eng.Fori(1, E // 2) as i:
                weights(2 * i, 0, (2 * i - 1) * NT)
                weights(2 * i + 1, 1, 2 * i * NT)
            weights(E, 0, (E - 1) * NT)
            phase_end(eng, 5)
            o_v = out.rearrange("(t p) d -> p t d", p=P)
            for h in range(2):
                eng.wait_ge(sem("s_final"), h + 1)
                eng.dma_start(o_v[:, 4 * h:4 * h + 4, :], x2[:, 4 * h:4 * h + 4, :]).then_inc(sem("s_out"), 16)
            eng.wait_ge(sem("s_out"), 32)

        def layer_norm_stats(eng, link, src, wait=None):
            for t in range(NT):
                if wait is not None:
                    wait(t)
                last = nc.vector.bn_stats(st[:, t, :], src[:, t, :])
            link(last)
            for t in range(NT):
                last = nc.vector.bn_aggr(mv[:, t, :], st[:, t, :])
            link(last)

        @block.vector
        def _(dve):
            link = chain(dve, "s_dve_chain")
            told = {}

            def tell(ins, name):
                told[name] = told.get(name, 0) + 1
                ins.then_inc(sem(name), 1)
                dve.wait_ge(sem(name), told[name])
            tt = nc.vector.tensor_tensor
            tsc = nc.vector.tensor_scalar

            def normalise(k, src, dst, signal, wait=None):
                layer_norm_stats(dve, link, src, wait)
                tsc(ve[:, :], mv[:, :, 1], 1e-5, None, ALU.add).then_inc(sem("s_var"), 1)
                dve.wait_ge(sem("s_rstd"), k)
                for t in range(NT):
                    tsc(dst[:, t, :], src[:, t, :], mv[:, t, 0:1], rstd[:, t:t + 1], ALU.subtract, ALU.mult)\
                        .then_inc(sem(signal), 1)

            nc.vector.memset(ones[:, :], 1.0).then_inc(sem("s_ones"), 1)
            nc.vector.memset(krep[:, :, :, :], 0.0)
            normalise(1, x_res, xn, "s_xn0", lambda t: dve.wait_ge(sem(f"s_x{t // 4}"), 16) if t % 4 == 0 else None)

            for k in range(8):
                dve.wait_ge(sem("s_wprep"), max(k + 1, 4))
                if k < 2:
                    nc.vector.tensor_copy(w_abs0[:, 8 * k:8 * k + 8, :],
                                          ps[:, k, :].rearrange("p (h c) -> p h c", h=8)).then_inc(sem("s_wprep_sb"), 1)
                elif k < 4:
                    nc.vector.tensor_copy(w_abs1[:, 8 * (k - 2):8 * (k - 2) + 8, :],
                                          ps[0:QL2, k, :].rearrange("p (h c) -> p h c", h=8)).then_inc(sem("s_wprep_sb"), 1)
                else:
                    nc.vector.tensor_copy(wo_abs[:, 2 * (k - 4):2 * (k - 4) + 2, :],
                                          ps[:, k, :].rearrange("p (h c) -> p h c", h=2)).then_inc(sem("s_wprep_sb"), 1)
            for t in range(NT):
                dve.wait_ge(sem("s_kvp"), t + 1)
                nc.vector.tensor_copy(kvraw[:, t, :], ps[:, 4 + t % 2, :]).then_inc(sem("s_kvraw"), 1)
            for g in range(4):
                dve.wait_ge(sem("s_QTp"), g + 1)
                tsc(QT[:, g, :], ps[:, 2 * (g % 2):2 * (g % 2) + 2, :].rearrange("p k c -> p (k c)"), -FSCALE, None, ALU.mult)\
                    .then_inc(sem("s_QT"), 1)

            dve.wait_ge(sem("s_small"), 16 * 14)
            dve.wait_ge(sem("s_sumsq"), NT)
            tsc(small[:, 0, :], small[:, 2, :], 1.0 / QL, 1e-6, ALU.mult, ALU.add)
            tsc(small[:, 1, :], small[:, 3, :], 1.0 / KVL, 1e-6, ALU.mult, ALU.add).then_inc(sem("s_ms"), 1)
            dve.wait_ge(sem("s_rms"), 1)
            rq = small[:, 4, :]
            rk = small[:, 5, :]
            tt(qs[:, :, :], praw[:, :, 0:QL], rq.unsqueeze(2).broadcast_to([P, NT, QL]), ALU.mult).then_inc(sem("s_qs"), 1)
            link(tt(kc[:, :, 0:KVL], praw[:, :, QL:QL + KVL], rk.unsqueeze(2).broadcast_to([P, NT, KVL]), ALU.mult))
            link(tt(kc[:, :, 0:KVL], kc[:, :, 0:KVL], lnkv[:, :].unsqueeze(1).broadcast_to([P, NT, KVL]), ALU.mult))
            pe_v = praw[:, :, QL + KVL:QL + KVL + ROPE].rearrange("p (b h) c -> p b h c", b=NB)
            kp_v = kc[:, :, KVL:P].rearrange("p (b h) c -> p b h c", b=NB)
            rt = [gtmp.rearrange("p t d h -> p (t d h)")[:, k * 256:(k + 1) * 256]
                  .rearrange("p (b h c) -> p b h c", b=NB, h=2) for k in range(4)]
            for h in range(2):
                co = rope_tok[:, h, :].unsqueeze(1).broadcast_to([P, NB, 32])
                si = rope_tok[:, 2 + h, :].unsqueeze(1).broadcast_to([P, NB, 32])
                a1, a2 = pe_v[:, :, h, 0:32], pe_v[:, :, h, 32:64]
                tt(rt[0][:, :, h, :], a1, co, ALU.mult)
                tt(rt[1][:, :, h, :], a2, si, ALU.mult)
                tt(rt[2][:, :, h, :], a2, co, ALU.mult)
                link(tt(rt[3][:, :, h, :], a1, si, ALU.mult))
                tt(kp_v[:, :, h, 0:32], rt[0][:, :, h, :], rt[1][:, :, h, :], ALU.subtract)
                last = tt(kp_v[:, :, h, 32:64], rt[2][:, :, h, :], rt[3][:, :, h, :], ALU.add)
            tell(last, "s_kc")

            gl = praw[:, :, QL + KVL + ROPE:W_IN]
            gm = small[:, 6, :]
            bc = lambda v: v.unsqueeze(2).broadcast_to([P, NT, NH])
            io = iota[:, :].unsqueeze(1).broadcast_to([P, NT, NH])
            link(nc.vector.tensor_reduce(gm, gl, X, ALU.max))
            tt(gsm[:, :, :], gl, bc(gm), ALU.subtract).then_inc(sem("s_gsub"), 1)
            link(tt(oneh[:, :, :], gl, bc(gm), ALU.is_equal))
            link(nc.vector.scalar_tensor_tensor(oneh[:, :, :], oneh[:, :, :], -float(NH), io, ALU.mult, ALU.add))
            link(nc.vector.tensor_reduce(small[:, 7, :], oneh[:, :, :], X, ALU.min))
            link(tsc(small[:, 7, :], small[:, 7, :], float(NH), None, ALU.add))
            link(tt(oneh[:, :, :], io, bc(small[:, 7, :]), ALU.is_equal))
            dve.wait_ge(sem("s_gexp"), 1)
            link(nc.vector.tensor_reduce(small[:, 8, :], gsm[:, :, :], X, ALU.add))
            link(nc.vector.reciprocal(small[:, 9, :], small[:, 8, :]))
            for w in range(2):
                for t in range(NT):
                    last = tt(gtmp[:, t], kvraw[:, t, w * D:(w + 1) * D].rearrange("p (h d) -> p d h", h=NH),
                              oneh[:, t, :].unsqueeze(1).broadcast_to([P, HD, NH]), ALU.mult)
                link(last)
                link(nc.vector.tensor_reduce(kred[:, w], gtmp, X, ALU.add))
            tt(vsh[:, :, :], kred[:, 1], small[:, 9, :].unsqueeze(2).broadcast_to([P, NT, HD]), ALU.mult)
            for r in range(4):
                last = nc.vector.tensor_copy(krep[:, :, r, 0:HD], kred[:, 0])
            last.then_inc(sem("s_krep"), 1)
            dve.wait_ge(sem("s_krep"), 1)

            for k in range(2):
                dve.wait_ge(sem("s_latT"), 2 * k + 1)
                tsc(qaT0[:, 512 * k:512 * k + 512], ps[:, k, :], lnq[:, 0:1], None, ALU.mult)
                dve.wait_ge(sem("s_latT"), 2 * k + 2)
                tsc(qaT1[:, 512 * k:512 * k + 512], ps[0:QL2, 2 + k, :], lnq[0:QL2, 1:2], None, ALU.mult)
            phase_end(dve, 0)

            def head_t1(n, first):
                dve.wait_ge(sem("s_rot"), 2 * n + 2)
                if not first:
                    dve.wait_ge(sem("s_qrope"), n)
                cs = rope_feat[64:P, 0, :].unsqueeze(1).broadcast_to([64, NB, S])
                tt(t1[64:P, :].rearrange("p (b s) -> p b s", b=NB), Qp[64:P, :].rearrange("p (b s) -> p b s", b=NB), cs, ALU.mult)\
                    .then_inc(sem("s_t1"), 1)

            def body(i, first, last):
                for l in range(mla.U):
                    u, j = i * mla.U + l, l // NB
                    n = 2 * i + j
                    dve_max(dve, mla, i, l, first)
                    if not (first and l == 0):
                        dve_turned(dve, mla, u - 1, l - 1, first and l < 3)
                    if l % NB == 1 and not (last and j == 1):
                        head_t1(n + 1, False)
                    if l % NB == 2 and not (first and j == 0):
                        if j == 1 and not first:
                            dve.wait_ge(sem("s_xT"), 2 * i)
                        m = (j - 1) % 2
                        dve_norm(dve, mla, n - 1, m, xcn[:, :, m * KVL:(m + 1) * KVL])
                if last:
                    dve_turned(dve, mla, i * mla.U + mla.U - 1, mla.U - 1, False)
                    dve_norm(dve, mla, 2 * i + 1, 1, xcn[:, :, KVL:P])
            head_t1(0, True)
            loop(dve, NP, body)
            phase_end(dve, 1)

            def bodyg(i, first, last):
                for l in range(gat.U):
                    u, j = i * gat.U + l, l // NB
                    n = 4 * i + j
                    dve_max(dve, gat, i, l, first)
                    if not (first and l == 0):
                        dve_turned(dve, gat, u - 1, l - 1, first and l < 3)
                    if l % NB == 2 and not (first and j == 0):
                        dve_norm(dve, gat, n - 1, j - 1, y[:, :, ds((n - 1) * HD, HD)])
                if last:
                    dve_turned(dve, gat, i * gat.U + gat.U - 1, gat.U - 1, False)
                    dve_norm(dve, gat, 4 * i + 3, 3, y[:, :, ds((4 * i + 3) * HD, HD)])
            loop(dve, 4, bodyg)
            dve.wait_ge(sem("s_g0"), 1)
            for k in range(4):
                dve.wait_ge(sem("s_sp"), k + 1)
                link(tt(y[:, 2 * k:2 * k + 2, :], ps[:, 5 + k % 2, :].rearrange("p (t c) -> p t c", t=2),
                        y[:, 2 * k:2 * k + 2, :], ALU.mult))
                tell(tt(x_res[:, 2 * k:2 * k + 2, :], x_res[:, 2 * k:2 * k + 2, :], y[:, 2 * k:2 * k + 2, :], ALU.add), "s_spr")
            phase_end(dve, 2)

            normalise(2, x_res, xn, "s_xn1")
            flat = lambda v: v.rearrange("p f b t -> p f (b t)")
            dve.wait_ge(sem("s_kh_sb"), 1)
            dve.wait_ge(sem("s_kh_sb"), 2)
            tell(tsc(mnh, hcat, 0.0, None, ALU.min), "s_mnh")
            dve.wait_ge(sem("s_absk"), 1)
            link(tsc(mk, kk, 0.0, None, ALU.min))
            link(tsc(kk, kk, 0.0, None, ALU.max))
            tsc(l3, hcat, 0.0, 2.0, ALU.max, ALU.mult).then_inc(sem("s_num"), 1)
            dve.wait_ge(sem("s_l1"), 1)
            tell(tt(sp, kk, e1, ALU.add), "s_softplus")
            link(tt(mk, mk, e1, ALU.subtract))
            dve.wait_ge(sem("s_l3"), 1)
            link(tt(l3, l3, e2, ALU.subtract))
            link(tt(l3, l3, mnh, ALU.add))
            v4 = lambda v, f: v[:, f].rearrange("p (b t) -> p b t", b=NB)
            for f in range(2):
                dve.wait_ge(sem("s_acum"), f + 1)
                link(nc.vector.tensor_copy(acum[:, f, :], ps[:, 2 * f:2 * f + 2, :].rearrange("p k c -> p (k c)")))
                link(tt(mk[:, f, :], mk[:, f, :], acum[:, f, :], ALU.add))
                link(tt(l3[:, f, :, 1:T1], l3[:, f, :, 1:T1], v4(mk, f), ALU.add))
            link(nc.vector.memset(dd, 0.0))
            for f in range(2):
                for b in range(NB):
                    last = nc.vector.tensor_tensor_scan(mm[:, f, b, :], l3[:, f, b, :], l3[:, f, b, :], -BIG,
                                                        op0=ALU.max, op1=ALU.max)
            link(last)
            for f in range(2):
                tt(dd[:, f, :, 1:T1], mm[:, f, :, 0:S], mm[:, f, :, 1:T1], ALU.subtract)
                last = tt(l3[:, f], l3[:, f], mm[:, f], ALU.subtract)
            last.then_inc(sem("s_scan_in"), 1)
            dve.wait_ge(sem("s_scan_exp"), 1)
            for f in range(2):
                for b in range(NB):
                    last = nc.vector.tensor_tensor_scan(ss[:, f, b, :], dd[:, f, b, :], l3[:, f, b, :], 0.0,
                                                        op0=ALU.mult, op1=ALU.add)
            last.then_inc(sem("s_scan"), 1)
            dve.wait_ge(sem("s_scan_ln"), 1)
            link(tt(ss, ss, mm, ALU.add))
            for f in range(2):
                last = tt(ss[:, f, :, 1:T1], ss[:, f, :, 1:T1], v4(acum, f), ALU.subtract)
            link(last)
            nc.vector.tensor_reduce(small[:, 10, 0:1], ss.rearrange("p f b t -> p (f b t)"), X, ALU.add)\
                .then_inc(sem("s_sum"), 1)
            N = NB * T1 * D
            dve.wait_ge(sem("s_tot"), 1)
            tell(tsc(small[:, 11, 0:1], ps[:, 4, 0:1], -1.0 / N, None, ALU.mult), "s_mean")
            dve.wait_ge(sem("s_tot"), 2)
            tsc(small[:, 13, :], ps[:, 4, 1:2].broadcast_to([P, NT]), 1.0 / (N - 1), None, ALU.mult).then_inc(sem("s_varh"), 1)
            dve.wait_ge(sem("s_rstdh"), 1)
            tell(tt(small[:, 15, 0:1], small[:, 14, 0:1], small[:, 11, 0:1], ALU.mult), "s_hscale")
            for k in range(4):
                dve.wait_ge(sem("s_hback"), k + 1)
                last = tt(x2[:, 2 * k:2 * k + 2, :], ps[:, k, :].rearrange("p (t c) -> p t c", t=2), xn[:, 2 * k:2 * k + 2, :],
                          ALU.add)
            link(last)
            normalise(3, x2, s1, "s_s1")
            dve.wait_ge(sem("s_s1"), NT)
            link(tt(s1, s1, ln1[:, 0, :].unsqueeze(1).broadcast_to([P, NT, D]), ALU.mult))
            link(tt(s1, s1, ln1[:, 1, :].unsqueeze(1).broadcast_to([P, NT, D]), ALU.add))
            phase_end(dve, 3)

            dve.wait_ge(sem("s_router"), 1)
            rv = ps[:, 0, 0:NT * E].rearrange("p (t e) -> p t e", t=NT)
            link(nc.vector.tensor_copy(rl[:, :, :], rv))
            rb = lambda v: v.unsqueeze(2).broadcast_to([P, NT, E])
            ie = iota[:, 0:E].unsqueeze(1).broadcast_to([P, NT, E])
            tell(nc.vector.tensor_reduce(small[:, 16, :], rl[:, :, :], X, ALU.max), "s_top")
            link(tt(roneh[:, :, :], rl[:, :, :], rb(small[:, 16, :]), ALU.is_equal))
            link(nc.vector.scalar_tensor_tensor(roneh[:, :, :], roneh[:, :, :], -float(E), ie, ALU.mult, ALU.add))
            link(nc.vector.tensor_reduce(small[:, 17, :], roneh[:, :, :], X, ALU.min))
            link(tsc(small[:, 17, :], small[:, 17, :], float(E), None, ALU.add))
            link(tt(roneh[:, :, :], ie, rb(small[:, 17, :]), ALU.is_equal))
            nc.vector.memset(gcol[:, :, :], 1.0)
            link(nc.vector.memset(ccol[:, :, :], 1.0))
            dve.wait_ge(sem("s_gate_exp"), 1)
            link(tsc(small[:, 19, :], small[:, 18, :], 1.0, None, ALU.add))
            link(nc.vector.reciprocal(small[:, 20, :], small[:, 19, :]))
            link(nc.vector.tensor_copy(gcol[:, :, 0:E], rb(small[:, 20, :])))
            link(tt(ccol[:, :, 0:E], gcol[:, :, 0:E], roneh[:, :, :], ALU.mult))
            nc.vector.memset(acc, 0.0).then_inc(sem("s_gates"), 1)
            phase_end(dve, 4)

            def steps(n, m0, first, last):
                for t in range(NT):
                    m = n * NT + t
                    dve.wait_ge(sem("s_silu"), m + 1)
                    if not (first and t < 2):
                        dve.wait_ge(sem("s_hT"), m - 1)
                    nc.vector.scalar_tensor_tensor(hh[t % 2], hg[t % 2], ccol[:, t, ds(n, 1)], ps[:, 2 + t % 2, :],
                                                   ALU.mult, ALU.mult).then_inc(sem("s_h"), 1)
                    if not (first and t < 2):
                        addup(m - 2, (t - 2) % NT)
            def addup(m, t):
                dve.wait_ge(sem("s_down"), m + 1)
                tt(acc[:, t, :], acc[:, t, :], ps[:, 6 + t % 2, 0:D], ALU.add).then_inc(sem("s_acc"), 1)
            steps(0, 0, True, False)
            with dve.Fori(1, NW) as n:
                steps(n, 0, False, False)
            addup(NW * NT - 2, NT - 2)
            addup(NW * NT - 1, NT - 1)
            phase_end(dve, 5)
            dve.wait_ge(sem("s_g1"), 1)
            for h in range(2):
                v = slice(4 * h, 4 * h + 4)
                link(tt(x2[:, v, :], s1[:, v, :], acc[:, v, :], ALU.mult))
                tt(x2[:, v, :], x2[:, v, :], x_res[:, v, :], ALU.add).then_inc(sem("s_final"), 1)

        @block.gpsimd
        def _(pool):
            tt = nc.gpsimd.tensor_tensor
            nc.gpsimd.memset(half_neg[:, :], -0.5).then_inc(sem("s_half"), 1)
            pool.wait_ge(sem("s_half"), 1)

            def root(k, dst, src, w, signal):
                tt(dst, src, half_neg[:, 0:w], ALU.pow).then_inc(sem(signal), 1)
            pool.wait_ge(sem("s_var"), 1)
            root(1, rstd[:, :], ve[:, :], NT, "s_rstd")
            pool.wait_ge(sem("s_ms"), 1)
            root(1, small[:, 4:6, :].rearrange("p a t -> p (a t)"), small[:, 0:2, :].rearrange("p a t -> p (a t)"), 2 * NT, "s_rms")
            phase_end(pool, 0)

            def stage(n, k, free):
                if free:
                    pool.wait_ge(sem("s_qp"), n - 1)
                nc.gpsimd.tensor_copy(ws0[k][:, 0:KVL], w_abs0[:, ds(n, 1), :].rearrange("p h c -> p (h c)"))
                nc.gpsimd.tensor_copy(ws0[k][:, KVL:P], w_pe0[:, ds(n, 1), :].rearrange("p h c -> p (h c)"))
                nc.gpsimd.tensor_copy(ws1[k][:, 0:KVL], w_abs1[:, ds(n, 1), :].rearrange("p h c -> p (h c)"))
                nc.gpsimd.tensor_copy(ws1[k][:, KVL:P], w_pe1[:, ds(n, 1), :].rearrange("p h c -> p (h c)"))\
                    .then_inc(sem("s_stage"), 1)
                pool.wait_ge(sem("s_stage"), n + 1)

            def rope(n, k, free):
                pool.wait_ge(sem("s_rot"), 2 * n + 2)
                sn = rope_feat[64:P, 1, :].unsqueeze(1).broadcast_to([64, NB, S])
                tt(t2[64:P, :].rearrange("p (b s) -> p b s", b=NB), rot[64:P, :].rearrange("p (b s) -> p b s", b=NB), sn,
                   ALU.mult).then_inc(sem("s_t2"), 1)
                pool.wait_ge(sem("s_t2"), n + 1)
                pool.wait_ge(sem("s_t1"), n + 1)
                if free:
                    pool.wait_ge(mla.s_S, 4 * n - 4)
                tt(qh[k][64:P, :], t1[64:P, :], t2[64:P, :], ALU.add).then_inc(sem("s_qrope"), 1)
                pool.wait_ge(sem("s_qrope"), n + 1)

            stage(0, 0, False)
            rope(0, 0, False)

            def body(i, first, last):
                for j in range(2):
                    n = 2 * i + j
                    if not (last and j == 1):
                        stage(n + 1, (j + 1) % 2, not (first and j == 0))
                        rope(n + 1, (j + 1) % 2, not (first and j == 0))
            loop(pool, NP, body)
            phase_end(pool, 1)

            def bodyg(i, first, last):
                for j in range(4):
                    n = 4 * i + j
                    if not first:
                        pool.wait_ge(gat.s_S, 4 * n - 12)
                    r = slice(SLOT * j, SLOT * (j + 1))
                    nc.gpsimd.tensor_copy(QS[r, :], QT[r, ds(i, 1), :].rearrange("p g t -> p (g t)"))\
                        .then_inc(sem("s_slot"), 1)
                    pool.wait_ge(sem("s_slot"), n + 1)
            loop(pool, 4, bodyg)
            phase_end(pool, 2)
            pool.wait_ge(sem("s_var"), 2)
            root(2, rstd[:, :], ve[:, :], NT, "s_rstd")
            pool.wait_ge(sem("s_varh"), 1)
            root(0, small[:, 14, :], small[:, 13, :], NT, "s_rstdh")
            pool.wait_ge(sem("s_var"), 3)
            root(3, rstd[:, :], ve[:, :], NT, "s_rstd")
            for k in range(3, 6):
                phase_end(pool, k)

        @block.scalar
        def _(act):
            A = nc.scalar.activation

            def turned_rows(signal_in, signal_out):
                for t in range(NT):
                    act.wait_ge(sem(signal_in), t + 1)
                    A(xnT[:, :, t * P:(t + 1) * P], ps[:, t % 2, 0:2 * P].rearrange("p (k c) -> p k c", k=2), ACT.Copy)\
                        .then_inc(sem(signal_out), 1)
            turned_rows("s_xT0", "s_xnT0")
            for t in range(NT):
                act.wait_ge(sem("s_inp"), t + 1)
                A(praw[:, t, :], ps[:, 2 + t % 2, 0:W_IN], ACT.Copy).then_inc(sem("s_praw"), 1)
            act.wait_ge(sem("s_praw"), NT)
            for t in range(NT):
                A(xn[:, t, 0:QL], praw[:, t, 0:QL], ACT.Square, accum_out=small[:, 2, t:t + 1])
                A(xn[:, t, QL:QL + KVL], praw[:, t, QL:QL + KVL], ACT.Square, accum_out=small[:, 3, t:t + 1])\
                    .then_inc(sem("s_sumsq"), 1)
            act.wait_ge(sem("s_gsub"), 1)
            A(gsm[:, :, :], gsm[:, :, :], ACT.Exp).then_inc(sem("s_gexp"), 1)
            for k in range(2):
                act.wait_ge(sem("s_kTT"), k + 1)
                A(kT[:, 512 * k:512 * k + 512], ps[:, 4 + k, :], ACT.Copy)
            for k in range(2):
                act.wait_ge(sem("s_kshTT"), k + 1)
                A(kshT[:, 512 * k:512 * k + 512], ps[:, 6 + k, :], ACT.Copy)
            phase_end(act, 0)

            def head_rot(n, first):
                act.wait_ge(sem("s_qp"), n + 1)
                if not first:
                    act.wait_ge(sem("s_t2"), n)
                A(rot[64:96, :], Qp[96:P, :], ACT.Copy).then_inc(sem("s_rot"), 1)
                A(rot[96:P, :], Qp[64:96, :], ACT.Copy).then_inc(sem("s_rot"), 1)

            def head_abs(n, k, first):
                if not first:
                    act.wait_ge(mla.s_S, 4 * n - 4)
                A(qh[k][0:64, :], Qp[0:64, :], ACT.Copy, scale=-SCALE).then_inc(sem("s_qabs"), 1)

            def out_turned(i, h):
                act.wait_ge(sem("s_xT"), 2 * i + h + 1)
                A(xcT[:, ds(i, 1), h * 512:(h + 1) * 512].rearrange("p n t -> p (n t)"), ps[:, XB, :], ACT.Copy)\
                    .then_inc(sem("s_xcT"), 1)

            def body(i, first, last):
                for l in range(mla.U):
                    n, j = 2 * i + l // NB, l // NB
                    act_exp(act, mla, i, l, first)
                    if not (last and j == 1):
                        if l % NB == 0:
                            head_rot(n + 1, False)
                        if l % NB == 1:
                            head_abs(n + 1, (j + 1) % 2, first and j == 0)
                    if not first and l in (3, 5):
                        out_turned(i - 1, (l - 3) // 2)
                if last:
                    out_turned(i, 0)
                    out_turned(i, 1)
            head_rot(0, True)
            head_abs(0, 0, True)
            loop(act, NP, body)
            phase_end(act, 1)

            def bodyg(i, first, last):
                for l in range(gat.U):
                    act_exp(act, gat, i, l, first)
            loop(act, 4, bodyg)
            act.wait_ge(gat.s_xn, NH)
            A(y[:, :, :], y[:, :, :], ACT.Silu).then_inc(sem("s_g0"), 1)
            phase_end(act, 2)

            turned_rows("s_xT1", "s_xnT1")
            act.wait_ge(sem("s_small"), 16 * 14)
            for f in range(2):
                act.wait_ge(sem("s_khp"), f + 1)
                last = A(kk[:, f, :], ps[:, 2 * f:2 * f + 2, :].rearrange("p k c -> p (k c)"), ACT.Identity, bias=bz[:, 0, f:f + 1])
            last.then_inc(sem("s_kh_sb"), 1)
            for f in range(2):
                act.wait_ge(sem("s_khp"), 3 + f)
                A(hcat[:, f, :, 1:T1], ps[:, 4 + 2 * f:6 + 2 * f, :].rearrange("p k (b t) -> p (k b) t", t=S), ACT.Identity,
                  bias=bz[:, 1, f:f + 1])
                last = A(hcat[:, f, :, 0], bz[:, 2, f:f + 1].broadcast_to([P, NB]), ACT.Copy)
            last.then_inc(sem("s_kh_sb"), 1)
            act.wait_ge(sem("s_kh_sb"), 1)
            A(e1, kk, ACT.Abs).then_inc(sem("s_absk"), 1)
            act.wait_ge(sem("s_absk"), 1)
            A(e1, e1, ACT.Exp, scale=-1.0).then_inc(sem("s_act1"), 1)
            act.wait_ge(sem("s_act1"), 1)
            A(e1, e1, ACT.Ln, bias=1.0).then_inc(sem("s_l1"), 1)
            act.wait_ge(sem("s_mnh"), 1)
            A(e2, mnh, ACT.Exp).then_inc(sem("s_act1"), 1)
            act.wait_ge(sem("s_act1"), 2)
            A(e2, e2, ACT.Ln, bias=1.0)
            act.wait_ge(sem("s_num"), 1)
            A(l3, l3, ACT.Ln, bias=1.0).then_inc(sem("s_l3"), 1)
            act.wait_ge(sem("s_scan_in"), 1)
            A(dd, dd, ACT.Exp)
            A(l3, l3, ACT.Exp).then_inc(sem("s_scan_exp"), 1)
            act.wait_ge(sem("s_scan"), 1)
            A(ss, ss, ACT.Ln).then_inc(sem("s_scan_ln"), 1)
            act.wait_ge(sem("s_mean"), 1)
            A(dd, ss, ACT.Square, bias=small[:, 11, 0:1], accum_out=small[:, 12, 0:1]).then_inc(sem("s_sumsqh"), 1)
            act.wait_ge(sem("s_hscale"), 1)
            for f in range(2):
                last = A(hout[:, f, :].rearrange("p (b t) -> p b t", b=NB), ss[:, f, :, 1:T1], ACT.Exp, scale=small[:, 14, 0:1],
                         bias=small[:, 15, 0:1])
            last.then_inc(sem("s_hout"), 1)
            phase_end(act, 3)
            act.wait_ge(sem("s_top"), 1)
            A(small[:, 18, :], small[:, 16, :], ACT.Exp, scale=-1.0).then_inc(sem("s_gate_exp"), 1)
            phase_end(act, 4)

            def inner_turned(m, k):
                act.wait_ge(sem("s_hT"), m + 1)
                A(hT[k], ps[:, 4 + k, :], ACT.Copy).then_inc(sem("s_hT_sb"), 1)

            def steps(n, first):
                for t in range(NT):
                    m = n * NT + t
                    act.wait_ge(sem("s_gu"), m + 1)
                    if not (first and t < 2):
                        act.wait_ge(sem("s_h"), m - 1)
                    A(hg[t % 2], ps[:, t % 2, :], ACT.Silu, scale=gcol[:, t, ds(n, 1)]).then_inc(sem("s_silu"), 1)
                    if not (first and t < 1):
                        if not (first and t < 3):
                            act.wait_ge(sem("s_down"), m - 2)
                        inner_turned(m - 1, (t - 1) % 2)
            steps(0, True)
            with act.Fori(1, NW) as n:
                steps(n, False)
            inner_turned(NW * NT - 1, 1)
            phase_end(act, 5)
            A(acc, acc, ACT.Silu).then_inc(sem("s_g1"), 1)

        @block.tensor
        def _(pe):
            mm_ = nc.tensor.matmul
            tr = lambda o, i_, k=P: nc.tensor.transpose(o, i_, ident[0:k, 0:k])
            pe.wait_ge(sem("s_wnope"), 16)
            pe.wait_ge(sem("s_wkabs"), 16)
            for k in range(2):
                for h in range(8):
                    last = mm_(ps[:, k, h * 64:(h + 1) * 64], w_nope[:, 8 * k + h, 0:P], w_kabs[:, 8 * k + h, :], start=True, stop=True)
                last.then_inc(sem("s_wprep"), 1)
            for k in range(2):
                for h in range(8):
                    last = mm_(ps[0:QL2, 2 + k, h * 64:(h + 1) * 64], w_nope[:, 8 * k + h, P:QL], w_kabs[:, 8 * k + h, :],
                               start=True, stop=True)
                last.then_inc(sem("s_wprep"), 1)
            pe.wait_ge(sem("s_woabs"), 16)
            pe.wait_ge(sem("s_wo"), 16)
            for k in range(4):
                for q in range(2):
                    for j in range(2):
                        h = 4 * k + 2 * q + j
                        last = mm_(ps[64 * j:64 * j + 64, 4 + k, q * D:(q + 1) * D], w_oabs[:, h, :], w_o[:, h, :],
                                   start=True, stop=True)
                last.then_inc(sem("s_wprep"), 1)

            def rows_turned(src, s_in, s_out, s_copied, banks_free):
                pe.wait_ge(sem("s_ident"), 16)
                for t in range(NT):
                    pe.wait_ge(sem(s_in), t + 1)
                    if t < 2:
                        banks_free(t)
                    else:
                        pe.wait_ge(sem(s_copied), t - 1)
                    tr(ps[:, t % 2, 0:P], src[:, t, 0:P])
                    tr(ps[:, t % 2, P:2 * P], src[:, t, P:2 * P]).then_inc(sem(s_out), 1)
            rows_turned(xn, "s_xn0", "s_xT0", "s_xnT0", lambda t: pe.wait_ge(sem("s_wprep_sb"), 8))

            pe.wait_ge(sem("s_win"), 16)
            pe.wait_ge(sem("s_wkv"), 16)
            pe.wait_ge(sem("s_wq"), 16)
            for t in range(NT):
                pe.wait_ge(sem("s_xnT0"), t + 1)
                if t >= 2:
                    pe.wait_ge(sem("s_praw"), t - 1)
                    pe.wait_ge(sem("s_kvraw"), t - 1)
                for k in range(DK):
                    last = mm_(ps[:, 2 + t % 2, 0:W_IN], xnT[:, k, t * P:(t + 1) * P], w_in[:, k, :], start=(k == 0), stop=(k == 1))
                last.then_inc(sem("s_inp"), 1)
                for k in range(DK):
                    last = mm_(ps[:, 4 + t % 2, :], xnT[:, k, t * P:(t + 1) * P], w_kv[:, k, :], start=(k == 0), stop=(k == 1))
                last.then_inc(sem("s_kvp"), 1)
            for g in range(4):
                if g < 2:
                    pe.wait_ge(sem("s_praw"), NT)
                else:
                    pe.wait_ge(sem("s_QT"), g - 1)
                for h in range(2):
                    for k in range(DK):
                        last = mm_(ps[:, 2 * (g % 2) + h, :], w_q[:, k, g * P:(g + 1) * P], xnT[:, k, h * 512:(h + 1) * 512],
                                   start=(k == 0), stop=(k == 1))
                last.then_inc(sem("s_QTp"), 1)
            pe.wait_ge(sem("s_QT"), 4)
            pe.wait_ge(sem("s_kvraw"), NT)
            pe.wait_ge(sem("s_qs"), 1)
            for k in range(2):
                for t in range(4):
                    last = tr(ps[:, k, t * P:(t + 1) * P], qs[:, 4 * k + t, 0:P])
                last.then_inc(sem("s_latT"), 1)
                for t in range(4):
                    last = tr(ps[0:QL2, 2 + k, t * P:(t + 1) * P], qs[:, 4 * k + t, P:QL])
                last.then_inc(sem("s_latT"), 1)
            pe.wait_ge(sem("s_kc"), 1)
            for k in range(2):
                for t in range(4):
                    last = tr(ps[:, 4 + k, t * P:(t + 1) * P], kc[:, 4 * k + t, :])
                last.then_inc(sem("s_kTT"), 1)
            pe.wait_ge(sem("s_krep"), 1)
            for k in range(2):
                for t in range(4):
                    last = tr(ps[:, 6 + k, t * P:(t + 1) * P], krep[:, 4 * k + t].rearrange("p r s -> p (r s)"))
                last.then_inc(sem("s_kshTT"), 1)
            phase_end(pe, 0)

            def queries(n, k, first):
                pe.wait_ge(sem("s_stage"), n + 1)
                if not first:
                    pe.wait_ge(sem("s_qabs"), n)
                    pe.wait_ge(sem("s_rot"), 2 * n)
                    pe.wait_ge(sem("s_t1"), n)
                for h in range(2):
                    mm_(ps[:, QB[h], :], ws0[k], qaT0[:, h * 512:(h + 1) * 512], start=True, stop=False)
                    last = mm_(ps[:, QB[h], :], ws1[k], qaT1[:, h * 512:(h + 1) * 512], start=False, stop=True)
                last.then_inc(sem("s_qp"), 1)

            def out_turned(i, h, first):
                if h == 0:
                    pe.wait_ge(mla.s_xn, 2 * i + 2)
                if not (first and h == 0):
                    pe.wait_ge(sem("s_xcT"), 2 * i + h)
                for t in range(4):
                    last = tr(ps[:, XB, t * P:(t + 1) * P], xcn[:, 4 * h + t, :])
                last.then_inc(sem("s_xT"), 1)

            def body(i, first, last, second=False):
                for l in range(mla.U):
                    j, b, u = l // NB, l % NB, i * mla.U + l
                    n = 2 * i + j
                    if b == 0:
                        if not (last and j == 1):
                            queries(n + 1, (j + 1) % 2, False)
                        pe.wait_ge(sem("s_qrope"), n + 1)
                        pe.wait_ge(sem("s_qabs"), n + 1)
                    pe_scores(pe, mla, i, l, first)
                    if not (first and l < 1):
                        pe_turn(pe, mla, u - 1, l - 1, first and l < 3)
                    if not (first and l < 2):
                        pe_heads(pe, mla, u - 2, l - 2, i * 2 + (l - 2) // NB, (b - 2) % NB, first and l < 6)
                    if not first and l in (2, 4):
                        out_turned(i - 1, (l - 2) // 2, False)
                if last:
                    u = i * mla.U + mla.U
                    pe_turn(pe, mla, u - 1, 1, False)
                    pe_heads(pe, mla, u - 2, 0, 2 * i + 1, 2, False)
                    pe_heads(pe, mla, u - 1, 1, 2 * i + 1, 3, False)
                    out_turned(i, 0, False)
                    out_turned(i, 1, False)
            queries(0, 0, True)
            loop(pe, NP, body)
            phase_end(pe, 1)

            def bodyg(i, first, last):
                for l in range(gat.U):
                    j, b, u = l // NB, l % NB, i * gat.U + l
                    if b == 0:
                        pe.wait_ge(sem("s_slot"), 4 * i + j + 1)
                    pe_scores(pe, gat, i, l, first)
                    if not (first and l < 1):
                        pe_turn(pe, gat, u - 1, l - 1, first and l < 3)
                    if not (first and l < 2):
                        pe_heads(pe, gat, u - 2, l - 2, i * 4 + (l - 2) // NB, (b - 2) % NB, first and l < 6)
                if last:
                    u = i * gat.U + gat.U
                    pe_turn(pe, gat, u - 1, 1, False)
                    pe_heads(pe, gat, u - 2, 0, 4 * i + 3, 2, False)
                    pe_heads(pe, gat, u - 1, 1, 4 * i + 3, 3, False)
            loop(pe, 4, bodyg)
            for k in range(4):
                if k >= 2:
                    pe.wait_ge(sem("s_spr"), k - 1)
                for q in range(2):
                    t = 2 * k + q
                    for n in range(NP):
                        last = mm_(ps[:, 5 + k % 2, q * D:(q + 1) * D], xcT[:, n, t * P:(t + 1) * P], wo_abs[:, n, :],
                                   start=(n == 0), stop=(n == NP - 1))
                last.then_inc(sem("s_sp"), 1)
            phase_end(pe, 2)

            rows_turned(xn, "s_xn1", "s_xT1", "s_xnT1", lambda t: None)
            pe.wait_ge(sem("s_xnT1"), NT)
            pe.wait_ge(sem("s_wz"), 32)
            for w, wt in enumerate((wz, wh)):
                for f in range(2):
                    for h in range(2):
                        for k in range(DK):
                            last = mm_(ps[:, 4 * w + 2 * f + h, :], wt[:, k, f * P:(f + 1) * P], xnT[:, k, h * 512:(h + 1) * 512],
                                       start=(k == 0), stop=(k == 1))
                    last.then_inc(sem("s_khp"), 1)
            pe.wait_ge(sem("s_softplus"), 1)
            pe.wait_ge(sem("s_ones"), 1)
            pe.wait_ge(sem("s_small"), 16 * 14)
            for f in range(2):
                for h in range(2):
                    v = slice(h * 512, (h + 1) * 512)
                    if f == 0:
                        last = mm_(ps[:, h, :], upper[:, :], sp[:, 0, v], start=True, stop=True)
                    else:
                        mm_(ps[:, 2 + h, :], ones[:, :], sp[:, 0, v], start=True, stop=False)
                        last = mm_(ps[:, 2 + h, :], upper[:, :], sp[:, 1, v], start=False, stop=True)
                last.then_inc(sem("s_acum"), 1)
            pe.wait_ge(sem("s_sum"), 1)
            mm_(ps[:, 4, 0:1], ones[:, :], small[:, 10, 0:1], start=True, stop=True).then_inc(sem("s_tot"), 1)
            pe.wait_ge(sem("s_sumsqh"), 1)
            mm_(ps[:, 4, 1:2], ones[:, :], small[:, 12, 0:1], start=True, stop=True).then_inc(sem("s_tot"), 1)
            pe.wait_ge(sem("s_hout"), 1)
            for k in range(4):
                for q in range(2):
                    for f in range(2):
                        t = 2 * k + q
                        last = tr(ps[:, k, q * D + f * P:q * D + (f + 1) * P], hout[:, f, t * P:(t + 1) * P])
                last.then_inc(sem("s_hback"), 1)
            phase_end(pe, 3)
            for t in range(NT):
                for k in range(DK):
                    last = mm_(ps[:, 0, t * E:(t + 1) * E], xnT[:, k, t * P:(t + 1) * P], wr[:, k, :], start=(k == 0), stop=(k == 1))
            last.then_inc(sem("s_router"), 1)
            phase_end(pe, 4)

            def inner(m, t, first):
                pe.wait_ge(sem("s_h"), m + 1)
                if not (first and t < 2):
                    pe.wait_ge(sem("s_hT_sb"), m - 1)
                for k in range(4):
                    last = tr(ps[:, 4 + t % 2, k * P:(k + 1) * P], hh[t % 2][:, k * P:(k + 1) * P])
                last.then_inc(sem("s_hT"), 1)

            def down(m, t, w, first):
                pe.wait_ge(sem("s_hT_sb"), m + 1)
                if not (first and t < 2):
                    pe.wait_ge(sem("s_acc"), m - 1)
                for k in range(4):
                    last = mm_(ps[:, 6 + t % 2, 0:D], hT[t % 2][:, k * P:(k + 1) * P], w[:, k, :], start=(k == 0), stop=(k == 3))
                last.then_inc(sem("s_down"), 1)

            def expert(n, e, s_seen, first, wl):
                pe.wait_ge(sem(f"s_wexp{e}"), s_seen)
                for t in range(NT):
                    m = n * NT + t
                    if not (first and t < 2):
                        pe.wait_ge(sem("s_silu"), m - 1)
                        pe.wait_ge(sem("s_h"), m - 1)
                    for w in range(2):
                        for k in range(DK):
                            last = mm_(ps[:, 2 * w + t % 2, :], xnT[:, k, t * P:(t + 1) * P], wgu[e][:, k, w * FF:(w + 1) * FF],
                                       start=(k == 0), stop=(k == 1))
                    last.then_inc(sem("s_gu"), 1)
                    if not (first and t < 1):
                        inner(m - 1, (t - 1) % NT, first and t < 3)
                    if not (first and t < 2):
                        down(m - 2, (t - 2) % NT, wd[e] if t >= 2 else wl, first and t < 4)
            expert(0, 0, 32, True, None)
            expert(1, 1, 32, False, wd[0])
            with pe.Fori(1, E // 2) as i:
                expert(2 * i, 0, 32 * i + 32, False, wd[1])
                expert(2 * i + 1, 1, 32 * i + 32, False, wd[0])
            expert(E, 0, 32 * (E // 2) + 32, False, wd[1])
            m = NW * NT
            inner(m - 1, NT - 1, False)
            down(m - 2, NT - 2, wd[0], False)
            down(m - 1, NT - 1, wd[0], False)
            phase_end(pe, 5)


def layouts(i):
    import numpy as np
    c = lambda v: np.ascontiguousarray(v)
    arr = {k: np.asarray(v) for k, v in i.items()}
    turned = np.concatenate([np.arange(0, ROPE, 2), np.arange(1, ROPE, 2)])
    wkv_a = arr["L0_attn_wkv_a"]
    wq_b = arr["L0_attn_wq_b"].reshape(NH, NOPE + ROPE, QL)
    wkv_b = arr["L0_attn_wkv_b"].reshape(NH, NOPE + VH, KVL)
    wqkv = arr["L0_ffn_W_qkv"]
    w_q = np.zeros((D, NH, SLOT), wqkv.dtype)
    w_q[:, :, 0:HD] = wqkv[0:D].reshape(NH, HD, D).transpose(2, 0, 1)
    d = {
        "x": arr["L0_attn_hidden_states"].reshape(TOK, D),
        "w_in": np.concatenate([arr["L0_attn_wq_a"], wkv_a[0:KVL], wkv_a[KVL:][turned], arr["L0_ffn_W_gate"]], axis=0).T,
        "w_kv": wqkv[D:].T,
        "w_q": w_q.reshape(D, NH * SLOT),
        "w_nope": wq_b[:, 0:NOPE],
        "w_pe": wq_b[:, NOPE:][:, turned].transpose(2, 0, 1).reshape(QL, NH * ROPE),
        "w_kabs": wkv_b[:, 0:NOPE],
        "w_oabs": wkv_b[:, VH:],
        "w_o": arr["L0_attn_wo"].T,
        "q_ln": arr["L0_attn_q_a_ln_w"], "kv_ln": arr["L0_attn_kv_a_ln_w"],
        "w_z": arr["L1_attn_W_z"].T, "w_h": arr["L1_attn_W_h"].T,
        "rows_l1": np.stack([arr[f"L1_attn_{n}"].reshape(DK, P) for n in ("b_z", "b_h", "h0")]).transpose(2, 0, 1),
        "ln_w": arr["L1_attn_ln_w"], "ln_b": arr["L1_attn_ln_b"],
        "w_router": arr["L1_ffn_router_w"].T,
        "w_gu": arr["L1_ffn_w_gate_up"], "w_dn": arr["L1_ffn_w_down"],
        "w_shared_gu": arr["L1_ffn_shared_gate_up"], "w_shared_dn": arr["L1_ffn_shared_down"],
    }
    return {k: c(v) for k, v in d.items()}


def kernel(**inputs):
    import concourse.bacc as _bacc
    from concourse import mybir as _mybir
    from concourse.bass_utils import run_bass_kernel_spmd as _run

    arrays = {**layouts(inputs), **constants()}
    nc = _bacc.Bacc("TRN2", target_bir_lowering=False, num_devices=1)
    a = {k: nc.dram_tensor(f"in_{k}", v.shape, _mybir.dt.from_np(v.dtype), kind="ExternalInput").ap() for k, v in arrays.items()}
    out = nc.dram_tensor("out", (TOK, D), _mybir.dt.float32, kind="ExternalOutput").ap()
    recurrent_kernel(nc, a, out)
    r = _run(nc, [{f"in_{k}": v for k, v in arrays.items()}], core_ids=[0])
    return r.results[0]["out"].reshape(NB, S, D)
```

```python
import concourse.bass as bass
from concourse import mybir
from contextlib import ExitStack

P = 128
NB, S, D = 4, 256, 256
TOK = NB * S
NT = TOK // P
DK = D // P
NH = 16
QL, KVL, NOPE, ROPE, VH = 192, 64, 128, 64, 128
QL2 = QL - P
SCALE = float(NOPE + ROPE) ** -0.5
HD = D // NH
SLOT = 32
FSCALE = float(HD) ** -0.5
W_IN = QL + KVL + ROPE + NH
FF, E = 512, 8
NBLK = NT + E - 1
FX = DK * 2 * FF + (FF // P) * D
T1 = S + 1
BIG = 3.0e38
SMALL = 16 * 13
WIDE = 3 * P


def constants():
    import numpy as np
    i = np.arange(P)
    ident = np.eye(P, dtype=np.float32)
    upper = (i[:, None] <= i[None, :]).astype(np.float32)
    diag = np.where(i[None, :] > i[:, None], np.float32(BIG), np.float32(0))
    mask = np.concatenate([diag, np.zeros((P, P), np.float32), diag], axis=1)
    inv = (np.float32(1.0) / np.float32(10000.0) ** (np.arange(0, ROPE, 2, dtype=np.float32) / np.float32(ROPE))).astype(np.float32)
    f = np.arange(S, dtype=np.float32)[:, None] * inv[None, :]
    cos, sin = np.cos(f.astype(np.float64)), np.sin(f.astype(np.float64))
    tok = np.concatenate([cos.reshape(2, P, 32), sin.reshape(2, P, 32)], axis=0).transpose(1, 0, 2)
    feat = np.zeros((P, 2, S))
    feat[:, 0] = np.concatenate([cos.T] * 4, axis=0) * -SCALE
    feat[:, 1] = np.concatenate([-sin.T, sin.T] * 2, axis=0) * -SCALE
    return {
        "c_ident": ident, "c_upper": upper, "c_after": upper - 1, "c_mask": mask,
        "c_rope_tok": np.ascontiguousarray(tok, dtype=np.float32).reshape(P, 4 * 32),
        "c_rope_feat": feat.astype(np.float32).reshape(P, 2 * S),
        "c_iota": np.broadcast_to(np.arange(NH, dtype=np.float32), (P, NH)).copy(),
    }


def recurrent_kernel(nc, a, out, debug=None):
    f32 = mybir.dt.float32
    ALU = mybir.AluOpType
    ACT = mybir.ActivationFunctionType
    X = mybir.AxisListType.X
    ds = bass.ds

    ctx = ExitStack()
    with ctx:
        def sb(name, shape):
            return ctx.enter_context(nc.sbuf_tensor(name, shape, f32))

        sems = {}

        def sem(name):
            if name not in sems:
                sems[name] = ctx.enter_context(nc.semaphore(name))
            return sems[name]

        ident = sb("ident", [P, P])
        upper = sb("upper", [P, P])
        after = sb("after", [P, P])
        ones = sb("ones", [P, P])
        tables = sb("tables", [P, 512])
        mask = tables[:, 0:WIDE]
        rope_tok = tables[:, WIDE:512].rearrange("p (k c) -> p k c", k=4)
        ln1 = tables[:, :].rearrange("p (k c) -> p k c", k=2)
        rope_feat = sb("rope_feat", [P, 2, S])
        iota = sb("iota", [P, NH])
        x_res = sb("x_res", [P, NT, D])
        xn = sb("xn", [P, NT, D])
        xnT = sb("xnT", [P, DK, TOK])
        y = sb("y", [P, NT, D])
        st = sb("st", [P, NT, 6])
        mv = sb("mv", [P, NT, 2])
        half_neg = sb("half_neg", [P, 2 * NT])
        ve = sb("ve", [P, NT])
        rstd = sb("rstd", [P, NT])
        mx = sb("mx", [P, 2, 8])
        stand = sb("stand", [P, 16])
        rs = sb("rs", [P, 2, 8])
        ri = sb("ri", [P, 2, 8])
        routing = sb("routing", [P, 2 * NT * E])
        EXP = sb("EXP", [P, E * FX])
        R2 = sb("R2", [P, 5 * DK * NB * T1])
        SH = sb("SH", [P, FX])
        MB = sb("MB", [P, 4608 + 256])
        RA, RB, RC = EXP[:, 0:8192], EXP[:, 8192:17408], EXP[:, 17408:21504]
        qaT0 = EXP[:, 21504:22528]
        qaT1 = EXP[0:QL2, 22528:23552]
        kT = EXP[:, 23552:24576]
        RD = R2[:, 0:8192]
        kc = R2[:, 7680:9216].rearrange("p (t c) -> p t c", t=NT)
        kshT = R2[:, 9216:10240]
        wo_abs = SH[:, 0:2048].rearrange("p (n c) -> p n c", n=NH // 2)
        w_q = SH[:, 2048:3072].rearrange("p (k c) -> p k c", k=DK)
        kTB = SH[:, 2048:3072]
        scr = [MB[:, k * WIDE:(k + 1) * WIDE] for k in range(2)]
        prob = [MB[:, (2 + k) * WIDE:(3 + k) * WIDE] for k in range(2)]
        probT = [MB[:, (4 + k) * WIDE:(5 + k) * WIDE] for k in range(2)]
        w_in = MB[:, 2304:2304 + DK * W_IN].rearrange("p (k c) -> p k c", k=DK)
        w_kv = MB[:, 3072:4096].rearrange("p (k c) -> p k c", k=DK)

        ps = ctx.enter_context(nc.psum_tensor("ps", [P, 8, 512], f32))

        kvraw = RA[:, 0:4096].rearrange("p (t c) -> p t c", t=NT)
        gtmp = RA[:, 4096:6144].rearrange("p (t d h) -> p t d h", t=NT, d=HD)
        qs = RA[:, 6144:6144 + NT * QL].rearrange("p (t c) -> p t c", t=NT)
        xcT = RA[:, :].rearrange("p (n t) -> p n t", n=NH // 2)
        w_nope = RB[:, 0:NH * QL].rearrange("p (h c) -> p h c", h=NH)
        w_kabs = RB[:, 3072:4096].rearrange("p (h c) -> p h c", h=NH)
        w_oabs = RB[:, 4096:5120].rearrange("p (h c) -> p h c", h=NH)
        w_o = RB[:, 5120:9216].rearrange("p (h c) -> p h c", h=NH)
        QT = RC[:, :].rearrange("p (g t) -> p g t", g=4)
        yflat = y[:, :, :].rearrange("p t c -> p (t c)")
        wcat0 = yflat.rearrange("p (n c) -> p n c", n=NH // 2)
        wcat1 = RD[0:QL2, 5632:7680].rearrange("p (n c) -> p n c", n=NH // 2)
        lnq = sb("lnq", [P, 2])
        lnkv = MB[:, 4736:4800]
        praw = RD[:, 0:NT * W_IN].rearrange("p (t c) -> p t c", t=NT)
        qh = [RD[:, k * 1024:(k + 1) * 1024] for k in range(2)]
        raw = RD[:, 2048:3072]
        rot = RD[:, 3072:4096]
        xcn = RD[:, 4096:5120].rearrange("p (t c) -> p t c", t=NT)
        ws0 = RD[:, 5120:5376]
        ws1 = RD[0:QL2, 5376:5632]
        QS = RD[:, 0:1024]
        kz = RB[:, 0:4096].rearrange("p (j t) -> p j t", j=4)
        probT8 = [RB[:, 4096 + k * WIDE:4096 + (k + 1) * WIDE] for k in range(8)]
        ysum = RB[:, 7168:8192]
        vsh = RB[:, 8192:8448].rearrange("p (t c) -> p t c", t=NT)
        small = sb("small", [P, 32, NT])
        oneh = MB[:, 4608:4736].rearrange("p (t h) -> p t h", h=NH)
        gsm = RD[:, 3200:3328].rearrange("p (t h) -> p t h", t=NT)
        kred = RD[:, 2944:3200].rearrange("p (w t d) -> p w t d", w=2, t=NT)
        krep = RD[:, 4096:5120].rearrange("p (t r s) -> p t r s", t=NT, r=4)

        bar = {}
        marks = []

        def dump(eng, name, ap):
            if debug is not None and name in debug:
                eng.dma_start(debug[name], ap).then_inc(sem("s_dbg"), 16)
                marks.append(name)
                eng.wait_ge(sem("s_dbg"), 16 * len(marks))

        def phase_end(eng, k):
            eng.drain().then_inc(sem(f"s_phase{k}"), 1)
            eng.wait_ge(sem(f"s_phase{k}"), 5)

        def chain(eng, name):
            n = [0]

            def link(ins):
                n[0] += 1
                ins.then_inc(sem(name), 1)
                eng.wait_ge(sem(name), n[0])
                return ins
            return link

        SB = [0, 1]
        TB = [2, 3]
        AB = 4

        class Core:
            def __init__(self, tag, heads, place, q_of, k_of, least, turned):
                self.tag, self.heads, self.place = tag, heads, place
                self.q_of, self.k_of, self.least, self.turned = q_of, k_of, least, turned
                self.U = heads * NB
                s = lambda x: sem(f"{x}_{tag}")
                self.s_S, self.s_mx, self.s_P, self.s_T = s("s_scores"), s("s_max"), s("s_probs"), s("s_turned")
                self.s_pt, self.s_av = s("s_turned_sb"), s("s_heads")

        def pe_scores(pe, c, i, l, first):
            (j, b), u = c.place(l), i * c.U + l
            if not (first and l < 2):
                pe.wait_ge(c.s_mx, u - 1)
            bank = ps[:, SB[l % 2], :]
            nc.tensor.matmul(bank[:, 0:P], c.q_of(j, 2 * b), c.k_of(j, b, P), start=True, stop=True)
            nc.tensor.matmul(bank[:, P:WIDE], c.q_of(j, 2 * b + 1), c.k_of(j, b, S), start=True, stop=True)\
                .then_inc(c.s_S, 1)

        def pe_turn(pe, c, u, l, early):
            pe.wait_ge(c.s_P, u + 1)
            if not early:
                pe.wait_ge(c.s_pt, u - 1)
            for k in range(3):
                last = nc.tensor.transpose(ps[:, TB[l % 2], k * P:(k + 1) * P], prob[l % 2][:, k * P:(k + 1) * P],
                                           ident[:, :])
            last.then_inc(c.s_T, 1)

        av = ps[:, AB, :].rearrange("p (t c) -> p t c", t=NT)

        def pe_heads(pe, c, u, l, n, b, early):
            pe.wait_ge(c.s_pt, u + 1)
            if b == 0 and not early:
                pe.wait_ge(sem("s_normed"), n)
            pt, v = c.turned(l), lambda t: kc[:, t, 0:KVL]
            nc.tensor.matmul(av[:, 2 * b, :], pt[:, 0:P], v(2 * b), start=True, stop=True)
            nc.tensor.matmul(av[:, 2 * b + 1, :], pt[:, P:2 * P], v(2 * b), start=True, stop=False)
            nc.tensor.matmul(av[:, 2 * b + 1, :], pt[:, 2 * P:WIDE], v(2 * b + 1), start=False, stop=True)\
                .then_inc(c.s_av, 1)

        def dve_max(dve, c, i, l, first):
            u = i * c.U + l
            dve.wait_ge(c.s_S, u + 1)
            if not (first and l < 2):
                dve.wait_ge(c.s_P, u - 1)
            if not isinstance(i, int):
                nc.vector.memset(stand[:, l:l + 1], 0.0)
            for q, (lo, hi) in enumerate(((0, P), (P, WIDE))):
                last = nc.vector.tensor_tensor_reduce(
                    out=scr[l % 2][:, lo:hi], in0=ps[:, SB[l % 2], lo:hi], in1=mask[:, lo:hi], scale=1.0, scalar=BIG,
                    op0=ALU.add, op1=ALU.min, accum_out=c.least(l, q))
            last.then_inc(c.s_mx, 1)

        def dve_turned(dve, c, u, l, used):
            dve.wait_ge(c.s_T, u + 1)
            if used is not None:
                dve.wait_ge(c.s_av, used)
            nc.vector.tensor_copy(c.turned(l), ps[:, TB[l % 2], 0:WIDE]).then_inc(c.s_pt, 1)

        def dve_norm(dve, c, n, j, dst):
            dve.wait_ge(c.s_P, 4 * n + 4)
            nc.vector.reciprocal(ri[:, j % 2, :], rs[:, j % 2, :]).then_inc(sem("s_recip"), 1)
            dve.wait_ge(c.s_av, 4 * n + 4)
            dve.wait_ge(sem("s_recip"), n + 1)
            nc.vector.tensor_tensor(dst, av, ri[:, j % 2, :].unsqueeze(2).broadcast_to([P, NT, KVL]), ALU.mult)\
                .then_inc(sem("s_normed"), 1)

        def act_exp(act, c, i, l, first, sums=None):
            u = i * c.U + l
            act.wait_ge(c.s_mx, u + 1)
            if not (first and l < 2):
                act.wait_ge(c.s_T, u - 1)
            for q, (lo, hi) in enumerate(((0, P), (P, WIDE))):
                last = nc.scalar.activation(prob[l % 2][:, lo:hi], scr[l % 2][:, lo:hi], ACT.Exp, bias=c.least(l, q), scale=-1.0,
                                            accum_out=None if sums is None else sums(l, q))
            last.then_inc(c.s_P, 1)

        by_head = lambda v: lambda l, q: v[:, l // NB % 2, 2 * (l % NB) + q:2 * (l % NB) + q + 1]
        by_step = lambda v: lambda l, q: v[:, l % 8 // 4, 2 * (l % 4) + q:2 * (l % 4) + q + 1]
        mla = Core("mla", 2, lambda l: (l // NB, l % NB), lambda j, t: qh[j][:, t * P:(t + 1) * P],
                   lambda j, b, w: (kT, kTB)[j][:, b * S:b * S + w], by_head(mx), lambda l: probT[l % 2])
        gat = Core("gat", 4, lambda l: (l % 4, l // 4), lambda j, t: QS[:, t * P:(t + 1) * P],
                   lambda j, b, w: kz[:, j, b * S:b * S + w], by_step(mx), lambda l: probT8[l % 8])

        def loop(eng, iters, body):
            body(0, True, False)
            with eng.Fori(1, iters - 1) as i:
                body(i, False, False)
            body(iters - 1, False, True)

        QB = (5, 6)
        XB = 7
        NP = NH // 2
        Qp = ps[:, 5:7, :].rearrange("p k c -> p (k c)")

        HW = DK * NB * T1
        seq = [R2[:, k * HW:(k + 1) * HW] for k in range(5)]
        steps4 = lambda v: v.rearrange("p (f b t) -> p f b t", f=DK, b=NB)
        plain = lambda v: v[:, 0:DK * TOK].rearrange("p (f t) -> p f t", f=DK)
        hseq = seq[0]
        kpos = seq[1]
        kraw = seq[2]
        e1 = seq[3]
        hmin = seq[4]
        hout = seq[0][:, 0:DK * TOK]
        x2 = seq[1][:, 0:NT * D].rearrange("p (t c) -> p t c", t=NT)
        s1 = seq[3][:, 0:NT * D].rearrange("p (t c) -> p t c", t=NT)
        routed = seq[2][:, 0:NT * D].rearrange("p (t c) -> p t c", t=NT)
        wz = w_kv[:, :, 0:D]
        wh = w_kv[:, :, D:2 * D]
        bz = sb("bz", [P, 3, 2])
        wr = sb("wr", [P, DK, E])
        act_sb = [MB[:, k * FF:(k + 1) * FF] for k in range(2)]
        inn_sb = [MB[:, 1024 + k * FF:1024 + (k + 1) * FF] for k in range(2)]
        innT_sb = [MB[:, 2048 + k * FF:2048 + (k + 1) * FF] for k in range(2)]
        xb = [MB[:, 3072 + k * D:3072 + (k + 1) * D] for k in range(2)]
        OB = 4
        ob = [MB[:, 3584 + k * D:3584 + (k + 1) * D] for k in range(OB)]
        blocks_of_buffer = lambda k: (NBLK - k + OB - 1) // OB
        xg = [MB[:, 4096 + k * D:4096 + (k + 1) * D] for k in range(2)]
        xbT = [rope_feat[:, k, :] for k in range(2)]
        roneh = routing[:, 0:NT * E].rearrange("p (t e) -> p t e", e=E)
        upto = routing[:, NT * E:].rearrange("p (t e) -> p t e", e=E)
        rl = MB[:, 4608:4608 + NT * E].rearrange("p (t e) -> p t e", e=E)
        rtmp = MB[:, 4672:4672 + 16 * E].rearrange("p (t e) -> p t e", e=E)
        pos_i = ctx.enter_context(nc.sbuf_tensor("pos_i", [P, NT], mybir.dt.int32))
        eid_i = ctx.enter_context(nc.sbuf_tensor("eid_i", [P, 16], mybir.dt.int32))
        sorted_rows = nc.dram_tensor("sorted_rows", (NBLK * P, D), f32, kind="Internal").ap()
        sorted_out = nc.dram_tensor("sorted_out", (NBLK * P, D), f32, kind="Internal").ap()
        zeros = RD[:, 2688:2688 + D]
        A0 = 5
        M = NT + NBLK
        is_block = lambda m: A0 <= m < A0 + NBLK
        tile_of = lambda m: m if m < A0 else m - NBLK
        BG, BU, BT, BD, B7 = (0, 1), (2, 3), (4, 5), 6, 7

        block = ctx.enter_context(nc.Block())

        @block.sync
        def _(sp_):
            eng = sp_
            x_v = a["x"].rearrange("(t p) d -> p t d", p=P)
            load = lambda s, dst, src: eng.dma_start(dst, src).then_inc(sem(s), 16)
            for h in range(2):
                load(f"s_x{h}", x_res[:, 4 * h:4 * h + 4, :], x_v[:, 4 * h:4 * h + 4, :])
            load("s_ident", ident[:, :], a["c_ident"])
            kview = lambda w: w.rearrange("(k p) c -> p k c", p=P)
            load("s_win", w_in[:, :, :], kview(a["w_in"]))
            load("s_win", w_kv[:, :, :], kview(a["w_kv"]))
            load("s_win", w_q[:, :, :], kview(a["w_q"]))
            load("s_wnope", w_nope, a["w_nope"].rearrange("h p c -> p h c"))
            load("s_wnope", w_kabs, a["w_kabs"].rearrange("h p c -> p h c"))
            load("s_wo", w_oabs, a["w_oabs"].rearrange("h p c -> p h c"))
            load("s_wo", w_o, a["w_o"].rearrange("(h p) c -> p h c", p=P))
            load("s_small", wcat0[:, :, P:2 * P], a["w_pe"][0:P].rearrange("p (n c) -> p n c", n=NP))
            load("s_small", wcat1[:, :, P:2 * P], a["w_pe"][P:QL].rearrange("p (n c) -> p n c", n=NP))
            load("s_small", lnq[:, 0:1], a["q_ln"][0:P].unsqueeze(1))
            load("s_small", lnq[0:QL2, 1:2], a["q_ln"][P:QL].unsqueeze(1))
            load("s_small", lnkv[:, :], a["kv_ln"].unsqueeze(0).broadcast_to([P, KVL]))
            load("s_small", mask, a["c_mask"])
            load("s_small", upper[:, :], a["c_upper"])
            load("s_small", rope_tok, a["c_rope_tok"].rearrange("p (k c) -> p k c", k=4))
            load("s_small", after[:, :], a["c_after"])
            load("s_small", rope_feat[:, :, :], a["c_rope_feat"].rearrange("p (k c) -> p k c", k=2))
            load("s_small", iota[:, :], a["c_iota"])
            load("s_small", bz[:, :, :], a["rows_l1"])
            load("s_small", wr[:, :, :], kview(a["w_router"]))
            eng.wait_ge(sem("s_zeros"), 1)
            eng.dma_start(sorted_rows.rearrange("(k p) c -> p k c", p=P), zeros.unsqueeze(1).broadcast_to([P, NBLK, D]))\
               .then_inc(sem("s_cleared"), 16)
            eng.wait_ge(sem("s_cleared"), 16)
            phase_end(eng, 0)
            load("s_wz", wz, kview(a["w_z"]))
            load("s_wz", wh, kview(a["w_h"]))

            def swap(n, first):
                eng.wait_ge(sem("s_raw"), 2 * n + 2)
                if not first:
                    eng.wait_ge(sem("s_qB"), n)
                for k in range(4):
                    eng.dma_start(rot[32 * k:32 * k + 32, :], raw[32 * (k ^ 1):32 * (k ^ 1) + 32, :]).then_inc(sem("s_swapped"), 16)
            swap(0, True)
            with eng.Fori(1, NP) as i:
                swap(i, False)
            for k in range(1, 3):
                phase_end(eng, k)
            def weights(dst, gu, dn, signal):
                load(signal, dst[:, 0:2048].rearrange("p (k c) -> p k c", k=DK), gu.rearrange("(k p) c -> p k c", p=P))
                load(signal, dst[:, 2048:FX].rearrange("p (k c) -> p k c", k=4), dn.rearrange("(k p) c -> p k c", p=P))
            weights(SH, a["w_shared_gu"], a["w_shared_dn"], "s_wsh")
            for k, name in enumerate(("ln_w", "ln_b")):
                load("s_ln1", ln1[:, k, :], a[name].unsqueeze(0).broadcast_to([P, D]))
            for e in range(E):
                weights(EXP[:, e * FX:(e + 1) * FX], a["w_gu"][e], a["w_dn"][e], "s_wexp")
            for k in range(NBLK):
                if k < 2:
                    eng.wait_ge(sem("s_scattered"), 16 * NT)
                    eng.wait_ge(sem("s_kh_sb"), 4)
                else:
                    eng.wait_ge(sem("s_xbT"), k - 1)
                eng.dma_start(xb[k % 2], sorted_rows[k * P:(k + 1) * P, :]).then_inc(sem(f"s_xb{k % 2}"), 16)
            o_v = out.rearrange("(t p) d -> p t d", p=P)
            for h in range(4):
                eng.wait_ge(sem("s_final"), h + 1)
                eng.dma_start(o_v[:, 2 * h:2 * h + 2, :], routed[:, 2 * h:2 * h + 2, :]).then_inc(sem("s_out"), 16)
            for k in range(OB):
                eng.wait_ge(sem(f"s_ob{k}"), 16 * blocks_of_buffer(k))
            eng.wait_ge(sem("s_out"), 64)

        def layer_norm_stats(eng, link, src, wait=None):
            for t in range(NT):
                if wait is not None:
                    wait(t)
                last = nc.vector.bn_stats(st[:, t, :], src[:, t, :])
            link(last)
            for t in range(NT):
                last = nc.vector.bn_aggr(mv[:, t, :], st[:, t, :])
            link(last)

        @block.vector
        def _(dve):
            link = chain(dve, "s_dve_chain")
            told = {}

            def tell(ins, name):
                told[name] = told.get(name, 0) + 1
                ins.then_inc(sem(name), 1)
                dve.wait_ge(sem(name), told[name])
            tt = nc.vector.tensor_tensor
            tsc = nc.vector.tensor_scalar

            def normalise(k, src, dst, signal, wait=None):
                layer_norm_stats(dve, link, src, wait)
                tsc(ve[:, :], mv[:, :, 1], 1e-5, None, ALU.add).then_inc(sem("s_var"), 1)
                dve.wait_ge(sem("s_rstd"), k)
                for t in range(NT):
                    tsc(dst[:, t, :], src[:, t, :], mv[:, t, 0:1], rstd[:, t:t + 1], ALU.subtract, ALU.mult)\
                        .then_inc(sem(signal), 1)

            nc.vector.memset(ones[:, :], 1.0).then_inc(sem("s_ones"), 1)
            nc.vector.memset(krep[:, :, :, :], 0.0)
            normalise(1, x_res, xn, "s_xn0", lambda t: dve.wait_ge(sem(f"s_x{t // 4}"), 16) if t % 4 == 0 else None)

            for k in range(8):
                dve.wait_ge(sem("s_wprep"), max(k + 1, 4))
                if k < 2:
                    nc.vector.tensor_copy(wcat0[:, 4 * k:4 * k + 4, 0:P],
                                          ps[:, k, :].rearrange("p (n c) -> p n c", n=4)).then_inc(sem("s_wprep_sb"), 1)
                elif k < 4:
                    nc.vector.tensor_copy(wcat1[:, 4 * (k - 2):4 * (k - 2) + 4, 0:P],
                                          ps[0:QL2, k, :].rearrange("p (n c) -> p n c", n=4)).then_inc(sem("s_wprep_sb"), 1)
                else:
                    nc.vector.tensor_copy(wo_abs[:, 2 * (k - 4):2 * (k - 4) + 2, :],
                                          ps[:, k, :].rearrange("p (h c) -> p h c", h=2)).then_inc(sem("s_wprep_sb"), 1)
            for t in range(NT):
                dve.wait_ge(sem("s_kvp"), t + 1)
                nc.vector.tensor_copy(kvraw[:, t, :], ps[:, 4 + t % 2, :]).then_inc(sem("s_kvraw"), 1)
            for g in range(4):
                dve.wait_ge(sem("s_QTp"), g + 1)
                tsc(QT[:, g, :], ps[:, 2 * (g % 2):2 * (g % 2) + 2, :].rearrange("p k c -> p (k c)"), -FSCALE, None, ALU.mult)\
                    .then_inc(sem("s_QT"), 1)

            dve.wait_ge(sem("s_small"), SMALL)
            dve.wait_ge(sem("s_sumsq"), NT)
            tsc(small[:, 0, :], small[:, 2, :], 1.0 / QL, 1e-6, ALU.mult, ALU.add)
            tsc(small[:, 1, :], small[:, 3, :], 1.0 / KVL, 1e-6, ALU.mult, ALU.add).then_inc(sem("s_ms"), 1)
            dve.wait_ge(sem("s_rms"), 1)
            rq = small[:, 4, :]
            rk = small[:, 5, :]
            tt(qs[:, :, :], praw[:, :, 0:QL], rq.unsqueeze(2).broadcast_to([P, NT, QL]), ALU.mult).then_inc(sem("s_qs"), 1)
            link(tt(kc[:, :, 0:KVL], praw[:, :, QL:QL + KVL], rk.unsqueeze(2).broadcast_to([P, NT, KVL]), ALU.mult))
            link(tt(kc[:, :, 0:KVL], kc[:, :, 0:KVL], lnkv[:, :].unsqueeze(1).broadcast_to([P, NT, KVL]), ALU.mult))
            pe_v = praw[:, :, QL + KVL:QL + KVL + ROPE].rearrange("p (b h) c -> p b h c", b=NB)
            nc.vector.tensor_copy(kc[:, :, P:P + KVL], kc[:, :, 0:KVL])
            kp_v = kc[:, :, KVL:P].rearrange("p (b h) c -> p b h c", b=NB)
            rt = [gtmp.rearrange("p t d h -> p (t d h)")[:, k * 256:(k + 1) * 256]
                  .rearrange("p (b h c) -> p b h c", b=NB, h=2) for k in range(4)]
            for h in range(2):
                co = rope_tok[:, h, :].unsqueeze(1).broadcast_to([P, NB, 32])
                si = rope_tok[:, 2 + h, :].unsqueeze(1).broadcast_to([P, NB, 32])
                a1, a2 = pe_v[:, :, h, 0:32], pe_v[:, :, h, 32:64]
                tt(rt[0][:, :, h, :], a1, co, ALU.mult)
                tt(rt[1][:, :, h, :], a2, si, ALU.mult)
                tt(rt[2][:, :, h, :], a2, co, ALU.mult)
                link(tt(rt[3][:, :, h, :], a1, si, ALU.mult))
                tt(kp_v[:, :, h, 0:32], rt[0][:, :, h, :], rt[1][:, :, h, :], ALU.subtract)
                last = tt(kp_v[:, :, h, 32:64], rt[2][:, :, h, :], rt[3][:, :, h, :], ALU.add)
            tell(last, "s_kc")

            gl = praw[:, :, QL + KVL + ROPE:W_IN]
            gm = small[:, 6, :]
            bc = lambda v: v.unsqueeze(2).broadcast_to([P, NT, NH])
            io = iota[:, :].unsqueeze(1).broadcast_to([P, NT, NH])
            link(nc.vector.tensor_reduce(gm, gl, X, ALU.max))
            tt(gsm[:, :, :], gl, bc(gm), ALU.subtract).then_inc(sem("s_gsub"), 1)
            link(tt(oneh[:, :, :], gl, bc(gm), ALU.is_equal))
            link(nc.vector.scalar_tensor_tensor(oneh[:, :, :], oneh[:, :, :], -float(NH), io, ALU.mult, ALU.add))
            link(nc.vector.tensor_reduce(small[:, 7, :], oneh[:, :, :], X, ALU.min))
            link(tsc(small[:, 7, :], small[:, 7, :], float(NH), None, ALU.add))
            link(tt(oneh[:, :, :], io, bc(small[:, 7, :]), ALU.is_equal))
            dve.wait_ge(sem("s_gexp"), 1)
            link(nc.vector.tensor_reduce(small[:, 8, :], gsm[:, :, :], X, ALU.add))
            link(nc.vector.reciprocal(small[:, 9, :], small[:, 8, :]))
            for w in range(2):
                for t in range(NT):
                    last = tt(gtmp[:, t], kvraw[:, t, w * D:(w + 1) * D].rearrange("p (h d) -> p d h", h=NH),
                              oneh[:, t, :].unsqueeze(1).broadcast_to([P, HD, NH]), ALU.mult)
                link(last)
                link(nc.vector.tensor_reduce(kred[:, w], gtmp, X, ALU.add))
            tt(vsh[:, :, 0:HD], kred[:, 1], small[:, 9, :].unsqueeze(2).broadcast_to([P, NT, HD]), ALU.mult)
            for r in range(4):
                last = nc.vector.tensor_copy(krep[:, :, r, 0:HD], kred[:, 0])
            last.then_inc(sem("s_krep"), 1)
            dve.wait_ge(sem("s_krep"), 1)
            nc.vector.memset(vsh[:, :, HD:], 1.0)

            for k in range(2):
                dve.wait_ge(sem("s_latT"), 2 * k + 1)
                tsc(qaT0[:, 512 * k:512 * k + 512], ps[:, k, :], lnq[:, 0:1], None, ALU.mult)
                dve.wait_ge(sem("s_latT"), 2 * k + 2)
                tsc(qaT1[:, 512 * k:512 * k + 512], ps[0:QL2, 2 + k, :], lnq[0:QL2, 1:2], None, ALU.mult).then_inc(sem("s_lat_sb"), 1)
            phase_end(dve, 0)

            def sine(n):
                dve.wait_ge(sem("s_swapped"), 64 * (n + 1))
                v = rot.rearrange("p (b s) -> p b s", b=NB)
                tt(v, v, rope_feat[:, 1, :].unsqueeze(1).broadcast_to([P, NB, S]), ALU.mult).then_inc(sem("s_sine"), 1)

            def body(i, first, last):
                for l in range(mla.U):
                    u = i * mla.U + l
                    if l == 3 and not first:
                        dve_norm(dve, mla, 2 * i - 1, 1, xcn[:, :, KVL:P])
                    if l == 7:
                        if not first:
                            dve.wait_ge(sem("s_xT"), 2 * i)
                        dve_norm(dve, mla, 2 * i, 0, xcn[:, :, 0:KVL])
                    dve_max(dve, mla, i, l, first)
                    if not (first and l < 2):
                        dve_turned(dve, mla, u - 2, l, None if first and l < 4 else u - 3)
                    if l == 5 and not last:
                        sine(i + 1)
                if last:
                    for u in (NP * mla.U - 2, NP * mla.U - 1):
                        dve_turned(dve, mla, u, u, u - 1)
                    dve_norm(dve, mla, 2 * i + 1, 1, xcn[:, :, KVL:P])
            sine(0)
            loop(dve, NP, body)
            phase_end(dve, 1)

            def heads_normed(i, h):
                dve.wait_ge(sem("s_yT"), 2 * i + h + 1)
                v = ps[:, 6 + h, :].rearrange("p (t j c) -> p t j c", t=4, j=4)
                rv = ri.rearrange("p a t -> p (a t)").rearrange("p (t j) -> p t j", t=4)
                nc.vector.reciprocal(rv, v[:, :, :, HD]).then_inc(sem("s_yrecip"), 1)
                dve.wait_ge(sem("s_yrecip"), 2 * i + h + 1)
                tt(y[:, 4 * h:4 * h + 4, ds(i * 4 * HD, 4 * HD)].rearrange("p t (j c) -> p t j c", j=4), v[:, :, :, 0:HD],
                   rv.unsqueeze(3).broadcast_to([P, 4, 4, HD]), ALU.mult).then_inc(sem("s_yn"), 1)
                dve.wait_ge(sem("s_yn"), 2 * i + h + 1)

            def bodyg(i, first, last):
                for l in range(gat.U):
                    u = i * gat.U + l
                    dve_max(dve, gat, i, l, first)
                    if not (first and l < 2):
                        dve_turned(dve, gat, u - 2, l - 2, None if first and l < 10 else 4 * i + (l - 2) // 4 - 1)
                    if l == 14:
                        heads_normed(i, 0)
                    if l == 6 and not first:
                        heads_normed(i - 1, 1)
                if last:
                    for l in (14, 15):
                        dve_turned(dve, gat, i * gat.U + l, l, 4 * i + 2)
                    heads_normed(i, 1)
            loop(dve, 4, bodyg)
            dve.wait_ge(sem("s_g0"), 1)
            for k in range(4):
                dve.wait_ge(sem("s_sp"), k + 1)
                link(tt(y[:, 2 * k:2 * k + 2, :], ps[:, 5 + k % 2, :].rearrange("p (t c) -> p t c", t=2),
                        y[:, 2 * k:2 * k + 2, :], ALU.mult))
                tell(tt(x_res[:, 2 * k:2 * k + 2, :], x_res[:, 2 * k:2 * k + 2, :], y[:, 2 * k:2 * k + 2, :], ALU.add), "s_spr")
            phase_end(dve, 2)

            normalise(2, x_res, xn, "s_xn1")

            dve.wait_ge(sem("s_router"), 1)
            link(nc.vector.tensor_copy(rl[:, :, :], ps[:, 2, 0:NT * E].rearrange("p (t e) -> p t e", t=NT)))
            rb = lambda v: v.unsqueeze(2).broadcast_to([P, NT, E])
            ie = iota[:, 0:E].unsqueeze(1).broadcast_to([P, NT, E])
            tell(nc.vector.tensor_reduce(small[:, 16, :], rl[:, :, :], X, ALU.max), "s_top")
            link(tt(roneh[:, :, :], rl[:, :, :], rb(small[:, 16, :]), ALU.is_equal))
            link(nc.vector.scalar_tensor_tensor(roneh[:, :, :], roneh[:, :, :], -float(E), ie, ALU.mult, ALU.add))
            link(nc.vector.tensor_reduce(small[:, 17, :], roneh[:, :, :], X, ALU.min))
            link(tsc(small[:, 17, :], small[:, 17, :], float(E), None, ALU.add))
            link(tt(roneh[:, :, :], ie, rb(small[:, 17, :]), ALU.is_equal))
            for e in range(E):
                last = nc.vector.tensor_tensor_scan(upto[:, :, e], ones[:, 0:NT], roneh[:, :, e], 0.0, op0=ALU.mult, op1=ALU.add)
            tell(last, "s_oneh")
            dve.wait_ge(sem("s_gate_exp"), 1)
            link(tsc(small[:, 19, :], small[:, 18, :], 1.0, None, ALU.add))
            tell(nc.vector.reciprocal(small[:, 20, :], small[:, 19, :]), "s_gate")
            link(tsc(small[:, 21, :], iota[:, 0:E], float(P), None, ALU.mult))
            dve.wait_ge(sem("s_rank"), 1)
            rank = ps[:, B7, 0:NT * E].rearrange("p (t e) -> p t e", t=NT)
            link(nc.vector.tensor_copy(small[:, 22, :], ps[:, B7, NT * E:NT * E + E]))
            link(tt(rtmp[:, 0:E, :], small[:, 22, :].unsqueeze(2).broadcast_to([P, E, E]),
                    small[:, 21, :].unsqueeze(1).broadcast_to([P, E, E]), ALU.is_gt))
            link(nc.vector.tensor_reduce(small[:, 23, :], rtmp[:, 0:E, :], X, ALU.add))
            link(nc.vector.tensor_tensor_scan(small[:, 24, :], ones[:, 0:E], small[:, 23, :], 0.0, op0=ALU.mult, op1=ALU.add))
            link(tt(small[:, 25, :], small[:, 24, :], small[:, 23, :], ALU.subtract))
            link(tsc(small[:, 25, :], small[:, 25, :], float(P), -1.0, ALU.mult, ALU.add))
            link(tt(rl[:, :, :], rank, small[:, 25, :].unsqueeze(1).broadcast_to([P, NT, E]), ALU.add))
            tell(tt(rl[:, :, :], rl[:, :, :], roneh[:, :, :], ALU.mult), "s_rank_used")
            link(nc.vector.tensor_reduce(small[:, 26, :], rl[:, :, :], X, ALU.add))
            nc.vector.tensor_copy(pos_i[:, :], small[:, 26, :]).then_inc(sem("s_pos"), 1)
            link(tt(rtmp[:, :, :], small[:, 24, :].unsqueeze(1).broadcast_to([P, 16, E]),
                    iota[:, :].unsqueeze(2).broadcast_to([P, 16, E]), ALU.is_le))
            eidf = small[:, 27:29, :].rearrange("p a t -> p (a t)")
            link(nc.vector.tensor_reduce(eidf, rtmp[:, :, :], X, ALU.add))
            link(tsc(eidf, eidf, float(E - 1), None, ALU.min))
            nc.vector.tensor_copy(eid_i[:, :], eidf).then_inc(sem("s_eid"), 1)

            def inner_rows(m):
                dve.wait_ge(sem("s_silu"), m + 1)
                if m >= 2:
                    dve.wait_ge(sem("s_hT"), m - 1)
                tt(inn_sb[m % 2], act_sb[m % 2], ps[:, BU[m % 2], :], ALU.mult).then_inc(sem("s_h"), 1)

            def out_rows(m):
                dve.wait_ge(sem("s_down"), m + 1)
                if not is_block(m):
                    dst = y[:, tile_of(m), :]
                else:
                    k = m - A0
                    if k >= OB:
                        dve.wait_ge(sem(f"s_ob{k % OB}"), 16 * (k // OB))
                    dst = ob[k % OB]
                nc.vector.tensor_copy(dst, ps[:, BD, 0:D]).then_inc(sem("s_acc"), 1)

            N = NB * T1 * D

            def maxima(f):
                dve.wait_ge(sem("s_mk"), 2 + f)
                link(tt(steps4(hseq)[:, f, :, 1:T1], steps4(hseq)[:, f, :, 1:T1], plain(kraw)[:, f].rearrange("p (b t) -> p b t", b=NB),
                        ALU.add))
                for b in range(NB):
                    last = nc.vector.tensor_tensor_scan(steps4(hmin)[:, f, b, :], steps4(hseq)[:, f, b, :],
                                                        steps4(hseq)[:, f, b, :], -BIG, op0=ALU.max, op1=ALU.max)
                last.then_inc(sem("s_maxima"), 1)

            def piece(m):
                if m == 0:
                    dve.wait_ge(sem("s_kh_sb"), 4)
                    tell(tsc(hmin, hseq, 0.0, None, ALU.min), "s_mnh")
                    tell(tsc(hseq, hseq, 0.0, 2.0, ALU.max, ALU.mult), "s_num")
                if m == 2:
                    dve.wait_ge(sem("s_l1"), 1)
                    tell(tt(plain(kpos), plain(kpos), plain(e1), ALU.add), "s_softplus")
                if m == 4:
                    dve.wait_ge(sem("s_l3"), 1)
                    dve.wait_ge(sem("s_cand"), 1)
                    link(tt(hseq, hseq, hmin, ALU.add))
                if m == 6:
                    maxima(0)
                if m == 7:
                    maxima(1)
                if m == 7:
                    dve.wait_ge(sem("s_maxima"), 2)
                    tt(hseq, hseq, hmin, ALU.subtract).then_inc(sem("s_scan_in"), 1)
                if m == 9:
                    dve.wait_ge(sem("s_scan_exp"), 1)
                    for f in range(DK):
                        for b in range(NB):
                            last = nc.vector.tensor_tensor_scan(steps4(kraw)[:, f, b, :], steps4(kpos)[:, f, b, :],
                                                                steps4(hseq)[:, f, b, :], 0.0, op0=ALU.mult, op1=ALU.add)
                    last.then_inc(sem("s_scan"), 1)
                if m == 11:
                    dve.wait_ge(sem("s_scan_ln"), 1)
                    dve.wait_ge(sem("s_mxa"), 1)
                    nc.vector.tensor_tensor_reduce(out=kraw, in0=kraw, in1=e1, scale=1.0, scalar=0.0, op0=ALU.add, op1=ALU.add,
                                                   accum_out=small[:, 10, 0:1]).then_inc(sem("s_sum"), 1)
                if m == 13:
                    dve.wait_ge(sem("s_tot"), 1)
                    tell(tsc(small[:, 11, 0:1], ps[:, B7, 0:1], -1.0 / N, None, ALU.mult), "s_mean")
                if m == 16:
                    dve.wait_ge(sem("s_tot"), 2)
                    tsc(small[:, 13, :], ps[:, B7, 0:1].broadcast_to([P, NT]), 1.0 / (N - 1), None, ALU.mult).then_inc(sem("s_varh"), 1)
                    dve.wait_ge(sem("s_rstdh"), 1)
                    tell(tt(small[:, 15, 0:1], small[:, 14, 0:1], small[:, 11, 0:1], ALU.mult), "s_hscale")
                if 18 <= m < 22:
                    k = m - 18
                    dve.wait_ge(sem("s_hback"), k + 1)
                    tell(tt(x2[:, 2 * k:2 * k + 2, :], ps[:, B7, :].rearrange("p (t c) -> p t c", t=2), xn[:, 2 * k:2 * k + 2, :],
                            ALU.add), "s_hback_used")
                    for t in (2 * k, 2 * k + 1):
                        last = nc.vector.bn_stats(st[:, t, :], x2[:, t, :])
                    link(last)
                if m == 21:
                    for t in range(NT):
                        last = nc.vector.bn_aggr(mv[:, t, :], st[:, t, :])
                    link(last)
                    tsc(ve[:, :], mv[:, :, 1], 1e-5, None, ALU.add).then_inc(sem("s_var"), 1)
                if m == 22:
                    dve.wait_ge(sem("s_ln1"), 32)
                    dve.wait_ge(sem("s_rstd"), 3)
                    for t in range(NT):
                        last = tsc(s1[:, t, :], x2[:, t, :], mv[:, t, 0:1], rstd[:, t:t + 1], ALU.subtract, ALU.mult)
                    link(last)
                    tt(s1, s1, ln1[:, 0, :].unsqueeze(1).broadcast_to([P, NT, D]), ALU.mult).then_inc(sem("s_s1w"), 1)

            for m in range(M):
                inner_rows(m)
                if m >= 2:
                    out_rows(m - 2)
                piece(m)
            out_rows(M - 2)
            out_rows(M - 1)
            dve.wait_ge(sem("s_s1"), 1)
            for h in range(4):
                v = slice(2 * h, 2 * h + 2)
                dve.wait_ge(sem(f"s_gathered{h}"), 32)
                tell(tt(y[:, v, :], y[:, v, :], routed[:, v, :], ALU.add), "s_ffn")
            for h in range(4):
                v = slice(2 * h, 2 * h + 2)
                dve.wait_ge(sem("s_g1"), h + 1)
                link(tt(y[:, v, :], s1[:, v, :], y[:, v, :], ALU.mult))
                tt(routed[:, v, :], y[:, v, :], x_res[:, v, :], ALU.add).then_inc(sem("s_final"), 1)

        @block.gpsimd
        def _(pool):
            tt = nc.gpsimd.tensor_tensor
            nc.gpsimd.memset(half_neg[:, :], -0.5).then_inc(sem("s_half"), 1)
            nc.gpsimd.memset(zeros, 0.0).then_inc(sem("s_zeros"), 1)
            pool.wait_ge(sem("s_half"), 1)

            def root(k, dst, src, w, signal):
                tt(dst, src, half_neg[:, 0:w], ALU.pow).then_inc(sem(signal), 1)
            pool.wait_ge(sem("s_var"), 1)
            root(1, rstd[:, :], ve[:, :], NT, "s_rstd")
            pool.wait_ge(sem("s_ms"), 1)
            root(1, small[:, 4:6, :].rearrange("p a t -> p (a t)"), small[:, 0:2, :].rearrange("p a t -> p (a t)"), 2 * NT, "s_rms")
            pool.wait_ge(sem("s_wprep_sb"), 8)
            nc.gpsimd.memset(kz[:, :, :], 0.0)
            phase_end(pool, 0)

            def stage(n, free):
                if free:
                    pool.wait_ge(sem("s_absp"), 2 * n)
                nc.gpsimd.tensor_copy(ws0, wcat0[:, ds(n, 1), :].rearrange("p h c -> p (h c)"))
                nc.gpsimd.tensor_copy(ws1, wcat1[:, ds(n, 1), :].rearrange("p h c -> p (h c)")).then_inc(sem("s_stage"), 1)

            def cosine(n):
                pool.wait_ge(sem("s_swapped"), 64 * (n + 1))
                v = raw.rearrange("p (b s) -> p b s", b=NB)
                tt(v, v, rope_feat[:, 0, :].unsqueeze(1).broadcast_to([P, NB, S]), ALU.mult).then_inc(sem("s_cosine"), 1)
                pool.wait_ge(sem("s_cosine"), n + 1)
                pool.wait_ge(sem("s_sine"), n + 1)

            def rotated_a(n, free):
                if free:
                    pool.wait_ge(mla.s_S, 8 * n - 4)
                tt(qh[0][64:P, :], raw[64:P, :], rot[64:P, :], ALU.add).then_inc(sem("s_qA"), 1)
                pool.wait_ge(sem("s_qA"), n + 1)

            def rotated_b(n, free):
                if free:
                    pool.wait_ge(mla.s_S, 8 * n)
                tt(qh[1][0:64, :], raw[0:64, :], rot[0:64, :], ALU.add).then_inc(sem("s_qB"), 1)
                pool.wait_ge(sem("s_qB"), n + 1)

            stage(0, False)
            cosine(0)
            rotated_a(0, False)
            stage(1, True)

            def body(i, first, last):
                rotated_b(i, not first)
                if not last:
                    cosine(i + 1)
                    rotated_a(i + 1, True)
            body(0, True, False)
            with pool.Fori(1, NP - 1) as i:
                stage(i + 1, True)
                body(i, False, False)
            body(NP - 1, False, True)
            for j in range(4):
                r = slice(SLOT * j, SLOT * (j + 1))
                nc.gpsimd.tensor_copy(kz[r, j, :], kshT[r, :]).then_inc(sem("s_kz"), 1)
                pool.wait_ge(sem("s_kz"), j + 1)
            phase_end(pool, 1)

            for b in range(NB):
                nc.gpsimd.tensor_copy(QS[:, b * S:(b + 1) * S], QT[:, 0, b * S:(b + 1) * S]).then_inc(sem("s_slot"), 1)
            with pool.Fori(1, 4) as i:
                for b in range(NB):
                    pool.wait_ge(gat.s_S, 16 * i + 4 * b - 12)
                    nc.gpsimd.tensor_copy(QS[:, b * S:(b + 1) * S], QT[:, ds(i, 1), b * S:(b + 1) * S].rearrange("p g t -> p (g t)"))\
                        .then_inc(sem("s_slot"), 1)
            phase_end(pool, 2)
            pool.wait_ge(sem("s_var"), 2)
            root(2, rstd[:, :], ve[:, :], NT, "s_rstd")
            pool.wait_ge(sem("s_gate"), 1)
            for t in range(NT):
                if t >= 2:
                    pool.wait_ge(sem(f"s_scat{t % 2}"), 16 * (t // 2))
                nc.gpsimd.tensor_scalar(xg[t % 2], xn[:, t, :], small[:, 20, t:t + 1], 1.0, ALU.mult, ALU.mult)\
                    .then_inc(sem("s_xg"), 1)
                pool.wait_ge(sem("s_xg"), t + 1)
                if t == 0:
                    pool.wait_ge(sem("s_pos"), 1)
                nc.gpsimd.indirect_dma_start(out=sorted_rows, out_offset=bass.IndirectOffsetOnAxis(pos_i[:, t:t + 1], 0),
                                             in_=xg[t % 2], in_offset=None).then_inc(sem(f"s_scat{t % 2}"), 16)
            for k in range(2):
                pool.wait_ge(sem(f"s_scat{k}"), 16 * (NT // 2))
            pool.sem_inc(sem("s_scattered"), 16 * NT)

            pool.wait_ge(sem("s_softplus"), 1)
            tt(plain(kraw), plain(kraw), plain(kpos), ALU.subtract).then_inc(sem("s_mk"), 1)
            pool.wait_ge(sem("s_e2"), 1)
            tt(hmin, hmin, e1, ALU.subtract).then_inc(sem("s_cand"), 1)
            pool.wait_ge(sem("s_cand"), 1)
            nc.gpsimd.memset(steps4(e1)[:, :, :, 0:1], 0.0).then_inc(sem("s_acum0"), 1)
            for f in range(DK):
                pool.wait_ge(sem("s_acum_sb"), 2 * f + 2)
                pool.wait_ge(sem("s_mk"), 1)
                v = plain(kraw)[:, f].rearrange("p (b t) -> p b t", b=NB)
                tt(v, v, steps4(e1)[:, f, :, 1:T1], ALU.add).then_inc(sem("s_mk"), 1)
            pool.wait_ge(sem("s_acum"), 4)
            pool.wait_ge(sem("s_mk"), 3)
            nc.gpsimd.memset(steps4(kpos)[:, :, :, 0:1], 0.0)
            for f in range(DK):
                pool.wait_ge(sem("s_maxima"), f + 1)
                tt(steps4(kpos)[:, f, :, 1:T1], steps4(hmin)[:, f, :, 0:S], steps4(hmin)[:, f, :, 1:T1], ALU.subtract)\
                    .then_inc(sem("s_dmax"), 1)
            tt(e1, hmin, e1, ALU.subtract).then_inc(sem("s_mxa"), 1)
            pool.wait_ge(sem("s_varh"), 1)
            root(0, small[:, 14, :], small[:, 13, :], NT, "s_rstdh")
            pool.wait_ge(sem("s_var"), 3)
            root(3, rstd[:, :], ve[:, :], NT, "s_rstd")
            pool.wait_ge(sem("s_s1w"), 1)
            tt(s1, s1, ln1[:, 1, :].unsqueeze(1).broadcast_to([P, NT, D]), ALU.add).then_inc(sem("s_s1"), 1)
            for k in range(OB):
                pool.wait_ge(sem(f"s_ob{k}"), 16 * blocks_of_buffer(k))
            pool.wait_ge(sem("s_hout"), 1)
            for t in range(NT):
                nc.gpsimd.indirect_dma_start(out=routed[:, t, :], out_offset=None, in_=sorted_out,
                                             in_offset=bass.IndirectOffsetOnAxis(pos_i[:, t:t + 1], 0))\
                    .then_inc(sem(f"s_gathered{t // 2}"), 16)

        @block.scalar
        def _(act):
            A = nc.scalar.activation

            def turned_rows(signal_in, signal_out):
                for t in range(NT):
                    act.wait_ge(sem(signal_in), t + 1)
                    A(xnT[:, :, t * P:(t + 1) * P], ps[:, t % 2, 0:2 * P].rearrange("p (k c) -> p k c", k=2), ACT.Copy)\
                        .then_inc(sem(signal_out), 1)
            turned_rows("s_xT0", "s_xnT0")
            for t in range(NT):
                act.wait_ge(sem("s_inp"), t + 1)
                A(praw[:, t, :], ps[:, 2 + t % 2, 0:W_IN], ACT.Copy).then_inc(sem("s_praw"), 1)
            act.wait_ge(sem("s_praw"), NT)
            for t in range(NT):
                A(xn[:, t, 0:QL], praw[:, t, 0:QL], ACT.Square, accum_out=small[:, 2, t:t + 1])
                A(xn[:, t, QL:QL + KVL], praw[:, t, QL:QL + KVL], ACT.Square, accum_out=small[:, 3, t:t + 1])\
                    .then_inc(sem("s_sumsq"), 1)
            act.wait_ge(sem("s_gsub"), 1)
            A(gsm[:, :, :], gsm[:, :, :], ACT.Exp).then_inc(sem("s_gexp"), 1)
            for k in range(2):
                act.wait_ge(sem("s_kTT"), k + 1)
                A(kT[:, 512 * k:512 * k + 512], ps[:, 4 + k, :], ACT.Copy)
            for k in range(2):
                act.wait_ge(sem("s_kTT"), k + 3)
                A(kTB[:, 512 * k:512 * k + 512], ps[:, k, :], ACT.Copy)
            for k in range(2):
                act.wait_ge(sem("s_kshTT"), k + 1)
                A(kshT[:, 512 * k:512 * k + 512], ps[:, 6 + k, :], ACT.Copy)
            phase_end(act, 0)

            def copy_raw(n, h, first):
                act.wait_ge(sem("s_ropep"), 2 * n + h + 1)
                if not first:
                    act.wait_ge(sem("s_qB"), n)
                A(raw[:, h * 512:(h + 1) * 512], ps[:, QB[h], :], ACT.Copy).then_inc(sem("s_raw"), 1)

            def copy_abs(n, j, first):
                act.wait_ge(sem("s_absp"), 2 * n + 2)
                if not first:
                    act.wait_ge(mla.s_S, 8 * n - 4 + 4 * j)
                r = slice(64 * j, 64 * j + 64)
                A(qh[j][r, :], Qp[r, :], ACT.Copy, scale=-SCALE).then_inc(sem(("s_absA", "s_absB")[j]), 1)

            def out_turned(i, h):
                act.wait_ge(sem("s_xT"), 2 * i + h + 1)
                A(xcT[:, ds(i, 1), h * 512:(h + 1) * 512].rearrange("p n t -> p (n t)"), ps[:, XB, :], ACT.Copy)\
                    .then_inc(sem("s_xcT"), 1)

            def body(i, first, last):
                for l in range(mla.U):
                    if l % NB == 0 and not first:
                        act.wait_ge(sem("s_normed"), 2 * i + l // NB - 1)
                    act_exp(act, mla, i, l, first, by_head(rs))
                    if l == 0:
                        copy_abs(i, 1, first)
                    if l in (2, 3) and not last:
                        copy_raw(i + 1, l - 2, False)
                    if l == 5 and not last:
                        copy_abs(i + 1, 0, False)
                    if not first and l in (4, 6):
                        out_turned(i - 1, (l - 4) // 2)
                if last:
                    out_turned(i, 0)
                    out_turned(i, 1)
            copy_raw(0, 0, True)
            copy_raw(0, 1, True)
            copy_abs(0, 0, True)
            loop(act, NP, body)
            phase_end(act, 1)

            def copy_heads(i, h):
                act.wait_ge(gat.s_av, 4 * i + 2 * h + 2)
                A(ysum[:, h * 512:(h + 1) * 512], ps[:, 4 + h, :], ACT.Copy).then_inc(sem("s_ysum"), 1)

            def bodyg(i, first, last):
                for l in range(gat.U):
                    act_exp(act, gat, i, l, first)
                    if l == 11:
                        copy_heads(i, 0)
                    if l == 3 and not first:
                        copy_heads(i - 1, 1)
                if last:
                    copy_heads(i, 1)
            loop(act, 4, bodyg)
            act.wait_ge(sem("s_yn"), 2 * 4)
            A(y[:, :, :], y[:, :, :], ACT.Silu).then_inc(sem("s_g0"), 1)
            phase_end(act, 2)

            turned_rows("s_xT1", "s_xnT1")
            act.wait_ge(sem("s_small"), SMALL)
            for f in range(DK):
                act.wait_ge(sem("s_khp"), f + 1)
                A(plain(kraw)[:, f, :], ps[:, 4 + 2 * f:6 + 2 * f, :].rearrange("p k c -> p (k c)"), ACT.Identity,
                  bias=bz[:, 0, f:f + 1]).then_inc(sem("s_kh_sb"), 1)
            for f in range(DK):
                act.wait_ge(sem("s_khp"), 3 + f)
                A(steps4(hseq)[:, f, :, 0], bz[:, 2, f:f + 1].broadcast_to([P, NB]), ACT.Copy)
                A(steps4(hseq)[:, f, :, 1:T1], ps[:, 2 * f:2 * f + 2, :].rearrange("p k (b t) -> p (k b) t", t=S), ACT.Identity,
                  bias=bz[:, 1, f:f + 1]).then_inc(sem("s_kh_sb"), 1)
            act.wait_ge(sem("s_top"), 1)
            A(small[:, 18, :], small[:, 16, :], ACT.Exp, scale=-1.0).then_inc(sem("s_gate_exp"), 1)

            def inner_turned(m):
                act.wait_ge(sem("s_hT"), m + 1)
                if m >= 2:
                    act.wait_ge(sem("s_down"), m - 1)
                A(innT_sb[m % 2], ps[:, BT[m % 2], :], ACT.Copy).then_inc(sem("s_hT_sb"), 1)

            def rows_in(k):
                act.wait_ge(sem("s_xbT"), k + 1)
                if k >= 2:
                    act.wait_ge(sem("s_gu"), A0 + k - 1)
                A(xbT[k % 2][:, :], ps[:, B7, 0:D], ACT.Copy).then_inc(sem("s_xbT_sb"), 1)

            def piece(m):
                if m == 0:
                    act.wait_ge(sem("s_kh_sb"), 2)
                    A(plain(e1), plain(kraw), ACT.Abs).then_inc(sem("s_absk"), 1)
                    A(plain(kpos), plain(kraw), ACT.Relu)
                if m == 1:
                    act.wait_ge(sem("s_absk"), 1)
                    A(plain(e1), plain(e1), ACT.Exp, scale=-1.0).then_inc(sem("s_act1"), 1)
                    act.wait_ge(sem("s_act1"), 1)
                    A(plain(e1), plain(e1), ACT.Ln, bias=1.0).then_inc(sem("s_l1"), 1)
                if m == 2:
                    act.wait_ge(sem("s_num"), 1)
                    A(hseq, hseq, ACT.Ln, bias=1.0).then_inc(sem("s_l3"), 1)
                if m == 3:
                    act.wait_ge(sem("s_softplus"), 1)
                    A(e1, hmin, ACT.Exp).then_inc(sem("s_act1"), 1)
                    act.wait_ge(sem("s_act1"), 2)
                    A(e1, e1, ACT.Ln, bias=1.0).then_inc(sem("s_e2"), 1)
                if 4 <= m < 8:
                    k = m - 4
                    act.wait_ge(sem("s_acum0"), 1)
                    act.wait_ge(sem("s_acum"), k + 1)
                    A(steps4(e1)[:, k // 2, 2 * (k % 2):2 * (k % 2) + 2, 1:T1], ps[:, B7, :].rearrange("p (b t) -> p b t", b=2),
                      ACT.Copy).then_inc(sem("s_acum_sb"), 1)
                if m == 8:
                    act.wait_ge(sem("s_scan_in"), 1)
                    A(hseq, hseq, ACT.Exp)
                    act.wait_ge(sem("s_dmax"), 2)
                    A(kpos, kpos, ACT.Exp).then_inc(sem("s_scan_exp"), 1)
                if m == 10:
                    act.wait_ge(sem("s_scan"), 1)
                    A(kraw, kraw, ACT.Ln).then_inc(sem("s_scan_ln"), 1)
                if m == 14:
                    act.wait_ge(sem("s_mean"), 1)
                    A(hseq, kraw, ACT.Square, bias=small[:, 11, 0:1], accum_out=small[:, 12, 0:1]).then_inc(sem("s_sumsqh"), 1)
                if m == 17:
                    act.wait_ge(sem("s_hscale"), 1)
                    act.wait_ge(sem("s_sumsqh"), 1)
                    for f in range(DK):
                        last = A(hout[:, f * TOK:(f + 1) * TOK].rearrange("p (b t) -> p b t", b=NB), steps4(kraw)[:, f, :, 1:T1],
                                 ACT.Exp, scale=small[:, 14, 0:1], bias=small[:, 15, 0:1])
                    last.then_inc(sem("s_hout"), 1)

            for m in range(M):
                act.wait_ge(sem("s_gu"), m + 1)
                if m >= 2:
                    act.wait_ge(sem("s_h"), m - 1)
                A(act_sb[m % 2], ps[:, BG[m % 2], :], ACT.Silu).then_inc(sem("s_silu"), 1)
                if m >= 1:
                    inner_turned(m - 1)
                if is_block(m + 1):
                    rows_in(m + 1 - A0)
                if is_block(m - 3):
                    k = m - 3 - A0
                    act.wait_ge(sem("s_acc"), m - 2)
                    act.dma_start(sorted_out[k * P:(k + 1) * P, :], ob[k % OB]).then_inc(sem(f"s_ob{k % OB}"), 16)
                piece(m)
            inner_turned(M - 1)
            for h in range(4):
                act.wait_ge(sem("s_ffn"), h + 1)
                A(y[:, 2 * h:2 * h + 2, :], y[:, 2 * h:2 * h + 2, :], ACT.Silu).then_inc(sem("s_g1"), 1)

        @block.tensor
        def _(pe):
            mm_ = nc.tensor.matmul
            tr = lambda o, i_, k=P: nc.tensor.transpose(o, i_, ident[0:k, 0:k])
            pe.wait_ge(sem("s_wnope"), 32)
            for k in range(2):
                for h in range(8):
                    last = mm_(ps[:, k, h * 64:(h + 1) * 64], w_nope[:, 8 * k + h, 0:P], w_kabs[:, 8 * k + h, :], start=True, stop=True)
                last.then_inc(sem("s_wprep"), 1)
            for k in range(2):
                for h in range(8):
                    last = mm_(ps[0:QL2, 2 + k, h * 64:(h + 1) * 64], w_nope[:, 8 * k + h, P:QL], w_kabs[:, 8 * k + h, :],
                               start=True, stop=True)
                last.then_inc(sem("s_wprep"), 1)
            pe.wait_ge(sem("s_wo"), 32)
            for k in range(4):
                for q in range(2):
                    for j in range(2):
                        h = 4 * k + 2 * q + j
                        last = mm_(ps[64 * j:64 * j + 64, 4 + k, q * D:(q + 1) * D], w_oabs[:, h, :], w_o[:, h, :],
                                   start=True, stop=True)
                last.then_inc(sem("s_wprep"), 1)

            def rows_turned(src, s_in, s_out, s_copied, banks_free):
                pe.wait_ge(sem("s_ident"), 16)
                for t in range(NT):
                    pe.wait_ge(sem(s_in), t + 1)
                    if t < 2:
                        banks_free(t)
                    else:
                        pe.wait_ge(sem(s_copied), t - 1)
                    tr(ps[:, t % 2, 0:P], src[:, t, 0:P])
                    tr(ps[:, t % 2, P:2 * P], src[:, t, P:2 * P]).then_inc(sem(s_out), 1)
            rows_turned(xn, "s_xn0", "s_xT0", "s_xnT0", lambda t: pe.wait_ge(sem("s_wprep_sb"), 8))

            pe.wait_ge(sem("s_win"), 48)
            for t in range(NT):
                pe.wait_ge(sem("s_xnT0"), t + 1)
                if t >= 2:
                    pe.wait_ge(sem("s_praw"), t - 1)
                    pe.wait_ge(sem("s_kvraw"), t - 1)
                for k in range(DK):
                    last = mm_(ps[:, 2 + t % 2, 0:W_IN], xnT[:, k, t * P:(t + 1) * P], w_in[:, k, :], start=(k == 0), stop=(k == 1))
                last.then_inc(sem("s_inp"), 1)
                for k in range(DK):
                    last = mm_(ps[:, 4 + t % 2, :], xnT[:, k, t * P:(t + 1) * P], w_kv[:, k, :], start=(k == 0), stop=(k == 1))
                last.then_inc(sem("s_kvp"), 1)
            for g in range(4):
                if g < 2:
                    pe.wait_ge(sem("s_praw"), NT)
                else:
                    pe.wait_ge(sem("s_QT"), g - 1)
                for h in range(2):
                    for k in range(DK):
                        last = mm_(ps[:, 2 * (g % 2) + h, :], w_q[:, k, g * P:(g + 1) * P], xnT[:, k, h * 512:(h + 1) * 512],
                                   start=(k == 0), stop=(k == 1))
                last.then_inc(sem("s_QTp"), 1)
            pe.wait_ge(sem("s_QT"), 4)
            pe.wait_ge(sem("s_kvraw"), NT)
            pe.wait_ge(sem("s_qs"), 1)
            for k in range(2):
                for t in range(4):
                    last = tr(ps[:, k, t * P:(t + 1) * P], qs[:, 4 * k + t, 0:P])
                last.then_inc(sem("s_latT"), 1)
                for t in range(4):
                    last = tr(ps[0:QL2, 2 + k, t * P:(t + 1) * P], qs[:, 4 * k + t, P:QL])
                last.then_inc(sem("s_latT"), 1)
            pe.wait_ge(sem("s_kc"), 1)
            for k in range(2):
                for t in range(4):
                    last = tr(ps[:, 4 + k, t * P:(t + 1) * P], kc[:, 4 * k + t, 0:P])
                last.then_inc(sem("s_kTT"), 1)
            for k in range(2):
                pe.wait_ge(sem("s_lat_sb"), k + 1)
                for t in range(4):
                    last = tr(ps[:, k, t * P:(t + 1) * P], kc[:, 4 * k + t, KVL:P + KVL])
                last.then_inc(sem("s_kTT"), 1)
            pe.wait_ge(sem("s_krep"), 1)
            for k in range(2):
                for t in range(4):
                    last = tr(ps[:, 6 + k, t * P:(t + 1) * P], krep[:, 4 * k + t].rearrange("p r s -> p (r s)"))
                last.then_inc(sem("s_kshTT"), 1)
            phase_end(pe, 0)

            def queries(n, part, h, first):
                at = (P, 0)[part]
                if part == 0 and h == 0:
                    pe.wait_ge(sem("s_stage"), n + 1)
                    if not first:
                        pe.wait_ge(sem("s_absB"), n)
                if part == 1:
                    pe.wait_ge(sem("s_raw"), 2 * n + h + 1)
                mm_(ps[:, QB[h], :], ws0[:, at:at + P], qaT0[:, h * 512:(h + 1) * 512], start=True, stop=False)
                mm_(ps[:, QB[h], :], ws1[:, at:at + P], qaT1[:, h * 512:(h + 1) * 512], start=False, stop=True)\
                    .then_inc(sem(("s_ropep", "s_absp")[part]), 1)

            def out_turned(i, h, first):
                if h == 0:
                    pe.wait_ge(sem("s_normed"), 2 * i + 2)
                if not (first and h == 0):
                    pe.wait_ge(sem("s_xcT"), 2 * i + h)
                for t in range(4):
                    last = tr(ps[:, XB, t * P:(t + 1) * P], xcn[:, 4 * h + t, :])
                last.then_inc(sem("s_xT"), 1)

            def body(i, first, last):
                for l in range(mla.U):
                    u = i * mla.U + l
                    if l % NB == 0:
                        for signal in (("s_qA", "s_absA"), ("s_qB", "s_absB"))[l // NB]:
                            pe.wait_ge(sem(signal), i + 1)
                    pe_scores(pe, mla, i, l, first)
                    if not (first and l < 2):
                        pe_turn(pe, mla, u - 2, l % 2, first and l < 4)
                    if l in (1, 2, 3, 4) and not last:
                        queries(i + 1, (l - 1) // 2, (l - 1) % 2, False)
                    if not (first and l < 3):
                        pe_heads(pe, mla, u - 3, (l - 3) % 2, (u - 3) // NB if first else 2 * i - (l < 3) + (l >= 7), (l - 3) % NB,
                                 first and l < 7)
                    if not first and l in (4, 5):
                        out_turned(i - 1, l - 4, False)
                if last:
                    u = NP * mla.U
                    pe_turn(pe, mla, u - 2, 0, False)
                    pe_heads(pe, mla, u - 3, 1, 2 * i + 1, 1, False)
                    pe_turn(pe, mla, u - 1, 1, False)
                    pe_heads(pe, mla, u - 2, 0, 2 * i + 1, 2, False)
                    pe_heads(pe, mla, u - 1, 1, 2 * i + 1, 3, False)
                    out_turned(i, 0, False)
                    out_turned(i, 1, False)
            for part in range(2):
                for h in range(2):
                    queries(0, part, h, True)
            loop(pe, NP, body)
            phase_end(pe, 1)

            def four_heads(i, b, first):
                pe.wait_ge(gat.s_pt, 16 * i + 4 * b + 4)
                if b % 2 == 0 and not first:
                    pe.wait_ge(sem("s_ysum"), 2 * i + b // 2 - 1)
                o = lambda j, lo, hi: ps[SLOT * j:SLOT * (j + 1), 4 + b // 2, b % 2 * S + lo:b % 2 * S + hi]
                for j in range(4):
                    mm_(o(j, 0, S), vsh[:, 2 * b, :], gat.turned(4 * b + j)[:, 0:S], start=True, stop=False)
                for j in range(4):
                    last = mm_(o(j, P, S), vsh[:, 2 * b + 1, :], gat.turned(4 * b + j)[:, S:WIDE], start=False, stop=True)
                last.then_inc(gat.s_av, 1)

            def heads_back(i, h):
                pe.wait_ge(sem("s_ysum"), 2 * i + h + 1)
                for t in range(4):
                    last = tr(ps[:, 6 + h, t * P:(t + 1) * P], ysum[:, h * 512 + t * P:h * 512 + (t + 1) * P])
                last.then_inc(sem("s_yT"), 1)

            def bodyg(i, first, last):
                for l in range(gat.U):
                    u = i * gat.U + l
                    if l % 4 == 0:
                        pe.wait_ge(sem("s_slot"), 4 * i + l // 4 + 1)
                    pe_scores(pe, gat, i, l, first)
                    if not (first and l < 2):
                        pe_turn(pe, gat, u - 2, l % 2, first and l < 4)
                    if l % 4 == 2 and l > 2:
                        four_heads(i, l // 4 - 1, first)
                    if l == 2 and not first:
                        four_heads(i - 1, 3, False)
                    if l == 12:
                        heads_back(i, 0)
                    if l == 4 and not first:
                        heads_back(i - 1, 1)
                if last:
                    pe_turn(pe, gat, i * gat.U + 14, 0, False)
                    pe_turn(pe, gat, i * gat.U + 15, 1, False)
                    four_heads(i, 3, False)
                    heads_back(i, 1)
            loop(pe, 4, bodyg)
            for k in range(4):
                if k >= 2:
                    pe.wait_ge(sem("s_spr"), k - 1)
                for q in range(2):
                    t = 2 * k + q
                    for n in range(NP):
                        last = mm_(ps[:, 5 + k % 2, q * D:(q + 1) * D], xcT[:, n, t * P:(t + 1) * P], wo_abs[:, n, :],
                                   start=(n == 0), stop=(n == NP - 1))
                last.then_inc(sem("s_sp"), 1)
            phase_end(pe, 2)

            rows_turned(xn, "s_xn1", "s_xT1", "s_xnT1", lambda t: None)
            pe.wait_ge(sem("s_xnT1"), NT)
            for t in range(NT):
                for k in range(DK):
                    last = mm_(ps[:, 2, t * E:(t + 1) * E], xnT[:, k, t * P:(t + 1) * P], wr[:, k, :], start=(k == 0), stop=(k == 1))
            last.then_inc(sem("s_router"), 1)
            pe.wait_ge(sem("s_wz"), 32)
            for w, wt in enumerate((wz, wh)):
                for f in range(DK):
                    bank = (4, 6, 0, 2)[2 * w + f]
                    if bank == 2:
                        pe.wait_ge(sem("s_top"), 1)
                    for h in range(2):
                        for k in range(DK):
                            last = mm_(ps[:, bank + h, :], wt[:, k, f * P:(f + 1) * P], xnT[:, k, h * 512:(h + 1) * 512],
                                       start=(k == 0), stop=(k == 1))
                    last.then_inc(sem("s_khp"), 1)
            pe.wait_ge(sem("s_ones"), 1)
            pe.wait_ge(sem("s_small"), SMALL)
            pe.wait_ge(sem("s_oneh"), 1)
            pe.wait_ge(sem("s_kh_sb"), 2)
            flat = lambda v: v[:, :, :].rearrange("p t e -> p (t e)")
            mm_(ps[:, B7, 0:NT * E], ones[:, :], flat(upto), start=True, stop=False)
            mm_(ps[:, B7, 0:NT * E], after[:, :], flat(roneh), start=False, stop=True)
            mm_(ps[:, B7, NT * E:NT * E + E], ones[:, :], upto[:, NT - 1, :], start=True, stop=True).then_inc(sem("s_rank"), 1)
            pe.wait_ge(sem("s_kh_sb"), 4)

            last_use = [("s_rank_used", 1)]

            def bank7(signal, value):
                pe.wait_ge(sem(last_use[0][0]), last_use[0][1])
                last_use[0] = (signal, value)

            def turn_inner(m):
                pe.wait_ge(sem("s_h"), m + 1)
                if m >= 2:
                    pe.wait_ge(sem("s_hT_sb"), m - 1)
                for k in range(4):
                    last = tr(ps[:, BT[m % 2], k * P:(k + 1) * P], inn_sb[m % 2][:, k * P:(k + 1) * P])
                last.then_inc(sem("s_hT"), 1)

            expert = [None] * M

            def weight(m, at, n):
                if not is_block(m):
                    return SH[:, at:at + n]
                return EXP[:, ds(expert[m] * FX + at, n)]

            def gate_up(m):
                if not is_block(m):
                    rows = lambda k: xnT[:, k, tile_of(m) * P:(tile_of(m) + 1) * P]
                else:
                    b = m - A0
                    pe.wait_ge(sem("s_xbT_sb"), b + 1)
                    rows = lambda k: xbT[b % 2][:, k * P:(k + 1) * P]
                    expert[m] = pe.value_load(eid_i[0:1, b:b + 1], min_val=0, max_val=E - 1)
                if m >= 2:
                    pe.wait_ge(sem("s_silu"), m - 1)
                    pe.wait_ge(sem("s_h"), m - 1)
                for w, bank in ((0, BG[m % 2]), (1, BU[m % 2])):
                    for k in range(DK):
                        last = mm_(ps[:, bank, :], rows(k), weight(m, k * 2 * FF + w * FF, FF), start=(k == 0), stop=(k == 1))
                last.then_inc(sem("s_gu"), 1)

            def down(m):
                pe.wait_ge(sem("s_hT_sb"), m + 1)
                if m >= 1:
                    pe.wait_ge(sem("s_acc"), m)
                for k in range(4):
                    last = mm_(ps[:, BD, 0:D], innT_sb[m % 2][:, k * P:(k + 1) * P], weight(m, DK * 2 * FF + k * D, D),
                               start=(k == 0), stop=(k == 3))
                last.then_inc(sem("s_down"), 1)

            def rows_in(k):
                pe.wait_ge(sem(f"s_xb{k % 2}"), 16 * (k // 2 + 1))
                bank7("s_xbT_sb", k + 1)
                tr(ps[:, B7, 0:P], xb[k % 2][:, 0:P])
                tr(ps[:, B7, P:2 * P], xb[k % 2][:, P:2 * P]).then_inc(sem("s_xbT"), 1)

            def piece(m):
                if 4 <= m < 8:
                    f, h = (m - 4) // 2, (m - 4) % 2
                    pe.wait_ge(sem("s_softplus"), 1)
                    bank7("s_acum_sb", m - 3)
                    v = lambda g: plain(kpos)[:, g, h * 512:(h + 1) * 512]
                    if f == 1:
                        mm_(ps[:, B7, :], ones[:, :], v(0), start=True, stop=False)
                    mm_(ps[:, B7, :], upper[:, :], v(f), start=(f == 0), stop=True).then_inc(sem("s_acum"), 1)
                if m == 13:
                    pe.wait_ge(sem("s_sum"), 1)
                    bank7("s_mean", 1)
                    mm_(ps[:, B7, 0:1], ones[:, :], small[:, 10, 0:1], start=True, stop=True).then_inc(sem("s_tot"), 1)
                if m == 16:
                    pe.wait_ge(sem("s_sumsqh"), 1)
                    bank7("s_varh", 1)
                    mm_(ps[:, B7, 0:1], ones[:, :], small[:, 12, 0:1], start=True, stop=True).then_inc(sem("s_tot"), 1)
                if 18 <= m < 22:
                    k = m - 18
                    pe.wait_ge(sem("s_hout"), 1)
                    bank7("s_hback_used", k + 1)
                    for q in range(2):
                        for f in range(DK):
                            t = 2 * k + q
                            last = tr(ps[:, B7, q * D + f * P:q * D + (f + 1) * P], hout[:, f * TOK + t * P:f * TOK + (t + 1) * P])
                    last.then_inc(sem("s_hback"), 1)

            pe.wait_ge(sem("s_wsh"), 32)
            for m in range(M):
                if m == A0:
                    pe.wait_ge(sem("s_wexp"), 32 * E)
                    pe.wait_ge(sem("s_eid"), 1)
                gate_up(m)
                if m >= 1:
                    turn_inner(m - 1)
                if m >= 2:
                    down(m - 2)
                if is_block(m + 1):
                    rows_in(m + 1 - A0)
                piece(m)
            turn_inner(M - 1)
            down(M - 2)
            down(M - 1)


def layouts(i):
    import numpy as np
    c = lambda v: np.ascontiguousarray(v)
    arr = {k: np.asarray(v) for k, v in i.items()}
    turned = np.concatenate([np.arange(0, ROPE, 2), np.arange(1, ROPE, 2)])
    wkv_a = arr["L0_attn_wkv_a"]
    wq_b = arr["L0_attn_wq_b"].reshape(NH, NOPE + ROPE, QL)
    wkv_b = arr["L0_attn_wkv_b"].reshape(NH, NOPE + VH, KVL)
    wqkv = arr["L0_ffn_W_qkv"]
    w_q = np.zeros((D, NH, SLOT), wqkv.dtype)
    w_q[:, :, 0:HD] = wqkv[0:D].reshape(NH, HD, D).transpose(2, 0, 1)
    d = {
        "x": arr["L0_attn_hidden_states"].reshape(TOK, D),
        "w_in": np.concatenate([arr["L0_attn_wq_a"], wkv_a[0:KVL], wkv_a[KVL:][turned], arr["L0_ffn_W_gate"]], axis=0).T,
        "w_kv": wqkv[D:].T,
        "w_q": w_q.reshape(D, NH * SLOT),
        "w_nope": wq_b[:, 0:NOPE],
        "w_pe": wq_b[:, NOPE:][:, turned].transpose(2, 0, 1).reshape(QL, NH // 2, 2, ROPE)[:, :, ::-1].reshape(QL, NH * ROPE),
        "w_kabs": wkv_b[:, 0:NOPE],
        "w_oabs": wkv_b[:, VH:],
        "w_o": arr["L0_attn_wo"].T,
        "q_ln": arr["L0_attn_q_a_ln_w"], "kv_ln": arr["L0_attn_kv_a_ln_w"],
        "w_z": arr["L1_attn_W_z"].T, "w_h": arr["L1_attn_W_h"].T,
        "rows_l1": np.stack([arr[f"L1_attn_{n}"].reshape(DK, P) for n in ("b_z", "b_h", "h0")]).transpose(2, 0, 1),
        "ln_w": arr["L1_attn_ln_w"], "ln_b": arr["L1_attn_ln_b"],
        "w_router": arr["L1_ffn_router_w"].T,
        "w_gu": arr["L1_ffn_w_gate_up"], "w_dn": arr["L1_ffn_w_down"],
        "w_shared_gu": arr["L1_ffn_shared_gate_up"], "w_shared_dn": arr["L1_ffn_shared_down"],
    }
    return {k: c(v) for k, v in d.items()}


def kernel(**inputs):
    import concourse.bacc as _bacc
    from concourse import mybir as _mybir
    from concourse.bass_utils import run_bass_kernel_spmd as _run

    arrays = {**layouts(inputs), **constants()}
    nc = _bacc.Bacc("TRN2", target_bir_lowering=False, num_devices=1)
    a = {k: nc.dram_tensor(f"in_{k}", v.shape, _mybir.dt.from_np(v.dtype), kind="ExternalInput").ap() for k, v in arrays.items()}
    out = nc.dram_tensor("out", (TOK, D), _mybir.dt.float32, kind="ExternalOutput").ap()
    recurrent_kernel(nc, a, out)
    r = _run(nc, [{f"in_{k}": v for k, v in arrays.items()}], core_ids=[0])
    return r.results[0]["out"].reshape(NB, S, D)
```

```python
import concourse.bass as bass
from concourse import mybir
from contextlib import ExitStack

P = 128
NB, S, D = 4, 256, 256
TOK = NB * S
NT = TOK // P
DK = D // P
NH = 16
QL, KVL, NOPE, ROPE, VH = 192, 64, 128, 64, 128
QL2 = QL - P
SCALE = float(NOPE + ROPE) ** -0.5
HD = D // NH
SLOT = 32
QROWS = 64
FSCALE = float(HD) ** -0.5
W_IN = QL + KVL + ROPE + NH
FF, E = 512, 8
NBLK = NT + E - 1
FX = DK * 2 * FF + (FF // P) * D
T1 = S + 1
BIG = 3.0e38
SMALL = 16 * 6
LATE = 16 * 9
WIDE = 3 * P


def constants():
    import numpy as np
    i = np.arange(P)
    ident = np.eye(P, dtype=np.float32)
    upper = (i[:, None] <= i[None, :]).astype(np.float32)
    diag = np.where(i[None, :] > i[:, None], np.float32(BIG), np.float32(0))
    mask = np.concatenate([diag, np.zeros((P, P), np.float32), diag], axis=1)
    inv = (np.float32(1.0) / np.float32(10000.0) ** (np.arange(0, ROPE, 2, dtype=np.float32) / np.float32(ROPE))).astype(np.float32)
    f = np.arange(S, dtype=np.float32)[:, None] * inv[None, :]
    cos, sin = np.cos(f.astype(np.float64)), np.sin(f.astype(np.float64))
    tok = np.concatenate([cos.reshape(2, P, 32), sin.reshape(2, P, 32)], axis=0).transpose(1, 0, 2)
    feat = np.zeros((P, 2, S))
    feat[:, 0] = np.concatenate([cos.T] * 4, axis=0) * -SCALE
    feat[:, 1] = np.concatenate([-sin.T, sin.T] * 2, axis=0) * -SCALE
    return {
        "c_ident": ident, "c_upper": upper, "c_after": upper - 1, "c_mask": mask,
        "c_rope_tok": np.ascontiguousarray(tok, dtype=np.float32).reshape(P, 4 * 32),
        "c_rope_feat": feat.astype(np.float32).reshape(P, 2 * S),
        "c_iota": np.broadcast_to(np.arange(NH, dtype=np.float32), (P, NH)).copy(),
    }


def recurrent_kernel(nc, a, out, debug=None):
    f32 = mybir.dt.float32
    f32r = mybir.dt.float32r
    ALU = mybir.AluOpType
    ACT = mybir.ActivationFunctionType
    X = mybir.AxisListType.X
    ds = bass.ds

    ctx = ExitStack()
    with ctx:
        def sb(name, shape):
            return ctx.enter_context(nc.sbuf_tensor(name, shape, f32))

        sems = {}

        def sem(name):
            if name not in sems:
                sems[name] = ctx.enter_context(nc.semaphore(name))
            return sems[name]

        ident = sb("ident", [P, P])
        upper = sb("upper", [P, P])
        after = sb("after", [P, P])
        ones = sb("ones", [P, P])
        tables = sb("tables", [P, 512])
        mask = tables[:, 0:WIDE]
        rope_tok = tables[:, WIDE:512].rearrange("p (k c) -> p k c", k=4)
        ln1 = tables[:, :].rearrange("p (k c) -> p k c", k=2)
        rope_feat = sb("rope_feat", [P, 2, S])
        iota = sb("iota", [P, NH])
        x_res = sb("x_res", [P, NT, D])
        xn = sb("xn", [P, NT, D])
        xnT = sb("xnT", [P, DK, TOK])
        y = sb("y", [P, NT, D])
        st = sb("st", [P, NT, 6])
        mv = sb("mv", [P, NT, 2])
        half_neg = sb("half_neg", [P, 2 * NT])
        ve = sb("ve", [P, NT])
        rstd = sb("rstd", [P, NT])
        mx = sb("mx", [P, 2, 8])
        stand = sb("stand", [P, 16])
        rs = sb("rs", [P, 2, 8])
        ri = sb("ri", [P, 2, 8])
        routing = sb("routing", [P, 2 * NT * E])
        def first_columns(*shapes):
            with ExitStack() as above:
                return [above.enter_context(nc.sbuf_tensor(name, shape, f32r)) for name, shape in shapes]
        kz_t, = first_columns(("kz", [P, 2, TOK]))
        EXP = sb("EXP", [P, E * FX])
        QS_t, tail_t, wtail_t = first_columns(("QS", [P, 2, TOK]), ("q_tail", [P, 2, TOK]), ("w_tail", [P, 2 * P]))
        R2 = sb("R2", [P, 5 * DK * NB * T1])
        SH = sb("SH", [P, FX])
        MB = sb("MB", [P, 4608 + 256])
        RB, RA, RC = EXP[:, 0:9216], EXP[:, 9216:17408], EXP[:, 17408:21504]
        qaT0 = EXP[:, 21504:22528]
        kT = EXP[:, 23552:24576]
        RD = R2[:, 0:8192]
        kc = R2[:, 8704:10240].rearrange("p (t c) -> p t c", t=NT)
        kshT = RA[:, 7168:8192]
        wo_abs = SH[:, 0:2048].rearrange("p (n c) -> p n c", n=NH // 2)
        kTB = SH[:, 2048:3072]
        scr = [MB[:, k * WIDE:(k + 1) * WIDE] for k in range(2)]
        prob = [MB[:, (2 + k) * WIDE:(3 + k) * WIDE] for k in range(2)]
        probT = [MB[:, (4 + k) * WIDE:(5 + k) * WIDE] for k in range(2)]
        w_in = MB[:, 2304:2304 + DK * W_IN].rearrange("p (k c) -> p k c", k=DK)
        w_kv = MB[:, 3072:4096].rearrange("p (k c) -> p k c", k=DK)
        w_q = MB[:, 4096:4608].rearrange("p (k c) -> p k c", k=DK)

        ps = ctx.enter_context(nc.psum_tensor("ps", [P, 8, 512], f32))

        kvraw = RA[:, 0:4096].rearrange("p (t c) -> p t c", t=NT)
        gtmp = [RC[:, w * 2048:(w + 1) * 2048].rearrange("p (t d h) -> p t d h", t=NT, d=HD) for w in range(2)]
        qs = RA[:, 5120:7168].rearrange("p (t c) -> p t c", t=NT)
        xcT = RA[:, :].rearrange("p (n t) -> p n t", n=NH // 2)
        w_nope = RB[:, 0:4096].rearrange("p (h c) -> p h c", h=NH)
        w_kabs = RA[:, 7168:8192].rearrange("p (h c) -> p h c", h=NH)
        w_oabs = RB[:, 4096:5120].rearrange("p (h c) -> p h c", h=NH)
        w_o = RB[:, 5120:9216].rearrange("p (h c) -> p h c", h=NH)
        QT = [v.rearrange("p (g t) -> p g t", g=4) for v in (RC[:, :], RB[:, 2048:6144])]
        q_hi = xn[:, :, :].rearrange("p (g t) c -> p g (t c)", g=2)
        q_lo = RB[:, 6144:8192].rearrange("p (g t) -> p g t", g=2)
        yflat = y[:, :, :].rearrange("p t c -> p (t c)")
        wcat0 = yflat.rearrange("p (n c) -> p n c", n=NH // 2)
        wcat1 = R2[:, 6656:8704].rearrange("p (n c) -> p n c", n=NH // 2)
        lnq = sb("lnq", [P, 2])
        lnkv = MB[:, 4736:4800]
        praw = RD[:, 0:NT * W_IN].rearrange("p (t c) -> p t c", t=NT)
        q_tail, w_tail = tail_t[:, :, :], wtail_t[:, :]
        qh = [RD[:, k * 1024:(k + 1) * 1024] for k in range(2)]
        raw = RD[:, 4352:5376]
        rot = RD[:, 5376:6400]
        ws0 = RD[:, 6400:6656]
        probT4 = probT + [EXP[:, 22528 + k * WIDE:22528 + (k + 1) * WIDE] for k in range(2)]
        wo_swapped = R2[:, 6144:8192].rearrange("p (n c) -> p n c", n=NH // 2)
        QS = QS_t[:, :, :]
        kz = kz_t[:, :, :]
        probT8 = [RB[:, 6144 + k * WIDE:6144 + (k + 1) * WIDE] for k in range(8)]
        ysum = RD[:, 2048:3072]
        scr4 = [RD[:, 3072 + k * WIDE:3072 + (k + 1) * WIDE] for k in range(4)]
        prob4 = [RD[:, 4608 + k * WIDE:4608 + (k + 1) * WIDE] for k in range(4)]
        vsh = MB[:, 2304:2560].rearrange("p (t c) -> p t c", t=NT)
        small = sb("small", [P, 32, NT])
        oneh = MB[:, 4608:4736].rearrange("p (t h) -> p t h", h=NH)
        krep = RB[:, 8192:9216].rearrange("p (t r d) -> p t r d", t=NT, r=8)
        glog = oneh
        gsm = MB[:, 2560:2688].rearrange("p (t h) -> p t h", t=NT)
        kred = MB[:, 2688:2944].rearrange("p (w t d) -> p w t d", w=2, t=NT)
        khi = MB[:, 2944:3072].rearrange("p (t d) -> p t d", t=NT)

        bar = {}
        marks = []

        def dump(eng, name, ap):
            if debug is not None and name in debug:
                eng.dma_start(debug[name], ap).then_inc(sem("s_dbg"), 16)
                marks.append(name)
                eng.wait_ge(sem("s_dbg"), 16 * len(marks))

        def phase_end(eng, k):
            eng.drain().then_inc(sem(f"s_phase{k}"), 1)
            eng.wait_ge(sem(f"s_phase{k}"), 5)

        def chain(eng, name):
            n = [0]

            def link(ins):
                n[0] += 1
                ins.then_inc(sem(name), 1)
                eng.wait_ge(sem(name), n[0])
                return ins
            return link

        TB = [2, 3]
        class Core:
            def __init__(self, tag, heads, place, q_of, k_of, least, turned, banks, scr, prob, ready=None):
                self.tag, self.heads, self.place = tag, heads, place
                self.banks, self.scr, self.prob, self.depth = banks, scr, prob, len(banks)
                self.q_of, self.k_of, self.least, self.turned = q_of, k_of, least, turned
                self.U = heads * NB
                s = lambda x: sem(f"{x}_{tag}")
                self.s_S, self.s_mx, self.s_P, self.s_T = s("s_scores"), s("s_max"), s("s_probs"), s("s_turned")
                self.s_pt, self.s_av = s("s_turned_sb"), s("s_heads")
                self.s_ready = sem(ready) if ready else self.s_P

        def pe_scores(pe, c, i, l, first):
            (j, b), u = c.place(l), i * c.U + l
            if not (first and l < c.depth):
                pe.wait_ge(c.s_mx, u - c.depth + 1)
            bank = ps[:, c.banks[l % c.depth], :]
            nc.tensor.matmul(bank[:, 0:P], c.q_of(j, 2 * b), c.k_of(j, b, P), start=True, stop=True)
            nc.tensor.matmul(bank[:, P:WIDE], c.q_of(j, 2 * b + 1), c.k_of(j, b, S), start=True, stop=True)\
                .then_inc(c.s_S, 1)

        def pe_turn(pe, c, u, l, bank_free):
            pe.wait_ge(c.s_ready, u + 1)
            bank_free()
            for k in range(3):
                last = nc.tensor.transpose(ps[:, TB[l % 2], k * P:(k + 1) * P], c.prob[l % c.depth][:, k * P:(k + 1) * P],
                                           ident[:, :])
            last.then_inc(c.s_T, 1)

        def dve_max(dve, c, i, l, first):
            u = i * c.U + l
            dve.wait_ge(c.s_S, u + 1)
            if not (first and l < c.depth):
                dve.wait_ge(c.s_P, u - c.depth + 1)
            if not isinstance(i, int):
                nc.vector.memset(stand[:, l:l + 1], 0.0)
            for q, (lo, hi) in enumerate(((0, P), (P, WIDE))):
                last = nc.vector.tensor_tensor_reduce(
                    out=c.scr[l % c.depth][:, lo:hi], in0=ps[:, c.banks[l % c.depth], lo:hi], in1=mask[:, lo:hi], scale=1.0, scalar=BIG,
                    op0=ALU.add, op1=ALU.min, accum_out=c.least(l, q))
            last.then_inc(c.s_mx, 1)

        def dve_turned(dve, c, u, l, used):
            dve.wait_ge(c.s_T, u + 1)
            if used is not None:
                dve.wait_ge(c.s_av, used)
            nc.vector.tensor_copy(c.turned(l), ps[:, TB[l % 2], 0:WIDE]).then_inc(c.s_pt, 1)

        def dve_scale(dve, u, l):
            dve.wait_ge(mla.s_P, u + 1)
            j, b = l // NB % 2, l % NB
            nc.vector.reciprocal(ri[:, j, 2 * b:2 * b + 2], rs[:, j, 2 * b:2 * b + 2]).then_inc(sem("s_recip"), 1)
            dve.wait_ge(sem("s_recip"), u + 1)
            for q, (lo, hi) in enumerate(((0, P), (P, WIDE))):
                last = nc.vector.tensor_scalar(prob[l % 2][:, lo:hi], prob[l % 2][:, lo:hi], ri[:, j, 2 * b + q:2 * b + q + 1], None,
                                               ALU.mult)
            last.then_inc(sem("s_scaled"), 1)

        def act_exp(act, c, i, l, first, sums=None):
            u = i * c.U + l
            act.wait_ge(c.s_mx, u + 1)
            if not (first and l < c.depth):
                act.wait_ge(c.s_T, u - c.depth + 1)
            for q, (lo, hi) in enumerate(((0, P), (P, WIDE))):
                last = nc.scalar.activation(c.prob[l % c.depth][:, lo:hi], c.scr[l % c.depth][:, lo:hi], ACT.Exp, bias=c.least(l, q), scale=-1.0,
                                            accum_out=None if sums is None else sums(l, q))
            last.then_inc(c.s_P, 1)

        by_head = lambda v: lambda l, q: v[:, l // NB % 2, 2 * (l % NB) + q:2 * (l % NB) + q + 1]
        by_step = lambda v: lambda l, q: v[:, l % 8 // 4, 2 * (l % 4) + q:2 * (l % 4) + q + 1]
        mla = Core("mla", 2, lambda l: (l // NB, l % NB), lambda j, t: qh[j][:, t * P:(t + 1) * P],
                   lambda j, b, w: (kT, kTB)[j][:, b * S:b * S + w], by_head(mx), lambda l: probT4[l % 4], (0, 1), scr, prob, "s_scaled")
        gat = Core("gat", 4, lambda l: (l % 4, l // 4), lambda j, t: QS[:, j // 2, t * P:(t + 1) * P],
                   lambda j, b, w: kz[:, j % 2, b * S:b * S + w], by_step(mx), lambda l: probT8[l % 8], (0, 1, 6, 7), scr4, prob4)

        def loop(eng, iters, body):
            body(0, True, False)
            with eng.Fori(1, iters - 1) as i:
                body(i, False, False)
            body(iters - 1, False, True)

        QB = (5, 6)
        AB = (4, 7)
        NP = NH // 2
        Qp = ps[:, 5:7, :].rearrange("p k c -> p (k c)")

        HW = DK * NB * T1
        seq = [R2[:, k * HW:(k + 1) * HW] for k in range(5)]
        steps4 = lambda v: v.rearrange("p (f b t) -> p f b t", f=DK, b=NB)
        plain = lambda v: v[:, 0:DK * TOK].rearrange("p (f t) -> p f t", f=DK)
        hseq = seq[0]
        kpos = seq[1]
        kraw = seq[2]
        e1 = seq[3]
        hmin = seq[4]
        hout = seq[0][:, 0:DK * TOK]
        x2 = seq[1][:, 0:NT * D].rearrange("p (t c) -> p t c", t=NT)
        s1 = seq[3][:, 0:NT * D].rearrange("p (t c) -> p t c", t=NT)
        routed = seq[2][:, 0:NT * D].rearrange("p (t c) -> p t c", t=NT)
        wz = w_kv[:, :, 0:D]
        wh = w_kv[:, :, D:2 * D]
        bz = sb("bz", [P, 3, 2])
        wr = sb("wr", [P, DK, E])
        act_sb = [MB[:, k * FF:(k + 1) * FF] for k in range(2)]
        inn_sb = [MB[:, 1024 + k * FF:1024 + (k + 1) * FF] for k in range(2)]
        innT_sb = [MB[:, 2048 + k * FF:2048 + (k + 1) * FF] for k in range(2)]
        xb = [MB[:, 3584 + k * D:3584 + (k + 1) * D] for k in range(2)]
        OB = 4
        ob = [MB[:, at:at + D] for at in (4096, 4352, 3072, 3328)]
        all_stored = lambda k: 16 * ((NBLK - k + OB - 1) // OB)
        xbT = [rope_feat[:, k, :] for k in range(2)]
        roneh = routing[:, 0:NT * E].rearrange("p (t e) -> p t e", e=E)
        upto = routing[:, NT * E:].rearrange("p (t e) -> p t e", e=E)
        rl = MB[:, 4608:4608 + NT * E].rearrange("p (t e) -> p t e", e=E)
        rtmp = MB[:, 4672:4672 + 16 * E].rearrange("p (t e) -> p t e", e=E)
        pos_i = ctx.enter_context(nc.sbuf_tensor("pos_i", [P, NT], mybir.dt.int32))
        eid_i = ctx.enter_context(nc.sbuf_tensor("eid_i", [P, 16], mybir.dt.int32))
        sorted_rows = nc.dram_tensor("sorted_rows", (NBLK * P, D), f32, kind="Internal").ap()
        sorted_out = nc.dram_tensor("sorted_out", (NBLK * P, D), f32, kind="Internal").ap()
        no_keys = RB[:, 2048:3072]
        zeros = no_keys[:, 0:D]
        A0 = 4
        M = NT + NBLK
        EARLY = 4
        is_block = lambda m: A0 <= m < A0 + NBLK
        blocks_in = lambda m: (0, 1) if m == A0 - 1 else (m + 2 - A0,) if A0 <= m < A0 + NBLK - 2 else ()
        tile_of = lambda m: m if m < A0 else m - NBLK
        BG, BU, BT, BD, B7 = (0, 1), (2, 3), (4, 5), 6, 7
        KH = (4, 5, 2, 6, 7, 0, 1, 3)

        block = ctx.enter_context(nc.Block())

        @block.sync
        def _(sp_):
            eng = sp_
            x_v = a["x"].rearrange("(t p) d -> p t d", p=P)
            load = lambda s, dst, src: eng.dma_start(dst, src).then_inc(sem(s), 16)
            for h in range(2):
                load(f"s_x{h}", x_res[:, 4 * h:4 * h + 4, :], x_v[:, 4 * h:4 * h + 4, :])
            load("s_ident", ident[:, :], a["c_ident"])
            kview = lambda w: w.rearrange("(k p) c -> p k c", p=P)
            load("s_win", w_in[:, :, :], kview(a["w_in"]))
            load("s_wnope", w_nope, a["w_nope"].rearrange("h p c -> p h c"))
            load("s_wnope", w_kabs, a["w_kabs"].rearrange("h p c -> p h c"))
            load("s_small", lnq[:, 0:1], a["q_ln"][0:P].unsqueeze(1))
            for k in range(2):
                load("s_small", lnq[QL2 * k:QL2 * (k + 1), 1:2], a["q_ln"][P:QL].unsqueeze(1))
            load("s_small", lnkv[:, :], a["kv_ln"].unsqueeze(0).broadcast_to([P, KVL]))
            load("s_small", rope_tok, a["c_rope_tok"].rearrange("p (k c) -> p k c", k=4))
            load("s_small", iota[:, :], a["c_iota"])
            load("s_wkv", w_kv[:, :, :], kview(a["w_kv"]))
            load("s_wkv", w_q[:, :, :], kview(a["w_q"]))
            load("s_late", wcat0[:, :, P:2 * P], a["w_pe"][0:P].rearrange("p (n c) -> p n c", n=NP))
            for k in range(2):
                load("s_late", wcat1[QL2 * k:QL2 * (k + 1), :, P:2 * P], a["w_pe"][P:QL].rearrange("p (n c) -> p n c", n=NP))
            load("s_wo", w_oabs, a["w_oabs"].rearrange("h p c -> p h c"))
            load("s_wo", w_o, a["w_o"].rearrange("(h p) c -> p h c", p=P))
            load("s_late", mask, a["c_mask"])
            load("s_late", rope_feat[:, :, :], a["c_rope_feat"].rearrange("p (k c) -> p k c", k=2))
            load("s_late", upper[:, :], a["c_upper"])
            load("s_late", after[:, :], a["c_after"])
            load("s_late", bz[:, :, :], a["rows_l1"])
            load("s_late", wr[:, :, :], kview(a["w_router"]))
            eng.wait_ge(sem("s_late"), LATE)

            def swap(n, first):
                eng.wait_ge(sem("s_raw"), 2 * n + 2)
                if not first:
                    eng.wait_ge(sem("s_qB"), n)
                for k in range(4):
                    eng.dma_start(rot[32 * k:32 * k + 32, :], raw[32 * (k ^ 1):32 * (k ^ 1) + 32, :]).then_inc(sem("s_swapped"), 16)
            swap(0, True)
            phase_end(eng, 0)

            def spread(a_):
                for j in range(4):
                    for k, part in enumerate((q_hi, q_lo, q_hi, q_lo)):
                        at = QROWS * (j % 2) + HD * k
                        src = HD * (4 * a_ + j)
                        eng.dma_start(QT[j // 2][at:at + HD, 2 * a_:2 * a_ + 2, :], part[src:src + HD, :, :]).then_inc(sem("s_spread"), 16)
            eng.dma_start(sorted_rows.rearrange("(k p) c -> p k c", p=P), zeros.unsqueeze(1).broadcast_to([P, NBLK, D]))\
               .then_inc(sem("s_cleared"), 16)
            swap(1, False)
            eng.wait_ge(sem("s_cleared"), 16)
            eng.wait_ge(sem("s_krep"), 1)
            spread(0)
            swap(2, False)
            spread(1)
            with eng.Fori(3, NP) as i:
                swap(i, False)
            load("s_wz", wz, kview(a["w_z"]))
            load("s_wz", wh, kview(a["w_h"]))
            phase_end(eng, 1)
            for k in range(2):
                load("s_swap_wo", wo_swapped[64 * k:64 * k + 64, :, :], wo_abs[64 * (1 - k):64 * (1 - k) + 64, :, :])
            def weights(dst, gu, dn, signal):
                load(signal, dst[:, 0:2048].rearrange("p (k c) -> p k c", k=DK), gu.rearrange("(k p) c -> p k c", p=P))
                load(signal, dst[:, 2048:FX].rearrange("p (k c) -> p k c", k=4), dn.rearrange("(k p) c -> p k c", p=P))
            order = (0, 1, 2, 6, 7, 3, 4, 5)
            for e in order[:5]:
                if e == 0:
                    eng.wait_ge(sem("s_yT"), 8)
                    eng.wait_ge(sem("s_slot"), 4 * NB)
                weights(EXP[:, e * FX:(e + 1) * FX], a["w_gu"][e], a["w_dn"][e], "s_wexp")
            eng.wait_ge(sem("s_sp"), 4)
            weights(SH, a["w_shared_gu"], a["w_shared_dn"], "s_wsh")
            for k, name in enumerate(("ln_w", "ln_b")):
                load("s_ln1", ln1[:, k, :], a[name].unsqueeze(0).broadcast_to([P, D]))
            for e in order[5:]:
                weights(EXP[:, e * FX:(e + 1) * FX], a["w_gu"][e], a["w_dn"][e], "s_wexp")
            for k in range(NBLK):
                if k < 2:
                    for q in range(OB):
                        eng.wait_ge(sem(f"s_scat{q}"), 16 * (NT // OB))
                    eng.wait_ge(sem("s_khp"), 8)
                else:
                    eng.wait_ge(sem("s_xbT"), k - 1)
                eng.dma_start(xb[k % 2], sorted_rows[k * P:(k + 1) * P, :]).then_inc(sem(f"s_xb{k % 2}"), 16)
            o_v = out.rearrange("(t p) d -> p t d", p=P)
            for h in range(4):
                eng.wait_ge(sem("s_final"), h + 1)
                eng.dma_start(o_v[:, 2 * h:2 * h + 2, :], routed[:, 2 * h:2 * h + 2, :]).then_inc(sem("s_out"), 16)
            for k in range(OB):
                eng.wait_ge(sem(f"s_ob{k}"), all_stored(k))
            eng.wait_ge(sem("s_out"), 64)

        def layer_norm_stats(eng, link, src, wait=None):
            for t in range(NT):
                if wait is not None:
                    wait(t)
                last = nc.vector.bn_stats(st[:, t, :], src[:, t, :])
            link(last)
            for t in range(NT):
                last = nc.vector.bn_aggr(mv[:, t, :], st[:, t, :])
            link(last)

        @block.vector
        def _(dve):
            link = chain(dve, "s_dve_chain")
            told = {}

            def tell(ins, name):
                told[name] = told.get(name, 0) + 1
                ins.then_inc(sem(name), 1)
                dve.wait_ge(sem(name), told[name])
            tt = nc.vector.tensor_tensor
            tsc = nc.vector.tensor_scalar

            def normalise(k, src, dst, signal, wait=None):
                layer_norm_stats(dve, link, src, wait)
                tsc(ve[:, :], mv[:, :, 1], 1e-5, None, ALU.add).then_inc(sem("s_var"), 1)
                dve.wait_ge(sem("s_rstd"), k)
                for t in range(NT):
                    tsc(dst[:, t, :], src[:, t, :], mv[:, t, 0:1], rstd[:, t:t + 1], ALU.subtract, ALU.mult)\
                        .then_inc(sem(signal), 1)

            nc.vector.memset(ones[:, :], 1.0).then_inc(sem("s_ones"), 1)
            normalise(1, x_res, xn, "s_xn0", lambda t: dve.wait_ge(sem(f"s_x{t // 4}"), 16) if t % 4 == 0 else None)

            for k in range(2):
                dve.wait_ge(sem("s_wprep"), k + 1)
                nc.vector.tensor_copy(wcat0[:, 4 * k:4 * k + 4, 0:P],
                                      ps[:, 4 + k, :].rearrange("p (n c) -> p n c", n=4)).then_inc(sem("s_wprep_sb"), 1)
            for k in range(2):
                dve.wait_ge(sem("s_wprep"), k + 3)
                nc.vector.tensor_copy(wcat1[:, 4 * k:4 * k + 4, 0:P],
                                      ps[:, 6 + k, :].rearrange("p (n c) -> p n c", n=4)).then_inc(sem("s_wprep_sb"), 1)

            dve.wait_ge(sem("s_small"), SMALL)
            dve.wait_ge(sem("s_sumsq"), NT)
            tsc(small[:, 0, :], small[:, 2, :], 1.0 / QL, 1e-6, ALU.mult, ALU.add)
            tsc(small[:, 1, :], small[:, 3, :], 1.0 / KVL, 1e-6, ALU.mult, ALU.add).then_inc(sem("s_ms"), 1)
            dve.wait_ge(sem("s_rms"), 1)
            rq = small[:, 4, :]
            rk = small[:, 5, :]
            tt(qs[:, :, 0:QL], praw[:, :, 0:QL], rq.unsqueeze(2).broadcast_to([P, NT, QL]), ALU.mult)
            tt(qs[:, :, QL:], praw[:, :, P:QL], rq.unsqueeze(2).broadcast_to([P, NT, QL2]), ALU.mult).then_inc(sem("s_qs"), 1)
            link(tt(kc[:, :, 0:KVL], praw[:, :, QL:QL + KVL], rk.unsqueeze(2).broadcast_to([P, NT, KVL]), ALU.mult))
            link(tt(kc[:, :, 0:KVL], kc[:, :, 0:KVL], lnkv[:, :].unsqueeze(1).broadcast_to([P, NT, KVL]), ALU.mult))
            pe_v = praw[:, :, QL + KVL:QL + KVL + ROPE].rearrange("p (b h) c -> p b h c", b=NB)
            nc.vector.tensor_copy(kc[:, :, P:P + KVL], kc[:, :, 0:KVL])
            kp_v = kc[:, :, KVL:P].rearrange("p (b h) c -> p b h c", b=NB)
            rt = [RA[:, 4096 + k * 256:4096 + (k + 1) * 256]
                  .rearrange("p (b h c) -> p b h c", b=NB, h=2) for k in range(4)]
            for h in range(2):
                co = rope_tok[:, h, :].unsqueeze(1).broadcast_to([P, NB, 32])
                si = rope_tok[:, 2 + h, :].unsqueeze(1).broadcast_to([P, NB, 32])
                a1, a2 = pe_v[:, :, h, 0:32], pe_v[:, :, h, 32:64]
                tt(rt[0][:, :, h, :], a1, co, ALU.mult)
                tt(rt[1][:, :, h, :], a2, si, ALU.mult)
                tt(rt[2][:, :, h, :], a2, co, ALU.mult)
                link(tt(rt[3][:, :, h, :], a1, si, ALU.mult))
                tt(kp_v[:, :, h, 0:32], rt[0][:, :, h, :], rt[1][:, :, h, :], ALU.subtract)
                last = tt(kp_v[:, :, h, 32:64], rt[2][:, :, h, :], rt[3][:, :, h, :], ALU.add)
            tell(last, "s_kc")

            link(nc.vector.tensor_copy(glog, praw[:, :, QL + KVL + ROPE:W_IN]))
            gm = small[:, 6, :]
            bc = lambda v: v.unsqueeze(2).broadcast_to([P, NT, NH])
            io = iota[:, :].unsqueeze(1).broadcast_to([P, NT, NH])
            link(nc.vector.tensor_reduce(gm, glog, X, ALU.max))
            tt(gsm, glog, bc(gm), ALU.subtract).then_inc(sem("s_gsub"), 1)
            link(tt(oneh, glog, bc(gm), ALU.is_equal))
            link(nc.vector.scalar_tensor_tensor(oneh, oneh, -float(NH), io, ALU.mult, ALU.add))
            link(nc.vector.tensor_reduce(small[:, 7, :], oneh, X, ALU.min))
            link(tsc(small[:, 7, :], small[:, 7, :], float(NH), None, ALU.add))
            tell(tt(oneh, io, bc(small[:, 7, :]), ALU.is_equal), "s_onehot")

            for k in range(2):
                dve.wait_ge(sem("s_latT"), 2 * k + 1)
                tsc(qaT0[:, 512 * k:512 * k + 512], ps[:, 4 + k, :], lnq[:, 0:1], None, ALU.mult)
                dve.wait_ge(sem("s_latT"), 2 * k + 2)
                v = slice(512 * k, 512 * k + 512)
                link(tsc(q_tail[:, 0, v], ps[:, 6 + k, :], lnq[:, 1:2], None, ALU.mult))
                nc.vector.scalar_tensor_tensor(q_tail[:, 1, v], ps[:, 6 + k, :], lnq[:, 1:2], q_tail[:, 0, v].bitcast(f32),
                                               ALU.mult, ALU.subtract).then_inc(sem("s_lat_sb"), 1)

            def output_weights(k):
                dve.wait_ge(sem("s_wprep"), k + 5)
                nc.vector.tensor_copy(wo_abs[:, 2 * k:2 * k + 2, :],
                                      ps[:, (2, 3, 0, 1)[k], :].rearrange("p (h c) -> p h c", h=2)).then_inc(sem("s_wprep_sb"), 1)

            def sine(n):
                dve.wait_ge(sem("s_swapped"), 64 * (n + 1))
                v = rot.rearrange("p (b s) -> p b s", b=NB)
                tt(v, v, rope_feat[:, 1, :].unsqueeze(1).broadcast_to([P, NB, S]), ALU.mult).then_inc(sem("s_sine"), 1)
            output_weights(0)
            output_weights(1)
            sine(0)
            output_weights(2)
            output_weights(3)
            for g in range(2):
                for h in range(2):
                    dve.wait_ge(sem("s_QTp"), 2 * g + h + 1)
                    bank, v = ps[:, (4, 7, 2, 3)[2 * g + h], :], slice(h * 512, (h + 1) * 512)
                    link(tsc(q_hi[:, g, v].bitcast(f32r), bank, -FSCALE, None, ALU.mult))
                    nc.vector.scalar_tensor_tensor(q_lo[:, g, v], bank, -FSCALE, q_hi[:, g, v], ALU.mult, ALU.subtract)
            nc.vector.memset(vsh[:, :, HD:], 1.0)
            phase_end(dve, 0)

            def gating(l):
                if l in (1, 3):
                    w = l // 2
                    dve.wait_ge(sem("s_gtmp"), NT * (w + 1))
                    link(nc.vector.tensor_reduce(kred[:, w], gtmp[w], X, ALU.add))
                if l == 2:
                    dve.wait_ge(sem("s_gexp"), 1)
                    link(nc.vector.tensor_reduce(small[:, 8, :], gsm, X, ALU.add))
                    link(nc.vector.reciprocal(small[:, 9, :], small[:, 8, :]))
                if l == 4:
                    tt(vsh[:, :, 0:HD], kred[:, 1], small[:, 9, :].unsqueeze(2).broadcast_to([P, NT, HD]), ALU.mult)
                    link(nc.vector.tensor_copy(khi.bitcast(f32r), kred[:, 0]))
                    for q in range(8):
                        last = tt(krep[:, :, q, :], kred[:, 0], khi, ALU.subtract) if q // 2 % 2 else nc.vector.tensor_copy(krep[:, :, q, :], khi)
                    tell(last, "s_krep")

            def body(i, first, last):
                for l in range(mla.U):
                    u = i * mla.U + l
                    dve_max(dve, mla, i, l, first)
                    if not (first and l < 1):
                        dve_scale(dve, u - 1, (l - 1) % 8)
                    if not (first and l < 2):
                        dve_turned(dve, mla, u - 2, l - 2, None if first and l < 6 else 4 * i + (l - 6) // 2 + 1)
                    if first:
                        gating(l)
                    if l == 5 and not last:
                        sine(i + 1)
                if last:
                    u = NP * mla.U
                    dve_scale(dve, u - 1, 7)
                    dve_turned(dve, mla, u - 2, 6, 4 * NP - 3)
                    dve_turned(dve, mla, u - 1, 7, 4 * NP - 2)
            loop(dve, NP, body)
            phase_end(dve, 1)

            def heads_normed(i, h):
                dve.wait_ge(sem("s_yT"), 2 * i + h + 1)
                v = ps[:, 4 + h, :].rearrange("p (t j c) -> p t j c", t=4, j=4)
                rv = ri.rearrange("p a t -> p (a t)").rearrange("p (t j) -> p t j", t=4)
                nc.vector.reciprocal(rv, v[:, :, :, HD]).then_inc(sem("s_yrecip"), 1)
                dve.wait_ge(sem("s_yrecip"), 2 * i + h + 1)
                tt(y[:, 4 * h:4 * h + 4, ds(i * 4 * HD, 4 * HD)].rearrange("p t (j c) -> p t j c", j=4), v[:, :, :, 0:HD],
                   rv.unsqueeze(3).broadcast_to([P, 4, 4, HD]), ALU.mult).then_inc(sem("s_yn"), 1)
                dve.wait_ge(sem("s_yn"), 2 * i + h + 1)

            def bodyg(i, first, last):
                for l in range(gat.U):
                    u = i * gat.U + l
                    dve_max(dve, gat, i, l, first)
                    if not (first and l < 3) and l % 4 != 2:
                        dve_turned(dve, gat, u - 3, l - 3, None if first and l < 11 else 4 * i + (l - 3) // 4 - 1)
                    if l in (3, 11) and not first:
                        heads_normed(i - 1, l // 8)
                if last:
                    for l in (13, 14):
                        dve_turned(dve, gat, i * gat.U + l, l, 4 * i + 2)
                    heads_normed(i, 0)
                    heads_normed(i, 1)
            loop(dve, 4, bodyg)
            dve.wait_ge(sem("s_g0"), 1)
            for k in range(4):
                v = slice(2 * k, 2 * k + 2)
                dve.wait_ge(sem("s_sp"), k + 1)
                link(tt(y[:, v, :], ps[:, 6 + k % 2, :].rearrange("p (t c) -> p t c", t=2), y[:, v, :], ALU.mult))
                tell(tt(x_res[:, v, :], x_res[:, v, :], y[:, v, :], ALU.add), "s_spr")
                for t in (2 * k, 2 * k + 1):
                    last = nc.vector.bn_stats(st[:, t, :], x_res[:, t, :])
                link(last)
                for t in (2 * k, 2 * k + 1):
                    last = nc.vector.bn_aggr(mv[:, t, :], st[:, t, :])
                link(last)
                tsc(ve[:, v], mv[:, v, 1], 1e-5, None, ALU.add).then_inc(sem("s_var"), 1)
                dve.wait_ge(sem("s_rstd"), 2 + k)
                for t in (2 * k, 2 * k + 1):
                    tsc(xn[:, t, :], x_res[:, t, :], mv[:, t, 0:1], rstd[:, t:t + 1], ALU.subtract, ALU.mult)\
                        .then_inc(sem("s_xn1"), 1)

            def k_rows(h):
                for n in (4 * h, 4 * h + 1):
                    f = n % 2
                    dve.wait_ge(sem("s_khp"), n + 1)
                    tsc(plain(kraw)[:, f, h * 512:(h + 1) * 512], ps[:, KH[n], :], bz[:, 0, f:f + 1], None, ALU.add)
                    tsc(plain(kpos)[:, f, h * 512:(h + 1) * 512], ps[:, KH[n], :], bz[:, 0, f:f + 1], 0.0, ALU.add, ALU.max)\
                        .then_inc(sem("s_k_sb"), 1)
            k_rows(0)

            dve.wait_ge(sem("s_router"), 1)
            link(nc.vector.tensor_copy(rl[:, :, :], ps[:, 3, 0:NT * E].rearrange("p (t e) -> p t e", t=NT)))
            rb = lambda v: v.unsqueeze(2).broadcast_to([P, NT, E])
            ie = iota[:, 0:E].unsqueeze(1).broadcast_to([P, NT, E])
            tell(nc.vector.tensor_reduce(small[:, 16, :], rl[:, :, :], X, ALU.max), "s_top")
            link(tt(roneh[:, :, :], rl[:, :, :], rb(small[:, 16, :]), ALU.is_equal))
            link(nc.vector.scalar_tensor_tensor(roneh[:, :, :], roneh[:, :, :], -float(E), ie, ALU.mult, ALU.add))
            link(nc.vector.tensor_reduce(small[:, 17, :], roneh[:, :, :], X, ALU.min))
            link(tsc(small[:, 17, :], small[:, 17, :], float(E), None, ALU.add))
            link(tt(roneh[:, :, :], ie, rb(small[:, 17, :]), ALU.is_equal))
            for e in range(E):
                last = nc.vector.tensor_tensor_scan(upto[:, :, e], ones[:, 0:NT], roneh[:, :, e], 0.0, op0=ALU.mult, op1=ALU.add)
            tell(last, "s_oneh")
            dve.wait_ge(sem("s_gate_exp"), 1)
            link(tsc(small[:, 19, :], small[:, 18, :], 1.0, None, ALU.add))
            tell(nc.vector.reciprocal(small[:, 20, :], small[:, 19, :]), "s_gate")
            k_rows(1)
            link(tsc(small[:, 21, :], iota[:, 0:E], float(P), None, ALU.mult))
            dve.wait_ge(sem("s_rank"), 1)
            rank = ps[:, BD, 0:NT * E].rearrange("p (t e) -> p t e", t=NT)
            link(nc.vector.tensor_copy(small[:, 22, :], ps[:, BD, NT * E:NT * E + E]))
            link(tt(rtmp[:, 0:E, :], small[:, 22, :].unsqueeze(2).broadcast_to([P, E, E]),
                    small[:, 21, :].unsqueeze(1).broadcast_to([P, E, E]), ALU.is_gt))
            link(nc.vector.tensor_reduce(small[:, 23, :], rtmp[:, 0:E, :], X, ALU.add))
            link(nc.vector.tensor_tensor_scan(small[:, 24, :], ones[:, 0:E], small[:, 23, :], 0.0, op0=ALU.mult, op1=ALU.add))
            link(tt(small[:, 25, :], small[:, 24, :], small[:, 23, :], ALU.subtract))
            link(tsc(small[:, 25, :], small[:, 25, :], float(P), -1.0, ALU.mult, ALU.add))
            link(tt(rl[:, :, :], rank, small[:, 25, :].unsqueeze(1).broadcast_to([P, NT, E]), ALU.add))
            tell(tt(rl[:, :, :], rl[:, :, :], roneh[:, :, :], ALU.mult), "s_rank_used")
            link(nc.vector.tensor_reduce(small[:, 26, :], rl[:, :, :], X, ALU.add))
            nc.vector.tensor_copy(pos_i[:, :], small[:, 26, :]).then_inc(sem("s_pos"), 1)
            link(tt(rtmp[:, :, :], small[:, 24, :].unsqueeze(1).broadcast_to([P, 16, E]),
                    iota[:, :].unsqueeze(2).broadcast_to([P, 16, E]), ALU.is_le))
            eidf = small[:, 27:29, :].rearrange("p a t -> p (a t)")
            link(nc.vector.tensor_reduce(eidf, rtmp[:, :, :], X, ALU.add))
            link(tsc(eidf, eidf, float(E - 1), None, ALU.min))
            nc.vector.tensor_copy(eid_i[:, :], eidf).then_inc(sem("s_eid"), 1)

            def inner_rows(m):
                dve.wait_ge(sem("s_silu"), m + 1)
                if m >= 2:
                    dve.wait_ge(sem("s_hT"), m - 1)
                tt(inn_sb[m % 2], act_sb[m % 2], ps[:, BU[m % 2], :], ALU.mult).then_inc(sem("s_h"), 1)

            def inner_turned(m):
                dve.wait_ge(sem("s_hT"), m + 1)
                if m >= 2:
                    dve.wait_ge(sem("s_down"), m - 1)
                nc.vector.tensor_copy(innT_sb[m % 2], ps[:, BT[m % 2], :]).then_inc(sem("s_hT_sb"), 1)

            def out_rows(m):
                dve.wait_ge(sem("s_down"), m + 1)
                if not is_block(m):
                    dst = y[:, tile_of(m), :]
                else:
                    k = m - A0
                    if k >= OB:
                        dve.wait_ge(sem(f"s_ob{k % OB}"), 16 * (k // OB))
                    dst = ob[k % OB]
                nc.vector.tensor_copy(dst, ps[:, BD, 0:D]).then_inc(sem("s_acc"), 1)

            N = NB * T1 * D

            def maxima(f):
                dve.wait_ge(sem("s_mk"), 2 + f)
                link(tt(steps4(hseq)[:, f, :, 1:T1], steps4(hseq)[:, f, :, 1:T1], plain(kraw)[:, f].rearrange("p (b t) -> p b t", b=NB),
                        ALU.add))
                for b in range(NB):
                    last = nc.vector.tensor_tensor_scan(steps4(hmin)[:, f, b, :], steps4(hseq)[:, f, b, :],
                                                        steps4(hseq)[:, f, b, :], -BIG, op0=ALU.max, op1=ALU.max)
                last.then_inc(sem("s_maxima"), 1)

            def piece(m):
                if m == 0:
                    dve.wait_ge(sem("s_kh_sb"), 4)
                    tell(tsc(hmin, hseq, 0.0, None, ALU.min), "s_mnh")
                    tell(tsc(hseq, hseq, 0.0, 2.0, ALU.max, ALU.mult), "s_num")
                if m == 2:
                    dve.wait_ge(sem("s_l1"), 1)
                    tell(tt(plain(kpos), plain(kpos), plain(e1), ALU.add), "s_softplus")
                if m == 4:
                    dve.wait_ge(sem("s_l3"), 1)
                    dve.wait_ge(sem("s_cand"), 1)
                    link(tt(hseq, hseq, hmin, ALU.add))
                if m == 6:
                    maxima(0)
                if m == 7:
                    maxima(1)
                if m == 7:
                    dve.wait_ge(sem("s_maxima"), 2)
                    tt(hseq, hseq, hmin, ALU.subtract).then_inc(sem("s_scan_in"), 1)
                if m == 9:
                    dve.wait_ge(sem("s_scan_exp"), 1)
                    for f in range(DK):
                        for b in range(NB):
                            last = nc.vector.tensor_tensor_scan(steps4(kraw)[:, f, b, :], steps4(kpos)[:, f, b, :],
                                                                steps4(hseq)[:, f, b, :], 0.0, op0=ALU.mult, op1=ALU.add)
                    last.then_inc(sem("s_scan"), 1)
                if m == 11:
                    dve.wait_ge(sem("s_scan_ln"), 1)
                    dve.wait_ge(sem("s_mxa"), 1)
                    nc.vector.tensor_tensor_reduce(out=kraw, in0=kraw, in1=e1, scale=1.0, scalar=0.0, op0=ALU.add, op1=ALU.add,
                                                   accum_out=small[:, 10, 0:1]).then_inc(sem("s_sum"), 1)
                if m == 12:
                    dve.wait_ge(sem("s_tot"), 1)
                    tell(tsc(small[:, 11, 0:1], ps[:, B7, 0:1], -1.0 / N, None, ALU.mult), "s_mean")
                if m == 14:
                    dve.wait_ge(sem("s_tot"), 2)
                    tsc(small[:, 13, :], ps[:, B7, 0:1].broadcast_to([P, NT]), 1.0 / (N - 1), None, ALU.mult).then_inc(sem("s_varh"), 1)
                    dve.wait_ge(sem("s_rstdh"), 1)
                    tell(tt(small[:, 15, 0:1], small[:, 14, 0:1], small[:, 11, 0:1], ALU.mult), "s_hscale")
                if 16 <= m < 20:
                    k = m - 16
                    dve.wait_ge(sem("s_hback"), k + 1)
                    tell(tt(x2[:, 2 * k:2 * k + 2, :], ps[:, B7, :].rearrange("p (t c) -> p t c", t=2), xn[:, 2 * k:2 * k + 2, :],
                            ALU.add), "s_hback_used")
                    for t in (2 * k, 2 * k + 1):
                        last = nc.vector.bn_stats(st[:, t, :], x2[:, t, :])
                    link(last)
                if m == 19:
                    for t in range(NT):
                        last = nc.vector.bn_aggr(mv[:, t, :], st[:, t, :])
                    link(last)
                    tsc(ve[:, :], mv[:, :, 1], 1e-5, None, ALU.add).then_inc(sem("s_var"), 1)
                if m == 20:
                    dve.wait_ge(sem("s_ln1"), 32)
                    dve.wait_ge(sem("s_rstd"), 6)
                    for t in range(NT):
                        last = tsc(s1[:, t, :], x2[:, t, :], mv[:, t, 0:1], rstd[:, t:t + 1], ALU.subtract, ALU.mult)
                    link(last)
                    link(tt(s1, s1, ln1[:, 0, :].unsqueeze(1).broadcast_to([P, NT, D]), ALU.mult))
                if m == 21:
                    link(tt(s1, s1, ln1[:, 1, :].unsqueeze(1).broadcast_to([P, NT, D]), ALU.add))

            for m in range(M):
                inner_rows(m)
                if 1 <= m <= EARLY:
                    inner_turned(m - 1)
                if m >= 2:
                    out_rows(m - 2)
                piece(m)

            def with_routed(h):
                v = slice(2 * h, 2 * h + 2)
                dve.wait_ge(sem(f"s_gathered{h}"), 32)
                tell(tt(y[:, v, :], y[:, v, :], routed[:, v, :], ALU.add), "s_ffn")

            def result(h):
                v = slice(2 * h, 2 * h + 2)
                dve.wait_ge(sem("s_g1"), h + 1)
                link(tt(y[:, v, :], s1[:, v, :], y[:, v, :], ALU.mult))
                tt(routed[:, v, :], y[:, v, :], x_res[:, v, :], ALU.add).then_inc(sem("s_final"), 1)
            with_routed(0)
            with_routed(1)
            out_rows(M - 2)
            result(0)
            out_rows(M - 1)
            with_routed(2)
            with_routed(3)
            result(1)
            result(2)
            result(3)

        @block.gpsimd
        def _(pool):
            tt = nc.gpsimd.tensor_tensor
            nc.gpsimd.memset(half_neg[:, :], -0.5).then_inc(sem("s_half"), 1)
            pool.wait_ge(sem("s_half"), 1)

            def root(dst, src, w, signal):
                tt(dst, src, half_neg[:, 0:w], ALU.pow).then_inc(sem(signal), 1)
            pool.wait_ge(sem("s_var"), 1)
            root(rstd[:, :], ve[:, :], NT, "s_rstd")
            pool.wait_ge(sem("s_ms"), 1)
            root(small[:, 4:6, :].rearrange("p a t -> p (a t)"), small[:, 0:2, :].rearrange("p a t -> p (a t)"), 2 * NT, "s_rms")

            def stage(n, free):
                if free:
                    pool.wait_ge(sem("s_absp"), 2 * n)
                nc.gpsimd.tensor_copy(ws0, wcat0[:, ds(n, 1), :].rearrange("p h c -> p (h c)"))
                w = wcat1[:, ds(n, 1), :].rearrange("p h c -> p (h c)")
                nc.gpsimd.tensor_copy(w_tail, w).then_inc(sem("s_stage_hi"), 1)
                pool.wait_ge(sem("s_stage_hi"), n + 1)
                tt(w_tail[64:P, :], w[64:P, :], w_tail[64:P, :].bitcast(f32), ALU.subtract).then_inc(sem("s_stage"), 1)
                pool.wait_ge(sem("s_stage"), n + 1)

            def cosine(n):
                pool.wait_ge(sem("s_swapped"), 64 * (n + 1))
                v = raw.rearrange("p (b s) -> p b s", b=NB)
                tt(v, v, rope_feat[:, 0, :].unsqueeze(1).broadcast_to([P, NB, S]), ALU.mult).then_inc(sem("s_cosine"), 1)
                pool.wait_ge(sem("s_cosine"), n + 1)
                pool.wait_ge(sem("s_sine"), n + 1)

            def rotated_a(n, free):
                if free:
                    pool.wait_ge(mla.s_S, 8 * n - 4)
                tt(qh[0][64:P, :], raw[64:P, :], rot[64:P, :], ALU.add).then_inc(sem("s_qA"), 1)
                pool.wait_ge(sem("s_qA"), n + 1)

            def rotated_b(n, free):
                if free:
                    pool.wait_ge(mla.s_S, 8 * n)
                tt(qh[1][0:64, :], raw[0:64, :], rot[0:64, :], ALU.add).then_inc(sem("s_qB"), 1)
                pool.wait_ge(sem("s_qB"), n + 1)

            pool.wait_ge(sem("s_wprep_sb"), 4)
            nc.gpsimd.memset(no_keys, 0.0).then_inc(sem("s_kz"), 1)
            pool.wait_ge(sem("s_kz"), 1)
            nc.gpsimd.tensor_copy(kz, no_keys.unsqueeze(1).broadcast_to([P, 2, TOK])).then_inc(sem("s_kz"), 1)
            pool.wait_ge(sem("s_late"), LATE)
            stage(0, False)
            pool.wait_ge(sem("s_onehot"), 1)
            pool.wait_ge(sem("s_kvraw"), NT)
            for w in range(2):
                for t in range(NT):
                    tt(gtmp[w][:, t], kvraw[:, t, w * D:(w + 1) * D].rearrange("p (h d) -> p d h", h=NH),
                       oneh[:, t, :].unsqueeze(1).broadcast_to([P, HD, NH]), ALU.mult).then_inc(sem("s_gtmp"), 1)
            cosine(0)
            rotated_a(0, False)
            rotated_b(0, False)
            phase_end(pool, 0)
            stage(1, True)

            def body(i, first, staged):
                if not first:
                    rotated_b(i, True)
                if staged:
                    stage(i + 2, True)
                cosine(i + 1)
                rotated_a(i + 1, True)
            body(0, True, True)
            with pool.Fori(1, NP - 2) as i:
                body(i, False, True)
            body(NP - 2, False, False)
            rotated_b(NP - 1, True)
            for j in range(2):
                r = slice(QROWS * j, QROWS * (j + 1))
                nc.gpsimd.tensor_copy(kz[r, j, :], kshT[r, :]).then_inc(sem("s_kz"), 1)
                pool.wait_ge(sem("s_kz"), j + 3)
            pool.wait_ge(mla.s_S, 64)
            pool.wait_ge(sem("s_spread"), 16 * 2 * NH)

            def heads_in(i, b, at):
                v = slice(b * S, (b + 1) * S)
                for w in range(2):
                    last = nc.gpsimd.tensor_copy(QS[:, w, v], at(QT[w], i, v))
                last.then_inc(sem("s_slot"), 1)
            first_heads = lambda b: heads_in(0, b, lambda q, i, v: q[:, i, v])
            first_heads(0)
            phase_end(pool, 1)
            for b in range(1, NB):
                first_heads(b)

            with pool.Fori(1, 4) as i:
                for b in range(NB):
                    pool.wait_ge(gat.s_S, 16 * i + 4 * b - 12)
                    heads_in(i, b, lambda q, i, v: q[:, ds(i, 1), v].rearrange("p g t -> p (g t)"))
            for k in range(4):
                pool.wait_ge(sem("s_var"), 2 + k)
                root(rstd[:, 2 * k:2 * k + 2], ve[:, 2 * k:2 * k + 2], 2, "s_rstd")
            pool.wait_ge(sem("s_gate"), 1)
            for t in range(NT):
                if t == 2:
                    pool.wait_ge(sem("s_khp"), 8)
                if t >= OB:
                    pool.wait_ge(sem(f"s_scat{t % OB}"), 16 * (t // OB))
                nc.gpsimd.tensor_scalar(ob[t % OB], xn[:, t, :], small[:, 20, t:t + 1], 1.0, ALU.mult, ALU.mult)\
                    .then_inc(sem("s_xg"), 1)
                pool.wait_ge(sem("s_xg"), t + 1)
                if t == 0:
                    pool.wait_ge(sem("s_pos"), 1)
                nc.gpsimd.indirect_dma_start(out=sorted_rows, out_offset=bass.IndirectOffsetOnAxis(pos_i[:, t:t + 1], 0),
                                             in_=ob[t % OB], in_offset=None).then_inc(sem(f"s_scat{t % OB}"), 16)

            pool.wait_ge(sem("s_softplus"), 1)
            tt(plain(kraw), plain(kraw), plain(kpos), ALU.subtract).then_inc(sem("s_mk"), 1)
            pool.wait_ge(sem("s_e2"), 1)
            tt(hmin, hmin, e1, ALU.subtract).then_inc(sem("s_cand"), 1)
            pool.wait_ge(sem("s_cand"), 1)
            nc.gpsimd.memset(steps4(e1)[:, :, :, 0:1], 0.0).then_inc(sem("s_acum0"), 1)
            for f in range(DK):
                pool.wait_ge(sem("s_acum_sb"), 2 * f + 2)
                pool.wait_ge(sem("s_mk"), 1)
                v = plain(kraw)[:, f].rearrange("p (b t) -> p b t", b=NB)
                tt(v, v, steps4(e1)[:, f, :, 1:T1], ALU.add).then_inc(sem("s_mk"), 1)
            pool.wait_ge(sem("s_acum"), 4)
            pool.wait_ge(sem("s_mk"), 3)
            nc.gpsimd.memset(steps4(kpos)[:, :, :, 0:1], 0.0)
            for f in range(DK):
                pool.wait_ge(sem("s_maxima"), f + 1)
                tt(steps4(kpos)[:, f, :, 1:T1], steps4(hmin)[:, f, :, 0:S], steps4(hmin)[:, f, :, 1:T1], ALU.subtract)\
                    .then_inc(sem("s_dmax"), 1)
            tt(e1, hmin, e1, ALU.subtract).then_inc(sem("s_mxa"), 1)
            pool.wait_ge(sem("s_varh"), 1)
            root(small[:, 14, :], small[:, 13, :], NT, "s_rstdh")
            pool.wait_ge(sem("s_var"), 6)
            root(rstd[:, :], ve[:, :], NT, "s_rstd")
            for k in range(OB):
                pool.wait_ge(sem(f"s_ob{k}"), all_stored(k))
            pool.wait_ge(sem("s_hout"), 1)
            for t in range(NT):
                nc.gpsimd.indirect_dma_start(out=routed[:, t, :], out_offset=None, in_=sorted_out,
                                             in_offset=bass.IndirectOffsetOnAxis(pos_i[:, t:t + 1], 0))\
                    .then_inc(sem(f"s_gathered{t // 2}"), 16)

        @block.scalar
        def _(act):
            A = nc.scalar.activation

            def turned_rows(signal_in, signal_out, tiles=range(NT)):
                for t in tiles:
                    act.wait_ge(sem(signal_in), t + 1)
                    A(xnT[:, :, t * P:(t + 1) * P], ps[:, t % 2, 0:2 * P].rearrange("p (k c) -> p k c", k=2), ACT.Copy)\
                        .then_inc(sem(signal_out), 1)
            turned_rows("s_xT0", "s_xnT0")
            for t in range(NT):
                act.wait_ge(sem("s_inp"), t + 1)
                A(praw[:, t, :], ps[:, 2 + t % 2, 0:W_IN], ACT.Copy).then_inc(sem("s_praw"), 1)
            act.wait_ge(sem("s_praw"), NT)
            for t in range(NT):
                A(xn[:, t, 0:QL], praw[:, t, 0:QL], ACT.Square, accum_out=small[:, 2, t:t + 1])
                A(xn[:, t, QL:QL + KVL], praw[:, t, QL:QL + KVL], ACT.Square, accum_out=small[:, 3, t:t + 1])\
                    .then_inc(sem("s_sumsq"), 1)
            for t in range(NT):
                act.wait_ge(sem("s_kvp"), t + 1)
                A(kvraw[:, t, :], ps[:, t % 2, :], ACT.Copy).then_inc(sem("s_kvraw"), 1)
            for k in range(4):
                act.wait_ge(sem("s_kTT"), k + 1)
                A((kT, kTB)[k // 2][:, 512 * (k % 2):512 * (k % 2) + 512], ps[:, (2, 3, 0, 1)[k], :], ACT.Copy)\
                    .then_inc(sem("s_kT"), 1)

            def copy_raw(n, h, first):
                act.wait_ge(sem("s_ropep"), 2 * n + h + 1)
                if not first:
                    act.wait_ge(sem("s_qB"), n)
                A(raw[:, h * 512:(h + 1) * 512], ps[:, QB[h], :], ACT.Copy).then_inc(sem("s_raw"), 1)

            def copy_abs(n, j, h, first):
                act.wait_ge(sem("s_absp"), 2 * n + 2)
                if not first:
                    act.wait_ge(mla.s_S, 8 * n - 4 + 4 * j)
                r, v = slice(64 * j, 64 * j + 64), slice(h * 512, (h + 1) * 512)
                A(qh[j][r, v], ps[r, QB[h], :], ACT.Copy, scale=-SCALE).then_inc(sem(("s_absA", "s_absB")[j]), 1)

            def copy_out(i, a_):
                act.wait_ge(mla.s_av, 4 * i + a_ + 1)
                for s_ in range(2):
                    b, r = 2 * (a_ % 2) + (s_ ^ (a_ // 2)), slice(64 * s_, 64 * s_ + 64)
                    last = A(xcT[r, ds(i, 1), b * S:(b + 1) * S].rearrange("p n t -> p (n t)"), ps[r, AB[a_ % 2], 0:S], ACT.Copy)
                last.then_inc(sem("s_xbank_read"), 1)

            def body(i, first, last):
                for l in range(mla.U):
                    if l == 0 and not first:
                        copy_abs(i, 1, 0, False)
                    act_exp(act, mla, i, l, first, by_head(rs))
                    if l == 0 and not first:
                        copy_abs(i, 1, 1, False)
                    if l == 1 and first:
                        act.wait_ge(sem("s_gsub"), 1)
                        A(gsm, gsm, ACT.Exp).then_inc(sem("s_gexp"), 1)
                    at = l - 1 if first else l
                    if at in (1, 2) and not last:
                        copy_raw(i + 1, at - 1, False)
                    if at in (4, 5) and not last:
                        copy_abs(i + 1, 0, at - 4, False)
                    if l == 6 and last:
                        act.wait_ge(sem("s_kz"), 4)
                    if l in (6, 7):
                        copy_out(i, l - 6)
                    if l in (2, 3) and not first:
                        copy_out(i - 1, l)
                if first:
                    for k in range(2):
                        act.wait_ge(sem("s_kshTT"), k + 1)
                        A(kshT[:, 512 * k:512 * k + 512], ps[:, AB[k], :], ACT.Copy).then_inc(sem("s_xbank_read"), 1)
                if last:
                    copy_out(i, 2)
                    copy_out(i, 3)
            copy_raw(0, 0, True)
            copy_raw(0, 1, True)
            for j in range(2):
                for h in range(2):
                    copy_abs(0, j, h, True)
            phase_end(act, 0)
            loop(act, NP, body)
            phase_end(act, 1)

            def fourth_turned(B, k, first):
                act.wait_ge(gat.s_T, 4 * B + 4)
                if not first:
                    act.wait_ge(gat.s_av, B - 1)
                A(probT8[k], ps[:, TB[1], 0:WIDE], ACT.Copy).then_inc(sem("s_fourth"), 1)

            def copy_heads(i, h):
                act.wait_ge(gat.s_av, 4 * i + 2 * h + 2)
                A(ysum[:, h * 512:(h + 1) * 512], ps[:, 4 + h, :], ACT.Copy).then_inc(sem("s_ysum"), 1)

            def bodyg(i, first, last):
                for l in range(gat.U):
                    if l % 4 == 2 and not (first and l < 3):
                        fourth_turned(4 * i + (l - 3) // 4, (l - 3) % 8, first and l < 11)
                    act_exp(act, gat, i, l, first)
                    if l == 14:
                        copy_heads(i, 0)
                    if l == 6 and not first:
                        copy_heads(i - 1, 1)
                if last:
                    fourth_turned(4 * i + 3, 7, False)
                    copy_heads(i, 1)
            loop(act, 4, bodyg)
            act.wait_ge(sem("s_yn"), 2 * 4)
            A(y[:, :, :], y[:, :, :], ACT.Silu).then_inc(sem("s_g0"), 1)

            turned_rows("s_xT1", "s_xnT1")
            act.wait_ge(sem("s_late"), LATE)
            for n in (2, 3, 6, 7):
                h, f = n // 4, n % 2
                act.wait_ge(sem("s_khp"), n + 1)
                if h == 0:
                    A(steps4(hseq)[:, f, :, 0], bz[:, 2, f:f + 1].broadcast_to([P, NB]), ACT.Copy)
                A(steps4(hseq)[:, f, 2 * h:2 * h + 2, 1:T1], ps[:, KH[n], :].rearrange("p (b t) -> p b t", t=S), ACT.Identity,
                  bias=bz[:, 1, f:f + 1]).then_inc(sem("s_kh_sb"), 1)
                if n == 3:
                    act.wait_ge(sem("s_top"), 1)
                    A(small[:, 18, :], small[:, 16, :], ACT.Exp, scale=-1.0).then_inc(sem("s_gate_exp"), 1)

            def inner_turned(m):
                act.wait_ge(sem("s_hT"), m + 1)
                if m == EARLY:
                    act.wait_ge(sem("s_hT_sb"), EARLY)
                if m >= 2:
                    act.wait_ge(sem("s_down"), m - 1)
                A(innT_sb[m % 2], ps[:, BT[m % 2], :], ACT.Copy).then_inc(sem("s_hT_sb"), 1)

            def rows_in(k):
                act.wait_ge(sem("s_xbT"), k + 1)
                if k >= 2:
                    act.wait_ge(sem("s_gu"), A0 + k - 1)
                A(xbT[k % 2][:, :], ps[:, B7, 0:D], ACT.Copy).then_inc(sem("s_xbT_sb"), 1)

            def piece(m):
                if m == 0:
                    act.wait_ge(sem("s_k_sb"), 4)
                    A(plain(e1), plain(kraw), ACT.Abs).then_inc(sem("s_act1"), 1)
                if m == 1:
                    act.wait_ge(sem("s_act1"), 1)
                    A(plain(e1), plain(e1), ACT.Exp, scale=-1.0).then_inc(sem("s_act1"), 1)
                    act.wait_ge(sem("s_act1"), 2)
                    A(plain(e1), plain(e1), ACT.Ln, bias=1.0).then_inc(sem("s_l1"), 1)
                if m == 2:
                    act.wait_ge(sem("s_num"), 1)
                    A(hseq, hseq, ACT.Ln, bias=1.0).then_inc(sem("s_l3"), 1)
                if m == 3:
                    act.wait_ge(sem("s_softplus"), 1)
                    A(e1, hmin, ACT.Exp).then_inc(sem("s_act1"), 1)
                    act.wait_ge(sem("s_act1"), 3)
                    A(e1, e1, ACT.Ln, bias=1.0).then_inc(sem("s_e2"), 1)
                if 4 <= m < 8:
                    k = m - 4
                    act.wait_ge(sem("s_acum0"), 1)
                    act.wait_ge(sem("s_acum"), k + 1)
                    A(steps4(e1)[:, k // 2, 2 * (k % 2):2 * (k % 2) + 2, 1:T1], ps[:, B7, :].rearrange("p (b t) -> p b t", b=2),
                      ACT.Copy).then_inc(sem("s_acum_sb"), 1)
                if m == 8:
                    act.wait_ge(sem("s_scan_in"), 1)
                    A(hseq, hseq, ACT.Exp)
                    act.wait_ge(sem("s_dmax"), 2)
                    A(kpos, kpos, ACT.Exp).then_inc(sem("s_scan_exp"), 1)
                if m == 10:
                    act.wait_ge(sem("s_scan"), 1)
                    A(kraw, kraw, ACT.Ln).then_inc(sem("s_scan_ln"), 1)
                if m == 13:
                    act.wait_ge(sem("s_mean"), 1)
                    A(hseq, kraw, ACT.Square, bias=small[:, 11, 0:1], accum_out=small[:, 12, 0:1]).then_inc(sem("s_sumsqh"), 1)
                if m == 15:
                    act.wait_ge(sem("s_hscale"), 1)
                    act.wait_ge(sem("s_sumsqh"), 1)
                    for f in range(DK):
                        last = A(hout[:, f * TOK:(f + 1) * TOK].rearrange("p (b t) -> p b t", b=NB), steps4(kraw)[:, f, :, 1:T1],
                                 ACT.Exp, scale=small[:, 14, 0:1], bias=small[:, 15, 0:1])
                    last.then_inc(sem("s_hout"), 1)

            for m in range(M):
                act.wait_ge(sem("s_gu"), m + 1)
                if m >= 2:
                    act.wait_ge(sem("s_h"), m - 1)
                A(act_sb[m % 2], ps[:, BG[m % 2], :], ACT.Silu).then_inc(sem("s_silu"), 1)
                if m > EARLY:
                    inner_turned(m - 1)
                for k in blocks_in(m):
                    rows_in(k)
                if is_block(m - 3):
                    k = m - 3 - A0
                    act.wait_ge(sem("s_acc"), m - 2)
                    act.dma_start(sorted_out[k * P:(k + 1) * P, :], ob[k % OB]).then_inc(sem(f"s_ob{k % OB}"), 16)
                piece(m)
            inner_turned(M - 1)
            for h in range(4):
                act.wait_ge(sem("s_ffn"), h + 1)
                A(y[:, 2 * h:2 * h + 2, :], y[:, 2 * h:2 * h + 2, :], ACT.Silu).then_inc(sem("s_g1"), 1)

        @block.tensor
        def _(pe):
            mm_ = nc.tensor.matmul
            tr = lambda o, i_, k=P: nc.tensor.transpose(o, i_, ident[0:k, 0:k])
            def rows_turned(src, s_in, s_out, s_copied):
                pe.wait_ge(sem("s_ident"), 16)
                for t in range(NT):
                    pe.wait_ge(sem(s_in), t + 1)
                    if t >= 2:
                        pe.wait_ge(sem(s_copied), t - 1)
                    tr(ps[:, t % 2, 0:P], src[:, t, 0:P])
                    tr(ps[:, t % 2, P:2 * P], src[:, t, P:2 * P]).then_inc(sem(s_out), 1)
            rows_turned(xn, "s_xn0", "s_xT0", "s_xnT0")
            pe.wait_ge(sem("s_win"), 16)
            for t in range(NT):
                pe.wait_ge(sem("s_xnT0"), t + 1)
                if t >= 2:
                    pe.wait_ge(sem("s_praw"), t - 1)
                for k in range(DK):
                    last = mm_(ps[:, 2 + t % 2, 0:W_IN], xnT[:, k, t * P:(t + 1) * P], w_in[:, k, :], start=(k == 0), stop=(k == 1))
                last.then_inc(sem("s_inp"), 1)
            pe.wait_ge(sem("s_wnope"), 32)
            for k in range(4):
                for h in range(8):
                    w = w_nope[:, 8 * (k % 2) + h, :]
                    w = w[:, 0:P] if k < 2 else w[:, P:]
                    last = mm_(ps[:, 4 + k, h * 64:(h + 1) * 64], w, w_kabs[:, 8 * (k % 2) + h, :], start=True, stop=True)
                last.then_inc(sem("s_wprep"), 1)
            pe.wait_ge(sem("s_wkv"), 32)
            for t in range(NT):
                if t >= 2:
                    pe.wait_ge(sem("s_kvraw"), t - 1)
                for k in range(DK):
                    last = mm_(ps[:, t % 2, :], xnT[:, k, t * P:(t + 1) * P], w_kv[:, k, :], start=(k == 0), stop=(k == 1))
                last.then_inc(sem("s_kvp"), 1)
            pe.wait_ge(sem("s_wprep_sb"), 4)
            pe.wait_ge(sem("s_qs"), 1)
            for k in range(2):
                for t in range(4):
                    last = tr(ps[:, 4 + k, t * P:(t + 1) * P], qs[:, 4 * k + t, 0:P])
                last.then_inc(sem("s_latT"), 1)
                for t in range(4):
                    last = tr(ps[:, 6 + k, t * P:(t + 1) * P], qs[:, 4 * k + t, P:])
                last.then_inc(sem("s_latT"), 1)
            pe.wait_ge(sem("s_kc"), 1)
            for k in range(4):
                if k == 2:
                    pe.wait_ge(sem("s_kvraw"), NT)
                for t in range(4):
                    last = tr(ps[:, (2, 3, 0, 1)[k], t * P:(t + 1) * P], kc[:, 4 * (k % 2) + t, KVL * (k // 2):KVL * (k // 2) + P])
                last.then_inc(sem("s_kTT"), 1)
            pe.wait_ge(sem("s_lat_sb"), 2)

            def queries(n, part, h, first):
                at = (P, 0)[part]
                if part == 0:
                    pe.wait_ge(sem("s_stage"), n + 1)
                    if not first:
                        pe.wait_ge(sem("s_absB"), 2 * n + h - 1)
                if part == 1:
                    pe.wait_ge(sem("s_raw"), 2 * n + h + 1)
                mm_(ps[:, QB[h], :], ws0[:, at:at + P], qaT0[:, h * 512:(h + 1) * 512], start=True, stop=False)
                mm_(ps[:, QB[h], :], w_tail[:, at:at + P], q_tail[:, 0, h * 512:(h + 1) * 512], start=False, stop=False)
                mm_(ps[:, QB[h], :], w_tail[:, at:at + P], q_tail[:, 1, h * 512:(h + 1) * 512], start=False, stop=True)\
                    .then_inc(sem(("s_ropep", "s_absp")[part]), 1)

            def output_weights(k):
                pe.wait_ge(sem("s_kT"), k + 1)
                for q in range(2):
                    for j in range(2):
                        h = 4 * k + 2 * q + j
                        last = mm_(ps[64 * j:64 * j + 64, (2, 3, 0, 1)[k], q * D:(q + 1) * D], w_oabs[:, h, :], w_o[:, h, :],
                                   start=True, stop=True)
                last.then_inc(sem("s_wprep"), 1)

            queries(0, 0, 0, True)
            queries(0, 0, 1, True)
            pe.wait_ge(sem("s_wo"), 32)
            output_weights(0)
            output_weights(1)
            queries(0, 1, 0, True)
            queries(0, 1, 1, True)
            output_weights(2)
            output_weights(3)
            for g in range(2):
                if g == 1:
                    pe.wait_ge(sem("s_wprep_sb"), 6)
                for h in range(2):
                    for k in range(DK):
                        last = mm_(ps[:, (4, 7, 2, 3)[2 * g + h], :], w_q[:, k, g * P:(g + 1) * P], xnT[:, k, h * 512:(h + 1) * 512],
                                   start=(k == 0), stop=(k == 1))
                    last.then_inc(sem("s_QTp"), 1)
            phase_end(pe, 0)

            def two_batches(i, a_, first):
                j, c = a_ // 2, a_ % 2
                pe.wait_ge(mla.s_pt, 8 * i + 2 * a_ + 2)
                if not first:
                    pe.wait_ge(sem("s_xbank_read"), 4 * i + a_ + 1)
                for k in range(2):
                    for s_ in range(2):
                        b = 2 * c + (s_ ^ j)
                        pt = mla.turned(4 * j + b)
                        last = mm_(ps[64 * s_:64 * s_ + 64, AB[c], k * P:S], kc[:, 2 * b + k, 0:KVL],
                                   pt[:, 0:S] if k == 0 else pt[:, S:WIDE], start=(k == 0), stop=(k == 1))
                last.then_inc(mla.s_av, 1)

            def body(i, first, last):
                for l in range(mla.U):
                    u = i * mla.U + l
                    if l % NB == 0:
                        pe.wait_ge(sem(("s_qA", "s_qB")[l // NB]), i + 1)
                        pe.wait_ge(sem(("s_absA", "s_absB")[l // NB]), 2 * i + 2)
                    pe_scores(pe, mla, i, l, first)
                    if not (first and l < 2):
                        pe_turn(pe, mla, u - 2, l % 2, lambda: None if first and l < 4 else pe.wait_ge(mla.s_pt, u - 3))
                    at = l - 1 if first else l
                    if 0 <= at < 4 and not last:
                        queries(i + 1, at // 2, at % 2, False)
                    if l in (4, 6):
                        two_batches(i, (l - 4) // 2, first)
                    if l in (0, 2) and not first:
                        two_batches(i - 1, (l + 4) // 2, False)
                if first:
                    for k in range(2):
                        pe.wait_ge(sem("s_krep"), 1)
                        pe.wait_ge(sem("s_xbank_read"), k + 1)
                        for t in range(4):
                            last_ = tr(ps[:, AB[k], t * P:(t + 1) * P], krep[:, 4 * k + t].rearrange("p r d -> p (r d)"))
                        last_.then_inc(sem("s_kshTT"), 1)
                if last:
                    u = NP * mla.U
                    pe_turn(pe, mla, u - 2, 0, lambda: pe.wait_ge(mla.s_pt, u - 3))
                    pe_turn(pe, mla, u - 1, 1, lambda: pe.wait_ge(mla.s_pt, u - 2))
                    two_batches(i, 2, False)
                    two_batches(i, 3, False)
            loop(pe, NP, body)
            phase_end(pe, 1)

            def turned_read(i, l):
                if l % 4 == 3:
                    pe.wait_ge(sem("s_fourth"), 4 * i + l // 4 + 1)
                else:
                    pe.wait_ge(gat.s_pt, 12 * i + 3 * (l // 4) + l % 4 + 1)

            def four_heads(i, b, part):
                o = lambda j, lo, hi: ps[SLOT * j:SLOT * (j + 1), 4 + b // 2, b % 2 * S + lo:b % 2 * S + hi]
                if part == 0:
                    pe.wait_ge(gat.s_pt, 12 * i + 3 * b + 3)
                    pe.wait_ge(sem("s_fourth"), 4 * i + b + 1)
                    for j in range(4):
                        mm_(o(j, 0, S), vsh[:, 2 * b, :], gat.turned(4 * b + j)[:, 0:S], start=True, stop=False)
                else:
                    for j in range(4):
                        last = mm_(o(j, P, S), vsh[:, 2 * b + 1, :], gat.turned(4 * b + j)[:, S:WIDE], start=False, stop=True)
                    last.then_inc(gat.s_av, 1)

            def heads_back(i, h):
                pe.wait_ge(sem("s_ysum"), 2 * i + h + 1)
                for t in range(4):
                    last = tr(ps[:, 4 + h, t * P:(t + 1) * P], ysum[:, h * 512 + t * P:h * 512 + (t + 1) * P])
                last.then_inc(sem("s_yT"), 1)

            def bodyg(i, first, last):
                for l in range(gat.U):
                    u = i * gat.U + l
                    if l % 4 == 0:
                        pe.wait_ge(sem("s_slot"), 4 * i + l // 4 + 1)
                    pe_scores(pe, gat, i, l, first)
                    if not (first and l < 3):
                        pe_turn(pe, gat, u - 3, l - 3, lambda: None if first and l < 5 else turned_read(i, l - 5))
                    if l in (8, 9, 12, 13):
                        four_heads(i, l // 4 - 2, l % 4)
                    if l in (0, 1, 4, 5) and not first:
                        four_heads(i - 1, l // 4 + 2, l % 4)
                    if l in (1, 9) and not first:
                        heads_back(i - 1, l // 8)
                if last:
                    four_heads(i, 2, 0)
                    four_heads(i, 2, 1)
                    heads_back(i, 0)
                    for l in (13, 14, 15):
                        pe_turn(pe, gat, i * gat.U + l, l, lambda: turned_read(i, l - 2))
                    four_heads(i, 3, 0)
                    four_heads(i, 3, 1)
                    heads_back(i, 1)
            loop(pe, 4, bodyg)
            def turned(t):
                pe.wait_ge(sem("s_xn1"), t + 1)
                if t >= 2:
                    pe.wait_ge(sem("s_xnT1"), t - 1)
                tr(ps[:, t % 2, 0:P], xn[:, t, 0:P])
                tr(ps[:, t % 2, P:2 * P], xn[:, t, P:2 * P]).then_inc(sem("s_xT1"), 1)

            def recurrent_inputs(n, tiles=()):
                h = n // 4
                w, f = n // 2 % 2, n % 2
                if n == 3:
                    pe.wait_ge(sem("s_spr"), 3)
                if n == 4:
                    pe.wait_ge(sem("s_spr"), 4)
                if n == 7:
                    pe.wait_ge(sem("s_top"), 1)
                for k in range(DK):
                    last = mm_(ps[:, KH[n], :], (wz, wh)[w][:, k, f * P:(f + 1) * P], xnT[:, k, h * 512:(h + 1) * 512],
                               start=(k == 0), stop=(k == 1))
                last.then_inc(sem("s_khp"), 1)
                for t in tiles:
                    for k in range(DK):
                        last = mm_(ps[:, 3, t * E:(t + 1) * E], xnT[:, k, t * P:(t + 1) * P], wr[:, k, :],
                                   start=(k == 0), stop=(k == 1))
                if NT - 1 in tiles:
                    last.then_inc(sem("s_router"), 1)

            pe.wait_ge(sem("s_swap_wo"), 32)
            for k in range(4):
                if k >= 2:
                    pe.wait_ge(sem("s_spr"), k - 1)
                for q in range(2):
                    t = 2 * k + q
                    for n in range(NP):
                        last = mm_(ps[:, 6 + k % 2, q * D:(q + 1) * D], xcT[:, n, t * P:(t + 1) * P], (wo_abs, wo_swapped)[t // 2 % 2][:, n, :],
                                   start=(n == 0), stop=(n == NP - 1))
                last.then_inc(sem("s_sp"), 1)
                if k >= 1:
                    turned(2 * k - 2)
                    turned(2 * k - 1)

            pe.wait_ge(sem("s_wz"), 32)
            pe.wait_ge(sem("s_yn"), 8)
            pe.wait_ge(sem("s_xnT1"), 4)
            pe.wait_ge(sem("s_late"), LATE)
            recurrent_inputs(0, (0,))
            recurrent_inputs(1, (1, 2))
            pe.wait_ge(sem("s_xnT1"), 6)
            recurrent_inputs(2, (3, 4, 5))
            turned(6)
            turned(7)
            recurrent_inputs(3)
            pe.wait_ge(sem("s_xnT1"), NT)
            recurrent_inputs(4, (6, 7))
            recurrent_inputs(5)
            pe.wait_ge(sem("s_ones"), 1)
            pe.wait_ge(sem("s_oneh"), 1)
            pe.wait_ge(sem("s_kh_sb"), 2)
            flat = lambda v: v[:, :, :].rearrange("p t e -> p (t e)")
            mm_(ps[:, BD, 0:NT * E], ones[:, :], flat(upto), start=True, stop=False)
            mm_(ps[:, BD, 0:NT * E], after[:, :], flat(roneh), start=False, stop=True)
            mm_(ps[:, BD, NT * E:NT * E + E], ones[:, :], upto[:, NT - 1, :], start=True, stop=True).then_inc(sem("s_rank"), 1)
            recurrent_inputs(6)
            recurrent_inputs(7)
            pe.wait_ge(sem("s_kh_sb"), 4)
            pe.wait_ge(sem("s_k_sb"), 4)

            last_use = [("s_k_sb", 4)]

            def bank7(signal, value):
                pe.wait_ge(sem(last_use[0][0]), last_use[0][1])
                last_use[0] = (signal, value)

            def turn_inner(m):
                pe.wait_ge(sem("s_h"), m + 1)
                if m >= 2:
                    pe.wait_ge(sem("s_hT_sb"), m - 1)
                for k in range(4):
                    last = tr(ps[:, BT[m % 2], k * P:(k + 1) * P], inn_sb[m % 2][:, k * P:(k + 1) * P])
                last.then_inc(sem("s_hT"), 1)

            expert = [None] * M

            def weight(m, at, n):
                if not is_block(m):
                    return SH[:, at:at + n]
                return EXP[:, ds(expert[m] * FX + at, n)]

            def gate_up(m):
                if not is_block(m):
                    rows = lambda k: xnT[:, k, tile_of(m) * P:(tile_of(m) + 1) * P]
                else:
                    b = m - A0
                    pe.wait_ge(sem("s_xbT_sb"), b + 1)
                    rows = lambda k: xbT[b % 2][:, k * P:(k + 1) * P]
                    expert[m] = pe.value_load(eid_i[0:1, b:b + 1], min_val=0, max_val=E - 1)
                if m >= 2:
                    pe.wait_ge(sem("s_silu"), m - 1)
                    pe.wait_ge(sem("s_h"), m - 1)
                for w, bank in ((0, BG[m % 2]), (1, BU[m % 2])):
                    for k in range(DK):
                        last = mm_(ps[:, bank, :], rows(k), weight(m, k * 2 * FF + w * FF, FF), start=(k == 0), stop=(k == 1))
                last.then_inc(sem("s_gu"), 1)

            def down(m):
                pe.wait_ge(sem("s_hT_sb"), m + 1)
                if m >= 1:
                    pe.wait_ge(sem("s_acc"), m)
                else:
                    pe.wait_ge(sem("s_rank_used"), 1)
                for k in range(4):
                    last = mm_(ps[:, BD, 0:D], innT_sb[m % 2][:, k * P:(k + 1) * P], weight(m, DK * 2 * FF + k * D, D),
                               start=(k == 0), stop=(k == 3))
                last.then_inc(sem("s_down"), 1)

            def rows_in(k):
                pe.wait_ge(sem(f"s_xb{k % 2}"), 16 * (k // 2 + 1))
                bank7("s_xbT_sb", k + 1)
                tr(ps[:, B7, 0:P], xb[k % 2][:, 0:P])
                tr(ps[:, B7, P:2 * P], xb[k % 2][:, P:2 * P]).then_inc(sem("s_xbT"), 1)

            def piece(m):
                if 4 <= m < 8:
                    f, h = (m - 4) // 2, (m - 4) % 2
                    pe.wait_ge(sem("s_softplus"), 1)
                    bank7("s_acum_sb", m - 3)
                    v = lambda g: plain(kpos)[:, g, h * 512:(h + 1) * 512]
                    if f == 1:
                        mm_(ps[:, B7, :], ones[:, :], v(0), start=True, stop=False)
                    mm_(ps[:, B7, :], upper[:, :], v(f), start=(f == 0), stop=True).then_inc(sem("s_acum"), 1)
                if m == 12:
                    pe.wait_ge(sem("s_sum"), 1)
                    bank7("s_mean", 1)
                    mm_(ps[:, B7, 0:1], ones[:, :], small[:, 10, 0:1], start=True, stop=True).then_inc(sem("s_tot"), 1)
                if m == 14:
                    pe.wait_ge(sem("s_sumsqh"), 1)
                    bank7("s_varh", 1)
                    mm_(ps[:, B7, 0:1], ones[:, :], small[:, 12, 0:1], start=True, stop=True).then_inc(sem("s_tot"), 1)
                if 16 <= m < 20:
                    k = m - 16
                    pe.wait_ge(sem("s_hout"), 1)
                    bank7("s_hback_used", k + 1)
                    for q in range(2):
                        for f in range(DK):
                            t = 2 * k + q
                            last = tr(ps[:, B7, q * D + f * P:q * D + (f + 1) * P], hout[:, f * TOK + t * P:f * TOK + (t + 1) * P])
                    last.then_inc(sem("s_hback"), 1)

            pe.wait_ge(sem("s_wsh"), 32)
            for m in range(M):
                if m == A0:
                    pe.wait_ge(sem("s_wexp"), 32 * E)
                    pe.wait_ge(sem("s_eid"), 1)
                gate_up(m)
                if m >= 1:
                    turn_inner(m - 1)
                if m >= 2:
                    down(m - 2)
                for k in blocks_in(m):
                    rows_in(k)
                piece(m)
            turn_inner(M - 1)
            down(M - 2)
            down(M - 1)


def layouts(i):
    import numpy as np
    c = lambda v: np.ascontiguousarray(v)
    arr = {k: np.asarray(v) for k, v in i.items()}
    turned = np.concatenate([np.arange(0, ROPE, 2), np.arange(1, ROPE, 2)])
    wkv_a = arr["L0_attn_wkv_a"]
    wq_b = arr["L0_attn_wq_b"].reshape(NH, NOPE + ROPE, QL)
    wkv_b = arr["L0_attn_wkv_b"].reshape(NH, NOPE + VH, KVL)
    wqkv = arr["L0_ffn_W_qkv"]
    d = {
        "x": arr["L0_attn_hidden_states"].reshape(TOK, D),
        "w_in": np.concatenate([arr["L0_attn_wq_a"], wkv_a[0:KVL], wkv_a[KVL:][turned], arr["L0_ffn_W_gate"]], axis=0).T,
        "w_kv": wqkv[D:].T,
        "w_q": wqkv[0:D].T.reshape(D, 2, 2, 4, HD).transpose(0, 2, 1, 3, 4).reshape(D, D),
        "w_nope": np.concatenate([wq_b[:, 0:NOPE], wq_b[:, 0:NOPE, P:]], axis=2),
        "w_pe": wq_b[:, NOPE:][:, turned].transpose(2, 0, 1).reshape(QL, NH // 2, 2, ROPE)[:, :, ::-1].reshape(QL, NH * ROPE),
        "w_kabs": wkv_b[:, 0:NOPE],
        "w_oabs": wkv_b[:, VH:],
        "w_o": arr["L0_attn_wo"].T,
        "q_ln": arr["L0_attn_q_a_ln_w"], "kv_ln": arr["L0_attn_kv_a_ln_w"],
        "w_z": arr["L1_attn_W_z"].T, "w_h": arr["L1_attn_W_h"].T,
        "rows_l1": np.stack([arr[f"L1_attn_{n}"].reshape(DK, P) for n in ("b_z", "b_h", "h0")]).transpose(2, 0, 1),
        "ln_w": arr["L1_attn_ln_w"], "ln_b": arr["L1_attn_ln_b"],
        "w_router": arr["L1_ffn_router_w"].T,
        "w_gu": arr["L1_ffn_w_gate_up"], "w_dn": arr["L1_ffn_w_down"],
        "w_shared_gu": arr["L1_ffn_shared_gate_up"], "w_shared_dn": arr["L1_ffn_shared_down"],
    }
    return {k: c(v) for k, v in d.items()}


def kernel(**inputs):
    import concourse.bacc as _bacc
    from concourse import mybir as _mybir
    from concourse.bass_utils import run_bass_kernel_spmd as _run

    arrays = {**layouts(inputs), **constants()}
    nc = _bacc.Bacc("TRN2", target_bir_lowering=False, num_devices=1)
    a = {k: nc.dram_tensor(f"in_{k}", v.shape, _mybir.dt.from_np(v.dtype), kind="ExternalInput").ap() for k, v in arrays.items()}
    out = nc.dram_tensor("out", (TOK, D), _mybir.dt.float32, kind="ExternalOutput").ap()
    recurrent_kernel(nc, a, out)
    r = _run(nc, [{f"in_{k}": v for k, v in arrays.items()}], core_ids=[0])
    return r.results[0]["out"].reshape(NB, S, D)
```
